# Optimizing a Trainium2 kernel written in Bass

```python
import numpy as np
import jax
import jax.numpy as jnp

def _softmax(x, axis=-1):
    return jax.nn.softmax(x, axis=axis)

def _gelu(x):
    return jax.nn.gelu(x, approximate=True)

def _silu(x):
    return jax.nn.silu(x)

def _sigmoid(x):
    return jax.nn.sigmoid(x)

def _layernorm(x, axis=-1, eps=1e-05):
    m = jnp.mean(x, axis=axis, keepdims=True)
    v = jnp.var(x, axis=axis, keepdims=True)
    return (x - m) / jnp.sqrt(v + eps)

def _scatter_add(tgt, idx, src, axis=0):
    return tgt.at[idx].add(src)

def _segment_sum(src, seg, n):
    return jax.ops.segment_sum(src, seg, n)
kernel_name = 'mk_perceiver_d1_seqx_r4_918283'

def setup_inputs(seed: int=0):
    np.random.seed(seed)
    _w = jnp.asarray

    def _rec_inputs():
        import jax
        import jax.numpy as jnp
        _rk = jax.random.key(seed)
        x = 7.22e-05 + 1 * jax.random.normal(jax.random.fold_in(_rk, 1), (16, 64, 512), jnp.float32)
        _lenS = 64 - jax.random.randint(jax.random.fold_in(_rk, 7), (16,), 0, max(1, 64 // 4) + 1, jnp.int32)
        _lenS2 = 1601 - jax.random.randint(jax.random.fold_in(_rk, 8), (16,), 0, max(1, 1601 // 4) + 1, jnp.int32)
        _ctx_1024P = jax.random.normal(jax.random.fold_in(_rk, 11), (16, 16, 256), jnp.float32)
        _ctx_1024c = jax.random.dirichlet(jax.random.fold_in(_rk, 511), 0.3 * jnp.ones((16,), jnp.float32), (16, 1601))
        _ctx_1024t = jnp.einsum('bsk,bkd->bsd', _ctx_1024c, _ctx_1024P)
        _ctx_1024t = _ctx_1024t * jax.lax.rsqrt(jnp.mean(jnp.square(_ctx_1024t)) + 1e-12) * 0.953939
        ctx_1024 = -0.000673644 + 1.00013 * (_ctx_1024t + 0.3 * jax.random.normal(jax.random.fold_in(_rk, 611), (16, 1601, 256), jnp.float32))
        return (x, ctx_1024)
    x, ctx_1024 = _rec_inputs()

    def _L0_xattn_setup():
        import jax, jax.numpy as jnp
        import numpy as np
        B, S1, S2, DCA = (2, 512, 256, 16)
        QDIM, KDIM, H = (512, 256, 16)
        HD = QDIM // H
        SCALE = HD ** (-0.5)
        EPS = 1e-06
        DCA_WEIGHT = 1.0

        def _ln(t, w, b):
            m = jnp.mean(t, axis=-1, keepdims=True)
            v = jnp.var(t, axis=-1, keepdims=True)
            return (t - m) * jax.lax.rsqrt(v + EPS) * w + b

        def _attn(q, k, v):
            s = jnp.einsum('bhqd,bhkd->bhqk', q, k) * SCALE
            p = jax.nn.softmax(s, axis=-1)
            return jnp.einsum('bhqk,bhkd->bhqd', p, v)
        key = jax.random.key(seed)
        ks = jax.random.split(key, 8)
        w = lambda k, shape: jax.random.normal(k, shape, jnp.float32) * 0.02
        return {'x': jax.random.normal(ks[0], (B, S1, QDIM), jnp.float32), 'y': jax.random.normal(ks[1], (B, S2 + DCA, KDIM), jnp.float32), 'Wq': w(ks[2], (QDIM, QDIM)), 'bq': jnp.zeros((QDIM,), jnp.float32), 'Wk': w(ks[3], (KDIM, QDIM)), 'bk': jnp.zeros((QDIM,), jnp.float32), 'Wv': w(ks[4], (KDIM, QDIM)), 'bv': jnp.zeros((QDIM,), jnp.float32), 'Wkv_dca': w(ks[5], (KDIM, 2 * QDIM)), 'bkv_dca': jnp.zeros((2 * QDIM,), jnp.float32), 'qn_w': jnp.ones((HD,), jnp.float32), 'qn_b': jnp.zeros((HD,), jnp.float32), 'kn_w': jnp.ones((HD,), jnp.float32), 'kn_b': jnp.zeros((HD,), jnp.float32), 'kn_dca_w': jnp.ones((HD,), jnp.float32), 'kn_dca_b': jnp.zeros((HD,), jnp.float32), 'Wo': w(ks[6], (QDIM, QDIM)), 'bo': jnp.zeros((QDIM,), jnp.float32)}
    _L0_xattn_all = _L0_xattn_setup()
    _L0_xattn_in = {k: v for k, v in _L0_xattn_all.items() if k in ('Wq', 'bq', 'Wk', 'bk', 'Wv', 'bv', 'Wkv_dca', 'bkv_dca', 'qn_w', 'qn_b', 'kn_w', 'kn_b', 'kn_dca_w', 'kn_dca_b', 'Wo', 'bo')}
    del _L0_xattn_all

    def _L0_attn_setup():
        import jax, jax.numpy as jnp
        import numpy as np
        EPS = 1e-06
        ROPE_BASE = 10000.0

        def _rmsnorm(x, w):
            var = jnp.mean(x * x, axis=-1, keepdims=True)
            return x * jax.lax.rsqrt(var + EPS) * w

        def _rope(t):
            S, D = (t.shape[-2], t.shape[-1])
            inv_freq = 1.0 / ROPE_BASE ** (jnp.arange(0, D, 2, dtype=jnp.float32) / D)
            ang = jnp.arange(S, dtype=jnp.float32)[:, None] * inv_freq
            cos = jnp.concatenate([jnp.cos(ang), jnp.cos(ang)], axis=-1)
            sin = jnp.concatenate([jnp.sin(ang), jnp.sin(ang)], axis=-1)
            t1, t2 = jnp.split(t, 2, axis=-1)
            rot = jnp.concatenate([-t2, t1], axis=-1)
            return t * cos + rot * sin
        key = jax.random.key(seed)
        ks = jax.random.split(key, 9)
        B, S, H = (2, 512, 512)
        Hq, Hkv, D = (16, 4, 128)
        s = 0.02
        return {'x': jax.random.normal(ks[0], (B, S, H), jnp.float32), 'q_project': jax.random.normal(ks[1], (Hq * D, H), jnp.float32) * s, 'k_project': jax.random.normal(ks[2], (Hkv * D, H), jnp.float32) * s, 'v_project': jax.random.normal(ks[3], (Hkv * D, H), jnp.float32) * s, 'q_bias': jax.random.normal(ks[4], (Hq * D,), jnp.float32) * s, 'k_bias': jax.random.normal(ks[5], (Hkv * D,), jnp.float32) * s, 'v_bias': jax.random.normal(ks[6], (Hkv * D,), jnp.float32) * s, 'o_project': jax.random.normal(ks[7], (H, Hq * D), jnp.float32) * s, 'ln_weight': jnp.ones((H,), jnp.float32)}
    _L0_attn_all = _L0_attn_setup()
    _L0_attn_in = {k: v for k, v in _L0_attn_all.items() if k in ('q_project', 'k_project', 'v_project', 'q_bias', 'k_bias', 'v_bias', 'o_project', 'ln_weight')}
    del _L0_attn_all

    def _L0_ffn_setup():
        import jax, jax.numpy as jnp
        import numpy as np
        E = 8
        K = 2
        CAP = 128
        H = 512
        F = 2048
        key = jax.random.key(seed)
        ks = jax.random.split(key, 6)
        inp = {'hidden_states': jax.random.normal(ks[0], (2, 256, H), jnp.float32), 'router_w': jax.random.normal(ks[1], (E, H), jnp.float32) * (0.01 / np.sqrt(H)), 'w1': jax.random.normal(ks[2], (F, H), jnp.float32) * (1.0 / np.sqrt(H)), 'b1': jax.random.normal(ks[3], (F,), jnp.float32) * 0.01, 'w2': jax.random.normal(ks[4], (H, F), jnp.float32) * (1.0 / np.sqrt(F)), 'b2': jax.random.normal(ks[5], (H,), jnp.float32) * 0.01}
        return inp
    _L0_ffn_all = _L0_ffn_setup()
    _L0_ffn_in = {k: v for k, v in _L0_ffn_all.items() if k in ('router_w', 'w1', 'b1', 'w2', 'b2')}
    del _L0_ffn_all
    return {'x': x, 'ctx_1024': ctx_1024, 'L0_xattn_Wq': _L0_xattn_in['Wq'], 'L0_xattn_bq': _L0_xattn_in['bq'], 'L0_xattn_Wk': _L0_xattn_in['Wk'], 'L0_xattn_bk': _L0_xattn_in['bk'], 'L0_xattn_Wv': _L0_xattn_in['Wv'], 'L0_xattn_bv': _L0_xattn_in['bv'], 'L0_xattn_Wkv_dca': _L0_xattn_in['Wkv_dca'], 'L0_xattn_bkv_dca': _L0_xattn_in['bkv_dca'], 'L0_xattn_qn_w': _L0_xattn_in['qn_w'], 'L0_xattn_qn_b': _L0_xattn_in['qn_b'], 'L0_xattn_kn_w': _L0_xattn_in['kn_w'], 'L0_xattn_kn_b': _L0_xattn_in['kn_b'], 'L0_xattn_kn_dca_w': _L0_xattn_in['kn_dca_w'], 'L0_xattn_kn_dca_b': _L0_xattn_in['kn_dca_b'], 'L0_xattn_Wo': _L0_xattn_in['Wo'], 'L0_xattn_bo': _L0_xattn_in['bo'], 'L0_attn_q_project': _L0_attn_in['q_project'], 'L0_attn_k_project': _L0_attn_in['k_project'], 'L0_attn_v_project': _L0_attn_in['v_project'], 'L0_attn_q_bias': _L0_attn_in['q_bias'], 'L0_attn_k_bias': _L0_attn_in['k_bias'], 'L0_attn_v_bias': _L0_attn_in['v_bias'], 'L0_attn_o_project': _L0_attn_in['o_project'], 'L0_attn_ln_weight': _L0_attn_in['ln_weight'], 'L0_ffn_router_w': _L0_ffn_in['router_w'], 'L0_ffn_w1': _L0_ffn_in['w1'], 'L0_ffn_b1': _L0_ffn_in['b1'], 'L0_ffn_w2': _L0_ffn_in['w2'], 'L0_ffn_b2': _L0_ffn_in['b2']}

def reference(x, ctx_1024, L0_xattn_Wq, L0_xattn_bq, L0_xattn_Wk, L0_xattn_bk, L0_xattn_Wv, L0_xattn_bv, L0_xattn_Wkv_dca, L0_xattn_bkv_dca, L0_xattn_qn_w, L0_xattn_qn_b, L0_xattn_kn_w, L0_xattn_kn_b, L0_xattn_kn_dca_w, L0_xattn_kn_dca_b, L0_xattn_Wo, L0_xattn_bo, L0_attn_q_project, L0_attn_k_project, L0_attn_v_project, L0_attn_q_bias, L0_attn_k_bias, L0_attn_v_bias, L0_attn_o_project, L0_attn_ln_weight, L0_ffn_router_w, L0_ffn_w1, L0_ffn_b1, L0_ffn_w2, L0_ffn_b2):
    import jax
    import jax.numpy as jnp

    def _L0_xattn_ref(x, y, Wq, bq, Wk, bk, Wv, bv, Wkv_dca, bkv_dca, qn_w, qn_b, kn_w, kn_b, kn_dca_w, kn_dca_b, Wo, bo):
        import jax, jax.numpy as jnp
        import numpy as np
        B, S1, S2, DCA = (2, 512, 256, 16)
        QDIM, KDIM, H = (512, 256, 16)
        HD = QDIM // H
        SCALE = HD ** (-0.5)
        EPS = 1e-06
        DCA_WEIGHT = 1.0

        def _ln(t, w, b):
            m = jnp.mean(t, axis=-1, keepdims=True)
            v = jnp.var(t, axis=-1, keepdims=True)
            return (t - m) * jax.lax.rsqrt(v + EPS) * w + b

        def _attn(q, k, v):
            s = jnp.einsum('bhqd,bhkd->bhqk', q, k) * SCALE
            p = jax.nn.softmax(s, axis=-1)
            return jnp.einsum('bhqk,bhkd->bhqd', p, v)
        b, s1, _ = x.shape
        y_dca = y[:, -DCA:, :]
        y_main = y[:, :-DCA, :]
        kv_dca = (y_dca @ Wkv_dca + bkv_dca).reshape(b, DCA, 2, H, HD)
        k_dca = _ln(kv_dca[:, :, 0], kn_dca_w, kn_dca_b)
        v_dca = kv_dca[:, :, 1]
        s2 = y_main.shape[1]
        q = _ln((x @ Wq + bq).reshape(b, s1, H, HD), qn_w, qn_b)
        kv = jnp.concatenate([y_main @ Wk + bk, y_main @ Wv + bv], axis=-1)
        kv = kv.reshape(b, s2, H, 2 * HD)
        k = _ln(kv[..., :HD], kn_w, kn_b)
        v = kv[..., HD:]
        qT = q.transpose(0, 2, 1, 3)
        ctx = _attn(qT, k.transpose(0, 2, 1, 3), v.transpose(0, 2, 1, 3))
        ctx = ctx.transpose(0, 2, 1, 3).reshape(b, s1, QDIM)
        ctx_dca = _attn(qT, k_dca.transpose(0, 2, 1, 3), v_dca.transpose(0, 2, 1, 3))
        ctx_dca = ctx_dca.transpose(0, 2, 1, 3).reshape(b, s1, QDIM)
        ctx = ctx + DCA_WEIGHT * ctx_dca
        return ctx @ Wo + bo

    def _L0_attn_ref(x, q_project, k_project, v_project, q_bias, k_bias, v_bias, o_project, ln_weight):
        import jax, jax.numpy as jnp
        import numpy as np
        EPS = 1e-06
        ROPE_BASE = 10000.0

        def _rmsnorm(x, w):
            var = jnp.mean(x * x, axis=-1, keepdims=True)
            return x * jax.lax.rsqrt(var + EPS) * w

        def _rope(t):
            S, D = (t.shape[-2], t.shape[-1])
            inv_freq = 1.0 / ROPE_BASE ** (jnp.arange(0, D, 2, dtype=jnp.float32) / D)
            ang = jnp.arange(S, dtype=jnp.float32)[:, None] * inv_freq
            cos = jnp.concatenate([jnp.cos(ang), jnp.cos(ang)], axis=-1)
            sin = jnp.concatenate([jnp.sin(ang), jnp.sin(ang)], axis=-1)
            t1, t2 = jnp.split(t, 2, axis=-1)
            rot = jnp.concatenate([-t2, t1], axis=-1)
            return t * cos + rot * sin
        B, S, _ = x.shape
        Hq, Hkv, D = (16, 4, 128)
        rep = Hq // Hkv
        h = _rmsnorm(x, ln_weight)
        q = h @ q_project.T + q_bias
        k = h @ k_project.T + k_bias
        v = h @ v_project.T + v_bias
        q = q.reshape(B, S, Hq, D).transpose(0, 2, 1, 3)
        k = k.reshape(B, S, Hkv, D).transpose(0, 2, 1, 3)
        v = v.reshape(B, S, Hkv, D).transpose(0, 2, 1, 3)
        q = _rope(q)
        k = _rope(k)
        qg = q.reshape(B, Hkv, rep, S, D)
        scale = jnp.float32(1.0) / jnp.sqrt(jnp.float32(D))
        scores = jnp.einsum('bgrqd,bgkd->bgrqk', qg, k) * scale
        mask = jnp.where(jnp.tril(jnp.ones((S, S), bool)), 0.0, -jnp.inf).astype(scores.dtype)
        attn = jax.nn.softmax(scores + mask, axis=-1)
        out = jnp.einsum('bgrqk,bgkd->bgrqd', attn, v)
        out = out.reshape(B, Hq, S, D).transpose(0, 2, 1, 3).reshape(B, S, Hq * D)
        return out @ o_project.T

    def _L0_ffn_ref(hidden_states, router_w, w1, b1, w2, b2):
        import jax, jax.numpy as jnp
        import numpy as np
        E = 8
        K = 2
        CAP = 128
        H = 512
        F = 2048
        orig_shape = hidden_states.shape
        x = hidden_states.reshape(-1, H)
        N = x.shape[0]
        logits = x @ router_w.T
        probs = jax.nn.softmax(logits, axis=-1)
        top_p, top_i = jax.lax.top_k(probs, K)
        expert_flat = top_i.T.reshape(-1)
        probs_flat = top_p.T.reshape(-1)
        token_idx = jnp.tile(jnp.arange(N), K)
        onehot = (expert_flat[:, None] == jnp.arange(E)[None, :]).astype(jnp.int32)
        pos = jnp.take_along_axis(jnp.cumsum(onehot, axis=0), expert_flat[:, None], axis=1)[:, 0] - 1
        keep = pos < CAP
        dest = expert_flat * CAP + pos
        dest_m = jnp.where(keep, dest, E * CAP)
        buf = jnp.zeros((E * CAP, H), x.dtype).at[dest_m].set(x[token_idx], mode='drop')
        h = jax.nn.gelu(buf @ w1.T + b1, approximate=False) @ w2.T + b2
        gathered = jnp.where(keep[:, None], h[jnp.where(keep, dest, 0)], 0.0) * probs_flat[:, None]
        out = jnp.zeros_like(x).at[token_idx].add(gathered)
        return out.reshape(orig_shape)
    x = x + _L0_xattn_ref(_layernorm(x, axis=-1), ctx_1024, L0_xattn_Wq, L0_xattn_bq, L0_xattn_Wk, L0_xattn_bk, L0_xattn_Wv, L0_xattn_bv, L0_xattn_Wkv_dca, L0_xattn_bkv_dca, L0_xattn_qn_w, L0_xattn_qn_b, L0_xattn_kn_w, L0_xattn_kn_b, L0_xattn_kn_dca_w, L0_xattn_kn_dca_b, L0_xattn_Wo, L0_xattn_bo)
    x = x + _L0_attn_ref(_layernorm(x, axis=-1), L0_attn_q_project, L0_attn_k_project, L0_attn_v_project, L0_attn_q_bias, L0_attn_k_bias, L0_attn_v_bias, L0_attn_o_project, L0_attn_ln_weight)
    x = x + _L0_ffn_ref(_layernorm(x, axis=-1), L0_ffn_router_w, L0_ffn_w1, L0_ffn_b1, L0_ffn_w2, L0_ffn_b2)
    return x

_drawn_inputs = setup_inputs


def setup_inputs(seed=0):
    import zlib

    import numpy as np

    out = dict(_drawn_inputs(seed))
    spreads = {'L0_xattn_bq': (0.0, 0.517),
     'L0_xattn_bk': (0.0, 0.1),
     'L0_xattn_bv': (0.0, 0.1),
     'L0_xattn_bkv_dca': (0.0, 0.1),
     'L0_xattn_qn_w': (1.0, 0.6),
     'L0_xattn_qn_b': (0.0, 0.8),
     'L0_xattn_kn_w': (1.0, 0.6),
     'L0_xattn_kn_b': (0.0, 2.0),
     'L0_xattn_kn_dca_w': (1.0, 0.6),
     'L0_xattn_kn_dca_b': (0.0, 2.0),
     'L0_xattn_bo': (0.0, 0.1),
     'L0_attn_ln_weight': (1.0, 0.2)}
    factors = {'L0_attn_q_bias': 43.815, 'L0_attn_k_bias': 64.0, 'L0_ffn_b1': 64.0, 'L0_ffn_b2': 40.661}
    for name, (base, spread) in spreads.items():
        noise = np.random.default_rng([zlib.crc32(name.encode()), seed]).standard_normal(out[name].shape)
        drawn = base * np.exp(spread * noise) if base else spread * noise
        out[name] = jnp.asarray(drawn.astype(out[name].dtype))
    for name, factor in factors.items():
        out[name] = (out[name] * factor).astype(out[name].dtype)
    return out
```

```python
from contextlib import ExitStack

import numpy as np

import concourse.bass as bass
from concourse import mybir

F32 = mybir.dt.float32
I32 = mybir.dt.int32
ALU = mybir.AluOpType
ACT = mybir.ActivationFunctionType
AX = mybir.AxisListType

P = 128
B, S, H = 16, 64, 512
TOK = B * S
TILES = TOK // P
HC = H // P
KEYS, KD = 1601, 256
DCA = 16
MAIN = KEYS - DCA
XH, XD = 16, 32
KDC = KD // P
KT_FULL = MAIN // P
KTILES = KT_FULL + 1
DCA_AT = KT_FULL * P + 64
KCOLS = DCA_AT + DCA
LAST = KCOLS - KT_FULL * P
SCH = KCOLS // 4
MAIN3 = MAIN - 3 * SCH
XSCALE = float(XD) ** -0.5
HQ, HKV, D = 16, 4, 128
REP = HQ // HKV
SSCALE = float(1.0 / np.sqrt(np.float32(D)))
E, CAP, F = 8, 128, 2048
FC = F // P
LN_EPS, QK_EPS, RMS_EPS = 1e-5, 1e-6, 1e-6
MASKED = -1e30
PAIRS = 4
KTS = (KTILES + 1) // 2
USES = 2 * KTS
CHUNKS = ((0, 8), (8, KTILES))


def rsqrt(link, v, x, y, t):
    link(v.tensor_scalar(t.bitcast(I32), x.bitcast(I32), 1, None, ALU.logical_shift_right))
    link(v.tensor_scalar(y.bitcast(I32), t.bitcast(I32), -1.0, 1597463007.0, ALU.mult, ALU.add))
    for _ in range(3):
        link(v.tensor_tensor(t, y, y, ALU.mult))
        link(v.scalar_tensor_tensor(t, t, -0.5, x, ALU.mult, ALU.mult))
        link(v.scalar_tensor_tensor(y, t, 1.5, y, ALU.add, ALU.mult))


def chain(eng, sem):
    count = [0]

    def link(instruction):
        count[0] += 1
        instruction.then_inc(sem, 1)
        eng.wait_ge(sem, count[0])
    return link


def stage_a(nc, x, qT, ident, a):
    with ExitStack() as ctx:
        def sb(name, shape):
            return ctx.enter_context(nc.sbuf_tensor(name, shape, F32))

        def sem(name):
            return ctx.enter_context(nc.semaphore(name))

        wq = sb("wq", [P, HC, H])
        bq = sb("bq", [P, H])
        qnw = sb("qnw", [P, 1])
        qnb = sb("qnb", [P, 1])
        xn = sb("xn", [P, 2, H])
        xnT = sb("xnT", [P, 2, HC, P])
        q = sb("q", [P, TILES, H])
        sq = sb("sq_a", [P, TILES, H])
        stats = sb("stats_a", [P, TILES, 6])
        mv = sb("mv_a", [P, TILES, 2])
        r1 = sb("r1_a", [P, TILES])
        v1 = sb("v1_a", [P, TILES])
        t1 = sb("t1_a", [P, TILES])
        qm = sb("qm", [P, TILES * XH])
        qv = sb("qv", [P, TILES * XH])
        qr = sb("qr", [P, TILES * XH])
        qt = sb("qt", [P, TILES * XH])
        ps_t = [ctx.enter_context(nc.psum_tensor(f"a_t{i}", [P, H], F32)) for i in range(2)]
        ps_q = [ctx.enter_context(nc.psum_tensor(f"a_q{i}", [P, H], F32)) for i in range(2)]
        s_x, s_w, s_ch = sem("a_x"), sem("a_w"), sem("a_chain")
        xn_ready, xT_ready, xT_copied, q_ready = sem("xn_ready"), sem("xT_ready"), sem("xT_copied"), sem("q_ready")
        q_copied, qn_ready, qT_ready, qT_copied = sem("q_copied"), sem("qn_ready"), sem("qT_ready"), sem("qT_copied")
        block = ctx.enter_context(nc.Block())

        @block.sync
        def _(sp):
            sp.dma_start(x[:, :, :], a["x"]).then_inc(s_x, 16)
            sp.dma_start(ident[:, :], a["ident"]).then_inc(s_w, 16)
            sp.dma_start(wq[:, :, :], a["wq"]).then_inc(s_w, 16)
            sp.dma_start(bq[:, :], a["bq"]).then_inc(s_w, 16)
            sp.dma_start(qnw[:, :], a["qnw"]).then_inc(s_w, 16)
            sp.dma_start(qnb[:, :], a["qnb"]).then_inc(s_w, 16)

        @block.vector
        def _(dve):
            v = nc.vector
            link = chain(dve, s_ch)
            dve.wait_ge(s_x, 16)
            for t in range(TILES):
                link(v.bn_stats(stats[:, t, :], x[:, t, :]))
            for t in range(TILES):
                link(v.bn_aggr(mv[:, t, :], stats[:, t, :]))
            link(v.tensor_scalar(v1[:, :], mv[:, :, 1], LN_EPS, None, ALU.add))
            rsqrt(link, v, v1[:, :], r1[:, :], t1[:, :])
            dve.wait_ge(s_w, 80)

            def q_bias(t):
                dve.wait_ge(q_ready, t + 1)
                v.tensor_tensor(q[:, t, :], ps_q[t % 2][:, :], bq[:, :], ALU.add).then_inc(q_copied, 1)

            for t in range(TILES):
                if t >= 2:
                    dve.wait_ge(xT_ready, t - 1)
                v.tensor_scalar(xn[:, t % 2, :], x[:, t, :], mv[:, t, 0:1], r1[:, t:t + 1],
                                ALU.subtract, ALU.mult).then_inc(xn_ready, 1)
                if t:
                    q_bias(t - 1)
            q_bias(TILES - 1)
            dve.wait_ge(q_copied, TILES)
            heads = q[:, :, :].rearrange("p t (h d) -> p (t h) d", d=XD)
            sqh = sq[:, :, :].rearrange("p t (h d) -> p (t h) d", d=XD)
            link(v.tensor_reduce(qm[:, :], heads, AX.X, ALU.add))
            link(v.tensor_scalar(qm[:, :], qm[:, :], -1.0 / XD, None, ALU.mult))
            mean = qm[:, :].rearrange("p (n o) -> p n o", o=1).broadcast_to([P, TILES * XH, XD])
            link(v.tensor_tensor(heads, heads, mean, ALU.add))
            link(v.tensor_tensor(sqh, heads, heads, ALU.mult))
            link(v.tensor_reduce(qv[:, :], sqh, AX.X, ALU.add))
            link(v.tensor_scalar(qv[:, :], qv[:, :], 1.0 / XD, QK_EPS, ALU.mult, ALU.add))
            rsqrt(link, v, qv[:, :], qr[:, :], qt[:, :])
            for t in range(TILES):
                ht = q[:, t, :].rearrange("p (h d) -> p h d", d=XD)
                rt = qr[:, t * XH:(t + 1) * XH].rearrange("p (n o) -> p n o", o=1).broadcast_to([P, XH, XD])
                v.tensor_tensor(ht, ht, rt, ALU.mult).then_inc(qn_ready, 1)

        @block.scalar
        def _(act):
            for t in range(TILES):
                act.wait_ge(xT_ready, t + 1)
                if t >= 2:
                    act.wait_ge(q_ready, t - 1)
                nc.scalar.activation(xnT[:, t % 2, :, :].rearrange("p c n -> p (c n)"), ps_t[t % 2][:, :],
                                     ACT.Copy).then_inc(xT_copied, 1)
            act.wait_ge(s_w, 80)
            for t in range(TILES):
                act.wait_ge(qT_ready, t + 1)
                nc.scalar.activation(qT[:, :, t * P:(t + 1) * P],
                                     ps_t[t % 2][:, :].rearrange("p (g n) -> p g n", n=P), ACT.Identity,
                                     bias=qnb[:, 0:1], scale=qnw[:, 0:1]).then_inc(qT_copied, 1)

        @block.tensor
        def _(pe):
            pe.wait_ge(s_w, 80)

            def project(t):
                pe.wait_ge(xT_copied, t + 1)
                if t >= 2:
                    pe.wait_ge(q_copied, t - 1)
                for c in range(HC):
                    last = nc.tensor.matmul(ps_q[t % 2][:, :], xnT[:, t % 2, c, :], wq[:, c, :],
                                            start=c == 0, stop=c == HC - 1)
                last.then_inc(q_ready, 1)

            for t in range(TILES):
                pe.wait_ge(xn_ready, t + 1)
                if t >= 2:
                    pe.wait_ge(xT_copied, t - 1)
                for c in range(HC):
                    last = nc.tensor.transpose(ps_t[t % 2][:, c * P:(c + 1) * P], xn[:, t % 2, c * P:(c + 1) * P],
                                               ident[:, :])
                last.then_inc(xT_ready, 1)
                if t:
                    project(t - 1)
            project(TILES - 1)
            for t in range(TILES):
                pe.wait_ge(qn_ready, t + 1)
                pe.wait_ge(xT_copied, TILES)
                if t >= 2:
                    pe.wait_ge(qT_copied, t - 1)
                for g in range(HC):
                    last = nc.tensor.transpose(ps_t[t % 2][:, g * P:(g + 1) * P], q[:, t, g * P:(g + 1) * P],
                                               ident[:, :])
                last.then_inc(qT_ready, 1)


def stage_b(nc, qT, ctxT, ident, a):
    with ExitStack() as ctx:
        def sb(name, shape):
            return ctx.enter_context(nc.sbuf_tensor(name, shape, F32))

        def sem(name):
            return ctx.enter_context(nc.semaphore(name))

        HW = 8 * XD
        wm = sb("w_main", [P, KDC, 2, 2 * HW])
        wd = sb("w_dca", [P, KDC, 2, 2 * HW])
        bkm = sb("bk_main", [P, 2, HW])
        bkd = sb("bk_dca", [P, 2, HW])
        cols = sb("cols", [P, 12])
        mean_w = sb("mean_w", [P, 4, 8])
        yT = sb("yT", [P, KDC, KCOLS])
        Kc = sb("Kc", [P, KTILES, HW])
        Sq = sb("Sq", [P, 8, HW])
        kT = sb("kT", [P, 2, 2, KCOLS])
        V = sb("V", [P, 2, KTILES, HW])
        qb = sb("qb", [P, 4, 2, P])
        Pr = sb("Pr", [P, PAIRS, KCOLS])
        PTs = sb("PTs", [P, 2, 512])
        nb = sb("nb", [P, PAIRS, 3])
        nbs = sb("nbs", [P, PAIRS, 2])
        sums = sb("sums", [P, PAIRS, 3])
        ls = sb("ls", [P, PAIRS, 2])
        linv = sb("linv", [P, PAIRS, 2])
        var = sb("var", [P, 64])
        rst = sb("rst", [P, 64])
        ntmp = sb("ntmp", [P, 64])
        ps_s = ctx.enter_context(nc.psum_tensor("ps_s", [P, 4, 512], F32))
        ps_d = ctx.enter_context(nc.psum_tensor("ps_d", [P, 512], F32))
        ps_a = ctx.enter_context(nc.psum_tensor("ps_a", [P, 512], F32))
        ps_v = ctx.enter_context(nc.psum_tensor("ps_v", [P, 512], F32))
        ps_k = ctx.enter_context(nc.psum_tensor("ps_k", [P, 512], F32))
        s_w = sem("b_w")
        s_y = [sem(f"b_y{c}") for c in range(3)]
        dve_chain, pool_chain = sem("dve_chain"), sem("pool_chain")
        w_centred, pads_zero = sem("w_centred"), sem("pads_zero")
        d_filled, a_filled, d_read, a_read = sem("d_filled"), sem("a_filled"), sem("d_read"), sem("a_read")
        s_done, bias_ready, exp_done, linv_ready, p_scaled = (
            sem("s_done"), sem("bias_ready"), sem("exp_done"), sem("linv_ready"), sem("p_scaled"))
        sq_done, var_ready, kn_ready = sem("sq_done"), sem("var_ready"), sem("kn_ready")
        kT_done, kT_copied, pv_done, ctx_copied, qb_ready = (
            sem("kT_done"), sem("kT_copied"), sem("pv_done"), sem("ctx_copied"), sem("qb_ready"))
        tile_bounds = ((0, 4), (4, 8), (8, KTILES))
        block = ctx.enter_context(nc.Block())

        def units(body, fori):
            with fori(0, B - 1) as i:
                body(i * 2, 0, True)
                body(i * 2, 1, True)
            body(2 * (B - 1), 0, True)
            body(2 * (B - 1), 1, False)

        @block.sync
        def _(sp):
            for dst, name in ((wm, "wm"), (wd, "wd"), (bkm, "bkm"), (bkd, "bkd"), (cols, "cols")):
                sp.dma_start(dst[tuple([slice(None)] * len(dst.shape))], a[name]).then_inc(s_w, 16)
            y0 = a["yT"][0:1, :, :, :].rearrange("b p c n -> p (b c) n")
            for c, (t0, t1) in enumerate(tile_bounds):
                n0, n1 = t0 * P, min(t1 * P, KCOLS)
                sp.dma_start(yT[:, :, n0:n1], y0[:, :, n0:n1]).then_inc(s_y[c], 16)
            with sp.Fori(1, B) as b:
                yb = a["yT"][bass.ds(b, 1), :, :, :].rearrange("b p c n -> p (b c) n")
                for c, (t0, t1) in enumerate(tile_bounds):
                    n0, n1 = t0 * P, min(t1 * P, KCOLS)
                    uses = (t1 + 1) // 2 + (KTS // 2 if c == 2 else 0)
                    sp.wait_ge(a_filled, (b - 1) * (2 * USES) + (KTS + uses))
                    sp.dma_start(yT[:, :, n0:n1], yb[:, :, n0:n1]).then_inc(s_y[c], 16)

        @block.tensor
        def _(pe):
            def project(r0, kd, ka, par, m, y_wait):
                for kv, bank, read, filled, k in ((0, ps_d, d_read, d_filled, kd), (1, ps_a, a_read, a_filled, ka)):
                    if not isinstance(r0, int) or r0 + k >= 1:
                        pe.wait_ge(read, r0 + k)
                    for i in range(2):
                        t = min(2 * m + i, KTILES - 1)
                        n = P if t < KT_FULL else LAST
                        w = wm if 2 * m + i < KTILES else wd
                        if kv == 0 and i == 0 and y_wait is not None:
                            for c, (t0, _) in enumerate(tile_bounds):
                                if t == t0:
                                    pe.wait_ge(s_y[c], y_wait)
                        for c in range(KDC):
                            last = nc.tensor.matmul(bank[0:n, i * HW:(i + 1) * HW], yT[:, c, t * P:t * P + n],
                                                    w[:, c, par, kv * HW:(kv + 1) * HW],
                                                    start=c == 0, stop=c == KDC - 1)
                    last.then_inc(filled, 1)

            def key_transposes(w0, dw, j):
                pe.wait_ge(kn_ready, (w0 + dw) * KTS + (j + 1))
                if not isinstance(w0, int) or (w0 + dw) * KTS + j >= 1:
                    pe.wait_ge(kT_copied, (w0 + dw) * KTS + j)
                for t in range(2 * j, min(2 * j + 2, KTILES)):
                    n = P if t < KT_FULL else LAST
                    for g in range(2):
                        at = g * 256 + (t % 2) * P
                        last = nc.tensor.transpose(ps_k[:, at:at + n], Kc[0:n, t, g * P:(g + 1) * P],
                                                   ident[0:n, 0:n])
                last.then_inc(kT_done, 1)

            pe.wait_ge(w_centred, 1)
            for m in range(KTS):
                project(0, m, m, 0, m, 16)
            for j in range(KTS):
                key_transposes(0, 0, j)

            def slot(u0, par, produce):
                r0 = (u0 + par) * USES + KTS

                def scores(p):
                    g, i = p // 2, p % 2
                    pe.wait_ge(exp_done, (u0 + par) * PAIRS + (p + 1))
                    if p == 0:
                        pe.wait_ge(kT_copied, (u0 + (par + 1)) * KTS)
                        if par == 0:
                            pe.wait_ge(qb_ready, u0 * 2 + 4)
                    for c in range(4):
                        last = nc.tensor.matmul(ps_s[:, c, 0:SCH], qb[:, 2 * par + g, i, :],
                                                kT[:, par, g, c * SCH:(c + 1) * SCH], start=True, stop=True)
                    last.then_inc(s_done, 1)

                def attend(g, kd, ka):
                    pe.wait_ge(p_scaled, (u0 + par) * PAIRS + (2 * g + 2))
                    place = [((j + g) % 2, (kd, ka)[(j + g) % 2] + j // 2) for j in range(KTS)]

                    def turn(j):
                        on_act, k = place[j]
                        bank = ps_a if on_act else ps_d
                        pe.wait_ge(a_read if on_act else d_read, r0 + k)
                        for t in range(2 * j, min(2 * j + 2, KTILES)):
                            n = P if t < KT_FULL else LAST
                            for i in range(2):
                                at = (t % 2) * 256 + i * P
                                last = nc.tensor.transpose(bank[0:n, at:at + P],
                                                           Pr[:, 2 * g + i, t * P:t * P + n], ident[:, :])
                        last.then_inc(a_filled if on_act else d_filled, 1)

                    def weigh(j):
                        on_act, k = place[j]
                        pe.wait_ge(a_read if on_act else d_read, r0 + (k + 1))
                        for t in range(2 * j, min(2 * j + 2, KTILES)):
                            n = P if t < KT_FULL else LAST
                            last = nc.tensor.matmul(ps_v[:, 0:256], V[0:n, par, t, g * P:(g + 1) * P],
                                                    PTs[0:n, on_act, (t % 2) * 256:(t % 2) * 256 + 256],
                                                    start=t == 0, stop=t == KTILES - 1)
                        return last

                    turn(0)
                    if g == 1 or par == 1:
                        pe.wait_ge(ctx_copied, (u0 + par) * 2 + g)
                    for j in range(KTS):
                        if j + 1 < KTS:
                            turn(j + 1)
                        last = weigh(j)
                    last.then_inc(pv_done, 1)

                y_wait = (u0 * 8 + 32) if par else None
                nxt = 1 - par
                k = 4 if produce else 0
                scores(0)
                if produce:
                    project(r0, 0, 0, nxt, 0, y_wait)
                    project(r0, 1, 1, nxt, 1, y_wait)
                scores(1)
                if produce:
                    project(r0, 2, 2, nxt, 2, y_wait)
                    project(r0, 3, 3, nxt, 3, y_wait)
                scores(2)
                attend(0, k, k)
                if produce:
                    for j in range(4):
                        key_transposes(u0, par + 1, j)
                scores(3)
                kd, ka = k + (KTS + 1) // 2, k + KTS // 2
                if produce:
                    for m in range(4, KTS):
                        project(r0, kd, ka, nxt, m, y_wait)
                        kd, ka = kd + 1, ka + 1
                attend(1, kd, ka)
                if produce:
                    for j in range(4, KTS):
                        key_transposes(u0, par + 1, j)

            units(slot, pe.Fori)

        @block.vector
        def _(dve):
            v = nc.vector
            links = [0]

            def link(instruction, steps=None):
                instruction.then_inc(dve_chain, 1)
                links[0] += 1
                dve.wait_ge(dve_chain, links[0])

            v.memset(Kc[:, KTILES - 1, :], 0.0)
            v.memset(Pr[:, :, MAIN:DCA_AT], 0.0)
            v.memset(qb[:, :, :, :], 0.0).then_inc(pads_zero, 1)
            dve.wait_ge(s_w, 80)
            for wt, bt in ((wm, bkm), (wd, bkd)):
                for c in range(KDC):
                    kw = wt[:, c, :, 0:HW].rearrange("p f (h d) -> p f h d", d=XD)
                    m = mean_w[:, 0:2, :]
                    link(v.tensor_reduce(m, kw, AX.X, ALU.add))
                    link(v.tensor_scalar(m, m, -1.0 / XD, None, ALU.mult))
                    for f in range(2):
                        mf = mean_w[:, f, :].rearrange("p (h o) -> p h o", o=1).broadcast_to([P, 8, XD])
                        link(v.tensor_tensor(kw[:, f, :, :], kw[:, f, :, :], mf, ALU.add))
                bh = bt[:, :, :].rearrange("p f (h d) -> p (f h) d", d=XD)
                m = mean_w[:, 0:2, :].rearrange("p f h -> p (f h)")
                link(v.tensor_reduce(m, bh, AX.X, ALU.add))
                link(v.tensor_scalar(m, m, -1.0 / XD, None, ALU.mult))
                link(v.tensor_tensor(bh, bh, m.rearrange("p (h o) -> p h o", o=1).broadcast_to([P, 16, XD]), ALU.add))
            v.memset(nb[:, :, :], 0.0).then_inc(w_centred, 1)
            chained = links[0]

            def steps(count):
                n = [0]

                def link(instruction):
                    n[0] += 1
                    instruction.then_inc(dve_chain, 1)
                    dve.wait_ge(dve_chain, count + n[0])
                link.made = n
                return link

            def key_bias(r0, k, par, m):
                dve.wait_ge(d_filled, r0 + (k + 1))
                if m < KTS - 1:
                    both = bkm[:, par:par + 1, :].broadcast_to([P, 2, HW])
                    v.tensor_tensor(Kc[:, 2 * m:2 * m + 2, :], ps_d[:, :].rearrange("p (t n) -> p t n", n=HW),
                                    both, ALU.add).then_inc(d_read, 1)
                else:
                    v.tensor_tensor(Kc[0:64, KT_FULL, :], ps_d[0:64, 0:HW], bkm[0:64, par, :], ALU.add)
                    v.tensor_tensor(Kc[64:LAST, KT_FULL, :], ps_d[64:LAST, HW:2 * HW], bkd[64:LAST, par, :],
                                    ALU.add).then_inc(d_read, 1)

            def variance(w0, dw, c, link):
                t0, t1 = CHUNKS[c]
                n = (t1 - t0) * 8
                dve.wait_ge(sq_done, (w0 + dw) * 2 + (c + 1))
                link(v.tensor_reduce(var[:, 0:n], Sq[:, 0:t1 - t0, :].rearrange("p t (h d) -> p (t h) d", d=XD),
                                     AX.X, ALU.add))
                link(v.tensor_scalar(var[:, 0:n], var[:, 0:n], 1.0 / XD, QK_EPS, ALU.mult, ALU.add))
                rsqrt(link, v, var[:, 0:n], rst[:, 0:n], ntmp[:, 0:n])
                v.tensor_copy(ntmp[:, 0:1], rst[:, 0:1]).then_inc(var_ready, 1)

            def keys_out(w0, dw, j, par):
                dve.wait_ge(kT_done, (w0 + dw) * KTS + (j + 1))
                src = ps_k[:, :].rearrange("p (g n) -> p g n", g=2)
                if j < KTS - 1:
                    v.tensor_scalar(kT[:, par, :, j * 256:(j + 1) * 256], src, cols[:, 0:1], cols[:, 1:2],
                                    ALU.mult, ALU.add).then_inc(kT_copied, 1)
                else:
                    v.tensor_scalar(kT[:, par, :, KT_FULL * P:DCA_AT], src[:, :, 0:64], cols[:, 0:1],
                                    cols[:, 1:2], ALU.mult, ALU.add)
                    v.tensor_scalar(kT[:, par, :, DCA_AT:KCOLS], src[:, :, 64:LAST], cols[:, 2:3],
                                    cols[:, 3:4], ALU.mult, ALU.add).then_inc(kT_copied, 1)

            first = steps(chained)
            for m in range(4):
                key_bias(0, m, 0, m)
            variance(0, 0, 0, first)
            for m in range(4, KTS):
                key_bias(0, m, 0, m)
            for j in range(4):
                keys_out(0, 0, j, 0)
            variance(0, 0, 1, first)
            for j in range(4, KTS):
                keys_out(0, 0, j, 0)
            chained += first.made[0]
            per_slot = 2 * 13 + 2 * PAIRS

            def slot(u0, par, produce):
                r0 = (u0 + par) * USES + KTS
                link = steps((u0 + par) * per_slot + chained)
                nxt = 1 - par

                def maxima(p):
                    dve.wait_ge(s_done, (u0 + par) * PAIRS + (p + 1))
                    v.tensor_reduce(nb[:, p, 0:1], ps_s[:, 0:3, 0:SCH], AX.XY, ALU.max, negate=True)
                    v.tensor_reduce(nb[:, p, 1:2], ps_s[:, 3, 0:MAIN3], AX.X, ALU.max, negate=True)
                    link(v.tensor_reduce(nb[:, p, 2:3], ps_s[:, 3, DCA_AT - 3 * SCH:SCH], AX.X, ALU.max,
                                         negate=True))
                    v.tensor_scalar(nbs[:, p, 0:1], nb[:, p, 0:1], nb[:, p, 1:2], XSCALE, ALU.min, ALU.mult)
                    v.tensor_scalar(nbs[:, p, 1:2], nb[:, p, 2:3], XSCALE, None,
                                    ALU.mult).then_inc(bias_ready, 1)

                def inverse(p):
                    dve.wait_ge(exp_done, (u0 + par) * PAIRS + (p + 2))
                    v.tensor_tensor(ls[:, p, 0:1], sums[:, p, 0:1], sums[:, p, 1:2], ALU.add)
                    link(v.tensor_copy(ls[:, p, 1:2], sums[:, p, 2:3]))
                    v.reciprocal(linv[:, p, :], ls[:, p, :]).then_inc(linv_ready, 1)

                def attend(g, k0):
                    for n_use, j in enumerate(range(g, KTS, 2)):
                        dve.wait_ge(d_filled, r0 + (k0 + n_use + 1))
                        n, c1 = (P, 512) if j < KTS - 1 else (LAST, 256)
                        v.tensor_copy(PTs[0:n, 0, 0:c1], ps_d[0:n, 0:c1]).then_inc(d_read, 1)
                    dve.wait_ge(pv_done, (u0 + par) * 2 + (g + 1))
                    gg = 2 * par + g
                    for i in range(4):
                        r = slice(32 * i, 32 * i + 32)
                        last = v.tensor_scalar(ctxT[r, gg, bass.ds(u0 * 32, S)], ps_v[r, 64 * i:64 * i + 64],
                                               cols[r, 4 + gg:5 + gg], cols[r, 8 + gg:9 + gg], ALU.add, ALU.add)
                    last.then_inc(ctx_copied, 1)

                maxima(0)
                if produce:
                    key_bias(r0, 0, nxt, 0)
                    key_bias(r0, 1, nxt, 1)
                inverse(0)
                maxima(1)
                if produce:
                    key_bias(r0, 2, nxt, 2)
                    key_bias(r0, 3, nxt, 3)
                inverse(1)
                if produce:
                    variance(u0, par + 1, 0, link)
                maxima(2)
                k = 4 if produce else 0
                attend(0, k)
                k += (KTS + 1) // 2
                inverse(2)
                if produce:
                    for j in range(4):
                        keys_out(u0, par + 1, j, nxt)
                maxima(3)
                if produce:
                    key_bias(r0, k, nxt, 4)
                inverse(3)
                if produce:
                    for m in range(5, KTS):
                        k += 1
                        key_bias(r0, k, nxt, m)
                    k += 1
                    variance(u0, par + 1, 1, link)
                attend(1, k)
                if produce:
                    for j in range(4, KTS):
                        keys_out(u0, par + 1, j, nxt)
                    assert link.made[0] == per_slot, link.made

            units(slot, dve.Fori)

        @block.scalar
        def _(act):
            s = nc.scalar

            def values_out(r0, k, par, m):
                act.wait_ge(a_filled, r0 + (k + 1))
                if m < KTS - 1:
                    s.activation(V[:, par, 2 * m:2 * m + 2, :], ps_a[:, :].rearrange("p (t n) -> p t n", n=HW),
                                 ACT.Copy).then_inc(a_read, 1)
                else:
                    s.activation(V[0:64, par, KT_FULL, :], ps_a[0:64, 0:HW], ACT.Copy)
                    s.activation(V[64:LAST, par, KT_FULL, :], ps_a[64:LAST, HW:2 * HW],
                                 ACT.Copy).then_inc(a_read, 1)

            def squares(r0, k, c):
                t0, t1 = CHUNKS[c]
                act.wait_ge(d_read, r0 + (k + 1))
                s.activation(Sq[:, 0:t1 - t0, :], Kc[:, t0:t1, :], ACT.Square).then_inc(sq_done, 1)

            for m in range(4):
                values_out(0, m, 0, m)
            squares(0, 3, 0)
            for m in range(4, KTS):
                values_out(0, m, 0, m)
            act.wait_ge(var_ready, 1)
            squares(0, KTS - 1, 1)
            s.activation(sums[:, 0, :], nb[:, 0, :], ACT.Copy).then_inc(exp_done, 1)

            def slot(u0, par, produce):
                r0 = (u0 + par) * USES + KTS
                nxt = 1 - par

                def exps(p):
                    act.wait_ge(bias_ready, (u0 + par) * PAIRS + (p + 1))
                    s.activation(Pr[:, p, 0:3 * SCH].rearrange("p (c n) -> p c n", n=SCH), ps_s[:, 0:3, 0:SCH],
                                 ACT.Exp, bias=nbs[:, p, 0:1], scale=XSCALE, accum_out=sums[:, p, 0:1])
                    s.activation(Pr[:, p, 3 * SCH:MAIN], ps_s[:, 3, 0:MAIN3], ACT.Exp, bias=nbs[:, p, 0:1],
                                 scale=XSCALE, accum_out=sums[:, p, 1:2])
                    s.activation(Pr[:, p, DCA_AT:KCOLS], ps_s[:, 3, DCA_AT - 3 * SCH:SCH], ACT.Exp,
                                 bias=nbs[:, p, 1:2], scale=XSCALE, accum_out=sums[:, p, 2:3]).then_inc(exp_done, 1)

                def attend(g, k0):
                    for n_use, j in enumerate(range(1 - g, KTS, 2)):
                        act.wait_ge(a_filled, r0 + (k0 + n_use + 1))
                        n, c1 = (P, 512) if j < KTS - 1 else (LAST, 256)
                        s.activation(PTs[0:n, 1, 0:c1], ps_a[0:n, 0:c1], ACT.Copy).then_inc(a_read, 1)

                exps(0)
                if produce:
                    values_out(r0, 0, nxt, 0)
                    values_out(r0, 1, nxt, 1)
                exps(1)
                if produce:
                    values_out(r0, 2, nxt, 2)
                    values_out(r0, 3, nxt, 3)
                    squares(r0, 3, 0)
                exps(2)
                k = 4 if produce else 0
                attend(0, k)
                k += KTS // 2
                exps(3)
                if produce:
                    for m in range(4, KTS):
                        values_out(r0, k, nxt, m)
                        k += 1
                    squares(r0, 4 + (KTS + 1) // 2 + 2, 1)
                attend(1, k)

            units(slot, act.Fori)

        @block.gpsimd
        def _(pool):
            g_ = nc.gpsimd

            def normalise(w0, dw, c):
                t0, t1 = CHUNKS[c]
                pool.wait_ge(var_ready, (w0 + dw) * 2 + (c + 1))
                for t in range(t0, t1, 2):
                    n = min(2, t1 - t)
                    kh = Kc[:, t:t + n, :].rearrange("p t (h d) -> p (t h) d", d=XD)
                    rr = rst[:, (t - t0) * 8:(t - t0 + n) * 8].rearrange("p (h o) -> p h o", o=1)
                    g_.tensor_tensor(kh, kh, rr.broadcast_to([P, n * 8, XD]), ALU.mult).then_inc(kn_ready, 1)

            def queries(at, made):
                for i in range(4):
                    r = slice(32 * i, 32 * i + 32)
                    c0 = 64 * (i % 2)
                    g_.tensor_copy(qb[r, :, i // 2, c0:c0 + 64], qT[r, :, bass.ds(at, S)]).then_inc(qb_ready, 1)
                    pool.wait_ge(qb_ready, made + (i + 1))

            pool.wait_ge(pads_zero, 1)
            queries(0, 0)
            normalise(0, 0, 0)
            normalise(0, 0, 1)

            def slot(u0, par, produce):
                def scale(p):
                    pool.wait_ge(linv_ready, (u0 + par) * PAIRS + (p + 1))
                    g_.tensor_tensor(Pr[:, p, DCA_AT:KCOLS], Pr[:, p, DCA_AT:KCOLS],
                                     linv[:, p, 1:2].broadcast_to([P, DCA]), ALU.mult)
                    g_.tensor_scalar(Pr[:, p, 0:MAIN], Pr[:, p, 0:MAIN], linv[:, p, 0:1], 1.0,
                                     ALU.mult, ALU.mult).then_inc(p_scaled, 1)

                scale(0)
                scale(1)
                if produce:
                    normalise(u0, par + 1, 0)
                scale(2)
                scale(3)
                if produce and par == 1:
                    pool.wait_ge(s_done, (u0 + par) * PAIRS + PAIRS)
                    pool.wait_ge(p_scaled, (u0 + par) * PAIRS + PAIRS)
                    queries(u0 * 32 + S, u0 * 2 + 4)
                if produce:
                    normalise(u0, par + 1, 1)

            units(slot, pool.Fori)


def stage_c_norms(nc, x, ctxT, hT, ident, a):
    with ExitStack() as ctx:
        def sb(name, shape):
            return ctx.enter_context(nc.sbuf_tensor(name, shape, F32))

        def sem(name):
            return ctx.enter_context(nc.semaphore(name))

        wo = sb("wo", [P, HC, H])
        bo = sb("bo", [P, H])
        lnw = sb("lnw", [P, H])
        h = sb("h", [P, TILES, H])
        hs = sb("hs", [P, 2, H])
        stats = sb("stats_c", [P, TILES, 6])
        mv = sb("mv_c", [P, TILES, 2])
        v1, r1, t1 = sb("v1_c", [P, TILES]), sb("r1_c", [P, TILES]), sb("t1_c", [P, TILES])
        ss, r2 = sb("ss_c", [P, TILES]), sb("r2_c", [P, TILES])
        ps_o = [ctx.enter_context(nc.psum_tensor(f"c_o{i}", [P, H], F32)) for i in range(2)]
        ps_t = [ctx.enter_context(nc.psum_tensor(f"c_t{i}", [P, H], F32)) for i in range(2)]
        s_w, s_ch = sem("c_w"), sem("c_chain")
        o_done, o_copied, h_ready, sq_done = sem("o_done"), sem("o_copied"), sem("h_ready"), sem("c_sq")
        hn_ready, hT_done, hT_copied = sem("hn_ready"), sem("hT_done"), sem("hT_copied")
        block = ctx.enter_context(nc.Block())

        @block.sync
        def _(sp):
            sp.dma_start(wo[:, :, :], a["wo"]).then_inc(s_w, 16)
            sp.dma_start(bo[:, :], a["bo"]).then_inc(s_w, 16)
            sp.dma_start(lnw[:, :], a["lnw"]).then_inc(s_w, 16)

        @block.tensor
        def _(pe):
            pe.wait_ge(s_w, 48)
            for t in range(TILES):
                if t >= 2:
                    pe.wait_ge(o_copied, t - 1)
                for g in range(HC):
                    last = nc.tensor.matmul(ps_o[t % 2][:, :], ctxT[:, g, t * P:(t + 1) * P], wo[:, g, :],
                                            start=g == 0, stop=g == HC - 1)
                last.then_inc(o_done, 1)
            for t in range(TILES):
                pe.wait_ge(hn_ready, t + 1)
                if t >= 2:
                    pe.wait_ge(hT_copied, t - 1)
                for c in range(HC):
                    last = nc.tensor.transpose(ps_t[t % 2][:, c * P:(c + 1) * P], h[:, t, c * P:(c + 1) * P],
                                               ident[:, :])
                last.then_inc(hT_done, 1)

        @block.vector
        def _(dve):
            v = nc.vector
            link = chain(dve, s_ch)
            dve.wait_ge(s_w, 48)
            for t in range(TILES):
                dve.wait_ge(o_done, t + 1)
                v.tensor_tensor(hs[:, 0, :], ps_o[t % 2][:, :], bo[:, :], ALU.add).then_inc(o_copied, 1)
                dve.wait_ge(o_copied, t + 1)
                link(v.tensor_tensor(x[:, t, :], x[:, t, :], hs[:, 0, :], ALU.add))
                link(v.bn_stats(stats[:, t, :], x[:, t, :]))
            for t in range(TILES):
                link(v.bn_aggr(mv[:, t, :], stats[:, t, :]))
            link(v.tensor_scalar(v1[:, :], mv[:, :, 1], LN_EPS, None, ALU.add))
            rsqrt(link, v, v1[:, :], r1[:, :], t1[:, :])
            for t in range(TILES):
                v.tensor_scalar(h[:, t, :], x[:, t, :], mv[:, t, 0:1], r1[:, t:t + 1],
                                ALU.subtract, ALU.mult).then_inc(h_ready, 1)
            dve.wait_ge(sq_done, TILES)
            link(v.tensor_scalar(ss[:, :], ss[:, :], 1.0 / H, RMS_EPS, ALU.mult, ALU.add))
            rsqrt(link, v, ss[:, :], r2[:, :], t1[:, :])
            for t in range(TILES):
                v.scalar_tensor_tensor(h[:, t, :], h[:, t, :], r2[:, t:t + 1], lnw[:, :],
                                       ALU.mult, ALU.mult).then_inc(hn_ready, 1)

        @block.scalar
        def _(act):
            for t in range(TILES):
                act.wait_ge(h_ready, t + 1)
                nc.scalar.activation(hs[:, 1, :], h[:, t, :], ACT.Square,
                                     accum_out=ss[:, t:t + 1]).then_inc(sq_done, 1)
                act.wait_ge(sq_done, t + 1)
            for t in range(TILES):
                act.wait_ge(hT_done, t + 1)
                nc.scalar.activation(hT[:, :, t * P:(t + 1) * P], ps_t[t % 2][:, :].rearrange("p (c n) -> p c n", n=P),
                                     ACT.Copy).then_inc(hT_copied, 1)


def stage_c_project(nc, hT, qk, a):
    heads = HQ + HKV
    half = TOK // 2
    with ExitStack() as ctx:
        def sb(name, shape):
            return ctx.enter_context(nc.sbuf_tensor(name, shape, F32))

        def sem(name):
            return ctx.enter_context(nc.semaphore(name))

        wqk = sb("wqk", [P, HC, heads * D])
        bqk = sb("bqk", [P, heads])
        rope = sb("rope", [P, 2, S])
        raw, swapped = sb("raw", [P, 2, half]), sb("swapped", [P, 2, half])
        ra, rb = sb("ra", [P, 2, half]), sb("rb", [P, 2, half])
        ps = [ctx.enter_context(nc.psum_tensor(f"cp{i}", [P, half], F32)) for i in range(2)]
        s_w = [sem(f"cp_w{c}") for c in range(3)]
        s_b = sem("cp_b")
        made, raw_ready, cos_ready, sin_ready, qk_ready = (
            sem("cp_made"), sem("raw_ready"), sem("cos_ready"), sem("sin_ready"), sem("qk_ready"))
        s_swap = [sem(f"swap{i}") for i in range(2)]
        block = ctx.enter_context(nc.Block())
        parts = ((0, 2), (2, 8), (8, heads))
        n_steps = 2 * heads

        @block.sync
        def _(sp):
            sp.dma_start(bqk[:, :], a["bqk"]).then_inc(s_b, 16)
            sp.dma_start(rope[:, :, :], a["rope"]).then_inc(s_b, 16)
            for i, (h0, h1) in enumerate(parts):
                sp.dma_start(wqk[:, :, h0 * D:h1 * D], a["wqk"][:, :, h0 * D:h1 * D]).then_inc(s_w[i], 16)
            for n in range(n_steps):
                sp.wait_ge(raw_ready, n + 1)
                if n >= 2:
                    sp.wait_ge(sin_ready, n - 1)
                sp.dma_start(swapped[0:64, n % 2, :], raw[64:P, n % 2, :]).then_inc(s_swap[n % 2], 16)
                sp.dma_start(swapped[64:P, n % 2, :], raw[0:64, n % 2, :]).then_inc(s_swap[n % 2], 16)

        @block.tensor
        def _(pe):
            for n in range(n_steps):
                hd, f = n // 2, n % 2
                for i, (h0, _) in enumerate(parts):
                    if f == 0 and hd == h0:
                        pe.wait_ge(s_w[i], 16)
                if n >= 2:
                    pe.wait_ge(raw_ready, n - 1)
                for c in range(HC):
                    last = nc.tensor.matmul(ps[n % 2][:, :], wqk[:, c, hd * D:(hd + 1) * D],
                                            hT[:, c, f * half:(f + 1) * half], start=c == 0, stop=c == HC - 1)
                last.then_inc(made, 1)

        @block.scalar
        def _(act):
            act.wait_ge(s_b, 32)
            for n in range(n_steps):
                act.wait_ge(made, n + 1)
                if n >= 2:
                    act.wait_ge(cos_ready, n - 1)
                    act.wait_ge(s_swap[n % 2], 32 * (n // 2))
                nc.scalar.activation(raw[:, n % 2, :], ps[n % 2][:, :], ACT.Identity,
                                     bias=bqk[:, n // 2:n // 2 + 1]).then_inc(raw_ready, 1)

        def table(k):
            return rope[:, k:k + 1, :].broadcast_to([P, half // S, S])

        def by_batch(t):
            return t.rearrange("p (b s) -> p b s", s=S)

        @block.vector
        def _(dve):
            dve.wait_ge(s_b, 32)

            def add(n):
                dve.wait_ge(sin_ready, n + 1)
                nc.vector.tensor_tensor(qk[:, n // 2, (n % 2) * half:(n % 2 + 1) * half], ra[:, n % 2, :],
                                        rb[:, n % 2, :], ALU.add).then_inc(qk_ready, 1)

            for n in range(n_steps):
                dve.wait_ge(raw_ready, n + 1)
                if n >= 2:
                    dve.wait_ge(qk_ready, n - 1)
                nc.vector.tensor_tensor(by_batch(ra[:, n % 2, :]), by_batch(raw[:, n % 2, :]), table(0),
                                        ALU.mult).then_inc(cos_ready, 1)
                if n >= 1:
                    if n == 1:
                        dve.wait_ge(cos_ready, 1)
                    dve.wait_ge(cos_ready, n)
                    add(n - 1)
            dve.wait_ge(cos_ready, n_steps)
            add(n_steps - 1)

        @block.gpsimd
        def _(pool):
            pool.wait_ge(s_b, 32)
            for n in range(n_steps):
                pool.wait_ge(s_swap[n % 2], 32 * (n // 2 + 1))
                if n >= 2:
                    pool.wait_ge(qk_ready, n - 1)
                nc.gpsimd.tensor_tensor(by_batch(rb[:, n % 2, :]), by_batch(swapped[:, n % 2, :]), table(1),
                                        ALU.mult).then_inc(sin_ready, 1)


def stage_c_attend(nc, x, hT, qk, ident, a):
    pairs = HQ // 2
    with ExitStack() as ctx:
        def sb(name, shape):
            return ctx.enter_context(nc.sbuf_tensor(name, shape, F32))

        def sem(name):
            return ctx.enter_context(nc.semaphore(name))

        wv = sb("wv", [P, HC, HKV * D])
        wot = sb("wot", [P, HQ, H])
        bv = sb("bv_c", [P, HKV])
        mask = sb("mask", [P, S])
        qs = sb("qs", [P, 2, HQ, S])
        hb = sb("hb", [P, 2, HC, S])
        Vs = sb("Vs", [S, 2, HKV * D])
        sc = sb("sc", [P, 2, pairs, S])
        pr = sb("pr", [P, 2, pairs, S])
        mx, sm = sb("mx", [P, 2, pairs]), sb("sm", [P, 2, pairs])
        pT = sb("pT", [S, 2, HQ * S])
        aT = sb("aT", [P, HQ, P])
        ps_s = [ctx.enter_context(nc.psum_tensor(f"ca_s{i}", [P, pairs, S], F32)) for i in range(2)]
        ps_v = ctx.enter_context(nc.psum_tensor("ca_v", [P, H], F32))
        ps_t = [ctx.enter_context(nc.psum_tensor(f"ca_t{i}", [P, H], F32)) for i in range(2)]
        ps_c = [ctx.enter_context(nc.psum_tensor(f"ca_c{i}", [P, 2, REP * S], F32)) for i in range(2)]
        ps_o = ctx.enter_context(nc.psum_tensor("ca_o", [P, H], F32))
        s_w, s_wo = sem("ca_w"), sem("ca_wo")
        q_staged, s_made, v_made, v_copied, masked = (
            sem("q_staged"), sem("s_made"), sem("v_made"), sem("v_copied"), sem("masked"))
        shifted, expd, p_ready, t_made = sem("shifted"), sem("expd"), sem("p_ready"), sem("t_made")
        t_act, t_dve, c_made, c_act, c_dve, o_made, o_added, soft = (
            sem("t_act"), sem("t_dve"), sem("c_made"), sem("c_act"), sem("c_dve"), sem("o_made"),
            sem("o_added"), sem("soft"))
        block = ctx.enter_context(nc.Block())

        @block.sync
        def _(sp):
            sp.dma_start(wv[:, :, :], a["wv"]).then_inc(s_w, 16)
            sp.dma_start(bv[:, :], a["bv_c"]).then_inc(s_w, 16)
            sp.dma_start(mask[:, :], a["mask"]).then_inc(s_w, 16)
            sp.dma_start(wot[:, :, :], a["wot"]).then_inc(s_wo, 16)

        @block.tensor
        def _(pe):
            def batch(i, par):
                n = i * 2 + par
                pe.wait_ge(q_staged, n * 2 + 2)
                for j in range(pairs):
                    kv = j // 2
                    last = nc.tensor.matmul(ps_s[par][:, j, :], qs[:, par, 2 * j:2 * j + 2, :],
                                            qk[:, HQ + kv, bass.ds(i * P + par * S, S)], start=True, stop=True)
                last.then_inc(s_made, 1)
                if par:
                    pe.wait_ge(v_copied, n)
                for c in range(HC):
                    last = nc.tensor.matmul(ps_v[0:S, :], hb[:, par, c, :], wv[:, c, :],
                                            start=c == 0, stop=c == HC - 1)
                last.then_inc(v_made, 1)

            def attend(i, par):
                n = i * 2 + par
                pe.wait_ge(p_ready, n + 1)
                nc.tensor.transpose(ps_t[0][:, 0:P], pr[:, par, 0:2, :], ident[:, :])
                for j in range(1, pairs):
                    last = nc.tensor.transpose(ps_t[j // 4][0:S, (j % 4) * P:(j % 4 + 1) * P], pr[:, par, j, :],
                                               ident[:, :])
                last.then_inc(t_made, 1)
                pe.wait_ge(t_act, n + 1)
                pe.wait_ge(t_dve, n + 1)
                for kv in range(HKV):
                    last = nc.tensor.matmul(ps_c[kv // 2][:, kv % 2, :], Vs[:, par, kv * D:(kv + 1) * D],
                                            pT[:, par, kv * REP * S:(kv + 1) * REP * S], start=True, stop=True)
                last.then_inc(c_made, 1)

            pe.wait_ge(s_w, 48)
            pe.wait_ge(s_wo, 16)
            with pe.Fori(0, TILES) as i:
                batch(i, 0)
                batch(i, 1)
                attend(i, 0)
                pe.wait_ge(c_act, i * 2 + 1)
                pe.wait_ge(c_dve, i * 2 + 1)
                attend(i, 1)
                pe.wait_ge(c_act, i * 2 + 2)
                pe.wait_ge(c_dve, i * 2 + 2)
                for h in range(HQ):
                    last = nc.tensor.matmul(ps_o[:, :], aT[:, h, :], wot[:, h, :], start=h == 0, stop=h == HQ - 1)
                last.then_inc(o_made, 1)

        @block.scalar
        def _(act):
            s = nc.scalar
            act.wait_ge(s_w, 48)
            with act.Fori(0, TILES) as i:
                for par in range(2):
                    at = bass.ds(i * P + par * S, S)
                    s.activation(qs[:, par, :, :], qk[:, 0:HQ, at], ACT.Copy).then_inc(q_staged, 1)
                    s.activation(hb[:, par, :, :], hT[:, :, at], ACT.Copy).then_inc(q_staged, 1)
                for par in range(2):
                    n = i * 2 + par
                    act.wait_ge(v_made, n + 1)
                    s.activation(Vs[:, par, :], ps_v[0:S, :], ACT.Copy).then_inc(v_copied, 1)
                    act.wait_ge(shifted, n + 1)
                    s.activation(pr[:, par, :, :], sc[:, par, :, :], ACT.Exp, scale=SSCALE).then_inc(expd, 1)
                for par in range(2):
                    n = i * 2 + par
                    act.wait_ge(t_made, n + 1)
                    s.activation(pT[:, par, 0:H], ps_t[0][0:S, :], ACT.Copy).then_inc(t_act, 1)
                    act.wait_ge(c_made, n + 1)
                    for kv in range(2):
                        last = s.activation(aT[:, kv * REP:(kv + 1) * REP, par * S:(par + 1) * S],
                                            ps_c[0][:, kv, :].rearrange("p (h q) -> p h q", q=S), ACT.Identity,
                                            bias=bv[:, kv:kv + 1])
                    last.then_inc(c_act, 1)

        @block.vector
        def _(dve):
            v = nc.vector
            dve.wait_ge(s_w, 48)
            with dve.Fori(0, TILES) as i:
                steps = [0]

                def link(instruction):
                    steps[0] += 1
                    instruction.then_inc(soft, 1)
                    dve.wait_ge(soft, i * 10 + steps[0])

                def shift(par):
                    dve.wait_ge(s_made, i * 2 + (par + 1))
                    m = mask[:, :].rearrange("p (o s) -> p o s", o=1).broadcast_to([P, pairs, S])
                    link(v.tensor_tensor(sc[:, par, :, :], ps_s[par][:, :, :], m, ALU.add))
                    link(v.tensor_reduce(mx[:, par, :], sc[:, par, :, :], AX.X, ALU.max))
                    top = mx[:, par, :].rearrange("p (j o) -> p j o", o=1).broadcast_to([P, pairs, S])
                    v.tensor_tensor(sc[:, par, :, :], sc[:, par, :, :], top, ALU.subtract).then_inc(shifted, 1)

                def norm(par):
                    dve.wait_ge(expd, i * 2 + (par + 1))
                    link(v.tensor_reduce(sm[:, par, :], pr[:, par, :, :], AX.X, ALU.add))
                    link(v.reciprocal(sm[:, par, :], sm[:, par, :]))
                    inv = sm[:, par, :].rearrange("p (j o) -> p j o", o=1).broadcast_to([P, pairs, S])
                    v.tensor_tensor(pr[:, par, :, :], pr[:, par, :, :], inv, ALU.mult).then_inc(p_ready, 1)

                shift(0)
                norm(0)
                shift(1)
                norm(1)
                for par in range(2):
                    n = i * 2 + par
                    dve.wait_ge(t_made, n + 1)
                    v.tensor_copy(pT[:, par, H:2 * H], ps_t[1][0:S, :]).then_inc(t_dve, 1)
                    dve.wait_ge(c_made, n + 1)
                    for kv in range(2, HKV):
                        last = v.tensor_scalar(aT[:, kv * REP:(kv + 1) * REP, par * S:(par + 1) * S],
                                               ps_c[1][:, kv - 2, :].rearrange("p (h q) -> p h q", q=S),
                                               bv[:, kv:kv + 1], None, ALU.add)
                    last.then_inc(c_dve, 1)
                dve.wait_ge(o_made, i + 1)
                xt = x[:, bass.ds(i, 1), :].rearrange("p o n -> p (o n)")
                link(v.tensor_tensor(xt, ps_o[:, :], xt, ALU.add))
                link(v.tensor_copy(sm[:, 0, 0:1], sm[:, 0, 1:2]))
                assert steps[0] == 10, steps


def stage_d(nc, x, xT, ident, a, out):
    with ExitStack() as ctx:
        def sb(name, shape):
            return ctx.enter_context(nc.sbuf_tensor(name, shape, F32))

        def sem(name):
            return ctx.enter_context(nc.semaphore(name))

        TE = TILES * E
        half = TOK // 2
        w1 = sb("w1", [P, HC, F])
        w2 = sb("w2", [P, FC, H])
        b1 = sb("b1", [P, FC])
        b2 = sb("b2", [P, H])
        rw = sb("rw", [P, HC, E])
        tri = sb("tri", [P, 2, P])
        iota = sb("iota", [P, 2, E])
        xf = sb("xf", [P, 2, H])
        hh = sb("hh", [P, FC, TOK])
        stats, mv = sb("stats_d", [P, TILES, 6]), sb("mv_d", [P, TILES, 2])
        v1, r1, t1 = sb("v1_d", [P, TILES]), sb("r1_d", [P, TILES]), sb("t1_d", [P, TILES])
        pp, cand = sb("pp", [P, TILES, E]), sb("cand", [P, TILES, E])
        oh = sb("oh", [P, 2, TILES, E])
        top, pick = sb("top", [P, 2, TILES]), sb("pick", [P, TILES])
        cum, off = sb("cum", [P, 2, TILES, E]), sb("off", [P, 2 * TILES, E])
        tot = sb("tot", [P, 2 * TILES, E])
        room, wt = sb("room", [P, 2, TILES]), sb("wt", [P, TILES])
        y = sb("y", [P, 2, H])
        ps_t = [ctx.enter_context(nc.psum_tensor(f"d_t{i}", [P, H], F32)) for i in range(2)]
        ps_r = ctx.enter_context(nc.psum_tensor("d_r", [P, TILES, E], F32))
        ps_c = ctx.enter_context(nc.psum_tensor("d_c", [P, 2, 2 * TE], F32))
        ps_f = [ctx.enter_context(nc.psum_tensor(f"d_f{i}", [P, half], F32)) for i in range(2)]
        ps_y = [ctx.enter_context(nc.psum_tensor(f"d_y{i}", [P, H], F32)) for i in range(2)]
        s_w, s_w1, s_w2, s_ch = sem("d_w"), sem("d_w1"), sem("d_w2"), sem("d_chain")
        xf_ready, xT_done, xT_copied, logits, r_shift, r_exp = (
            sem("xf_ready"), sem("d_xT_done"), sem("d_xT_copied"), sem("logits"), sem("r_shift"), sem("r_exp"))
        chosen, counted, f_made, f_out, y_made, y_read, y_ready, s_out = (
            sem("chosen"), sem("counted"), sem("f_made"), sem("f_out"), sem("y_made"), sem("y_read"),
            sem("y_ready"), sem("s_out"))
        block = ctx.enter_context(nc.Block())

        @block.sync
        def _(sp):
            for dst, name in ((b1, "b1"), (b2, "b2"), (rw, "rw"), (tri, "tri"), (iota, "iota")):
                sp.dma_start(dst[tuple([slice(None)] * len(dst.shape))], a[name]).then_inc(s_w, 16)
            sp.dma_start(w1[:, :, :], a["w1"]).then_inc(s_w1, 16)
            sp.dma_start(w2[:, :, :], a["w2"]).then_inc(s_w2, 16)
            for t in range(TILES):
                sp.wait_ge(y_ready, t + 1)
                sp.dma_start(out[t, :, :], x[:, t, :]).then_inc(s_out, 16)
            sp.wait_ge(s_out, 16 * TILES)

        @block.vector
        def _(dve):
            v = nc.vector
            link = chain(dve, s_ch)
            for t in range(TILES):
                link(v.bn_stats(stats[:, t, :], x[:, t, :]))
            for t in range(TILES):
                link(v.bn_aggr(mv[:, t, :], stats[:, t, :]))
            link(v.tensor_scalar(v1[:, :], mv[:, :, 1], LN_EPS, None, ALU.add))
            rsqrt(link, v, v1[:, :], r1[:, :], t1[:, :])
            for t in range(TILES):
                if t >= 2:
                    dve.wait_ge(xT_done, t - 1)
                v.tensor_scalar(xf[:, t % 2, :], x[:, t, :], mv[:, t, 0:1], r1[:, t:t + 1],
                                ALU.subtract, ALU.mult).then_inc(xf_ready, 1)

            def over_e(s_):
                return s_.rearrange("p (t o) -> p t o", o=1).broadcast_to([P, TILES, E])

            def experts(k):
                return iota[:, k:k + 1, :].broadcast_to([P, TILES, E])

            dve.wait_ge(s_w, 80)
            dve.wait_ge(logits, 1)
            link(v.tensor_reduce(pick[:, :], ps_r[:, :, :], AX.X, ALU.max))
            v.tensor_tensor(pp[:, :, :], ps_r[:, :, :], over_e(pick[:, :]), ALU.subtract).then_inc(r_shift, 1)
            dve.wait_ge(r_exp, 1)
            link(v.tensor_reduce(pick[:, :], pp[:, :, :], AX.X, ALU.add))
            link(v.reciprocal(pick[:, :], pick[:, :]))
            link(v.tensor_tensor(pp[:, :, :], pp[:, :, :], over_e(pick[:, :]), ALU.mult))
            for k in range(2):
                link(v.tensor_reduce(top[:, k, :], pp[:, :, :], AX.X, ALU.max))
                link(v.tensor_tensor(cand[:, :, :], pp[:, :, :], over_e(top[:, k, :]), ALU.is_equal))
                link(v.tensor_scalar(cand[:, :, :], cand[:, :, :], -100.0, None, ALU.mult))
                link(v.tensor_tensor(cand[:, :, :], cand[:, :, :], experts(1), ALU.add))
                link(v.tensor_reduce(pick[:, :], cand[:, :, :], AX.X, ALU.min))
                link(v.tensor_tensor(oh[:, k, :, :], over_e(pick[:, :]), experts(0), ALU.is_equal))
                if k == 0:
                    link(v.tensor_scalar(cand[:, :, :], oh[:, 0, :, :], -2.0, None, ALU.mult))
                    link(v.tensor_tensor(pp[:, :, :], pp[:, :, :], cand[:, :, :], ALU.add))
            v.memset(off[:, 0, :], 0.0).then_inc(chosen, 1)
            dve.wait_ge(counted, 1)
            link(v.tensor_copy(tot[:, :, :].rearrange("p n e -> p (n e)"), ps_c[:, 1, :]))
            for n in range(1, 2 * TILES):
                link(v.tensor_tensor(off[:, n, :], off[:, n - 1, :], tot[:, n - 1, :], ALU.add))
            flat = cum[:, :, :, :].rearrange("p k t e -> p (k t e)")
            link(v.tensor_tensor(flat, ps_c[:, 0, :], off[:, :, :].rearrange("p n e -> p (n e)"), ALU.add))
            link(v.tensor_tensor(flat, flat, oh[:, :, :, :].rearrange("p k t e -> p (k t e)"), ALU.mult))
            link(v.tensor_reduce(room[:, :, :].rearrange("p k t -> p (k t)"),
                                 cum[:, :, :, :].rearrange("p k t e -> p (k t) e"), AX.X, ALU.add))
            link(v.tensor_scalar(room[:, :, :], room[:, :, :], float(CAP), None, ALU.is_le))
            link(v.tensor_tensor(room[:, :, :], room[:, :, :], top[:, :, :], ALU.mult))
            link(v.tensor_tensor(wt[:, :], room[:, 0, :], room[:, 1, :], ALU.add))
            for t in range(TILES):
                dve.wait_ge(y_made, t + 1)
                v.tensor_tensor(y[:, t % 2, :], ps_y[t % 2][:, :], b2[:, :], ALU.add).then_inc(y_read, 1)
                dve.wait_ge(y_read, t + 1)
                v.scalar_tensor_tensor(x[:, t, :], y[:, t % 2, :], wt[:, t:t + 1], x[:, t, :],
                                       ALU.mult, ALU.add).then_inc(y_ready, 1)

        @block.scalar
        def _(act):
            s = nc.scalar
            for t in range(TILES):
                act.wait_ge(xT_done, t + 1)
                s.activation(xT[:, :, t * P:(t + 1) * P], ps_t[t % 2][:, :].rearrange("p (c n) -> p c n", n=P),
                             ACT.Copy).then_inc(xT_copied, 1)
            act.wait_ge(r_shift, 1)
            s.activation(pp[:, :, :], pp[:, :, :], ACT.Exp).then_inc(r_exp, 1)
            act.wait_ge(s_w, 80)
            for n in range(2 * FC):
                act.wait_ge(f_made, n + 1)
                s.activation(hh[:, n // 2, (n % 2) * half:(n % 2 + 1) * half], ps_f[n % 2][:, :], ACT.Gelu,
                             bias=b1[:, n // 2:n // 2 + 1]).then_inc(f_out, 1)

        @block.tensor
        def _(pe):
            for t in range(TILES):
                pe.wait_ge(xf_ready, t + 1)
                if t >= 2:
                    pe.wait_ge(xT_copied, t - 1)
                for c in range(HC):
                    last = nc.tensor.transpose(ps_t[t % 2][:, c * P:(c + 1) * P], xf[:, t % 2, c * P:(c + 1) * P],
                                               ident[:, :])
                last.then_inc(xT_done, 1)
            pe.wait_ge(s_w, 80)
            pe.wait_ge(xT_copied, TILES)
            for t in range(TILES):
                for c in range(HC):
                    last = nc.tensor.matmul(ps_r[:, t, :], xT[:, c, t * P:(t + 1) * P], rw[:, c, :],
                                            start=c == 0, stop=c == HC - 1)
            last.then_inc(logits, 1)
            pe.wait_ge(s_w1, 16)

            def hidden(n):
                if n >= 2:
                    pe.wait_ge(f_out, n - 1)
                for c in range(HC):
                    last = nc.tensor.matmul(ps_f[n % 2][:, :], w1[:, c, (n // 2) * P:(n // 2 + 1) * P],
                                            xT[:, c, (n % 2) * half:(n % 2 + 1) * half],
                                            start=c == 0, stop=c == HC - 1)
                last.then_inc(f_made, 1)

            for n in range(FC):
                hidden(n)
            pe.wait_ge(chosen, 1)
            for k in range(2):
                last = nc.tensor.matmul(ps_c[:, k, :], tri[:, k, :], oh[:, :, :, :].rearrange("p k t e -> p (k t e)"),
                                        start=True, stop=True)
            last.then_inc(counted, 1)
            for n in range(FC, 2 * FC):
                hidden(n)
            pe.wait_ge(s_w2, 16)
            pe.wait_ge(f_out, 2 * FC)
            for t in range(TILES):
                if t >= 2:
                    pe.wait_ge(y_read, t - 1)
                for f in range(FC):
                    last = nc.tensor.matmul(ps_y[t % 2][:, :], hh[:, f, t * P:(t + 1) * P], w2[:, f, :],
                                            start=f == 0, stop=f == FC - 1)
                last.then_inc(y_made, 1)


def perceiver_layer(nc, a, out):
    with ExitStack() as ctx:
        def sb(name, shape):
            return ctx.enter_context(nc.sbuf_tensor(name, shape, F32))

        x = sb("x_sb", [P, TILES, H])
        up = sb("up", [P, HC, TOK])
        ctxT = sb("ctxT", [P, HC, TOK])
        ident = sb("ident_sb", [P, P])
        stage_a(nc, x, up, ident, a)
        stage_b(nc, up, ctxT, ident, a)
        stage_c_norms(nc, x, ctxT, up, ident, a)
        with nc.sbuf_tensor("qk", [P, HQ + HKV, TOK], F32) as qk:
            stage_c_project(nc, up, qk, a)
            stage_c_attend(nc, x, up, qk, ident, a)
        stage_d(nc, x, up, ident, a, out)


def laid_out(i):
    n = {k.removeprefix("L0_"): np.asarray(v) for k, v in i.items()}
    x = {k: v for k, v in n.items()}
    o = {}
    f32 = np.float32
    o["x"] = x["x"].reshape(TILES, P, H).transpose(1, 0, 2)
    yT = x["ctx_1024"].transpose(0, 2, 1).reshape(B, KDC, P, KEYS)
    y = np.zeros((B, KDC, P, KCOLS), yT.dtype)
    y[..., :MAIN] = yT[..., :MAIN]
    y[..., DCA_AT:] = yT[..., MAIN:]
    o["yT"] = y.transpose(0, 2, 1, 3)
    o["wq"] = x["xattn_Wq"].reshape(HC, P, H).transpose(1, 0, 2)
    o["bq"] = np.broadcast_to(x["xattn_bq"], (P, H))
    rep = P // XD
    o["qnw"] = np.tile(x["xattn_qn_w"], rep)[:, None]
    o["qnb"] = np.tile(x["xattn_qn_b"], rep)[:, None]
    w = np.concatenate([x["xattn_Wk"], x["xattn_Wv"]], 1).reshape(KDC, P, 2, 8, 2, XD)
    o["wm"] = w.transpose(1, 0, 2, 4, 3, 5).reshape(P, KDC, 2, 16 * XD)
    w = x["xattn_Wkv_dca"].reshape(KDC, P, 2, 2, 8, XD)
    o["wd"] = w.transpose(1, 0, 3, 2, 4, 5).reshape(P, KDC, 2, 16 * XD)
    b = np.concatenate([x["xattn_bk"], x["xattn_bv"]]).reshape(XH, 2, XD)
    bd = x["xattn_bkv_dca"].reshape(2, XH, XD)
    o["bkm"] = np.broadcast_to(b[:, 0].reshape(2, 8 * XD), (P, 2, 8 * XD))
    o["bkd"] = np.broadcast_to(bd[0].reshape(2, 8 * XD), (P, 2, 8 * XD))
    norms = [np.tile(x["xattn_" + k], rep)[:, None] for k in ("kn_w", "kn_b", "kn_dca_w", "kn_dca_b")]
    o["cols"] = np.concatenate(norms + [b[:, 1].reshape(4, P).T, bd[1].reshape(4, P).T], 1)
    o["wo"] = x["xattn_Wo"].reshape(HC, P, H).transpose(1, 0, 2)
    o["bo"] = np.broadcast_to(x["xattn_bo"], (P, H))
    o["lnw"] = np.broadcast_to(x["attn_ln_weight"], (P, H))
    w = np.concatenate([x["attn_q_project"], x["attn_k_project"]], 0).T.reshape(HC, P, (HQ + HKV) * D)
    o["wqk"] = w.transpose(1, 0, 2)
    o["bqk"] = np.concatenate([x["attn_q_bias"], x["attn_k_bias"]]).reshape(HQ + HKV, D).T
    o["wv"] = x["attn_v_project"].T.reshape(HC, P, HKV * D).transpose(1, 0, 2)
    o["bv_c"] = x["attn_v_bias"].reshape(HKV, D).T
    o["wot"] = x["attn_o_project"].T.reshape(HQ, P, H).transpose(1, 0, 2)
    o["w1"] = x["ffn_w1"].T.reshape(HC, P, F).transpose(1, 0, 2)
    o["b1"] = x["ffn_b1"].reshape(FC, P).T
    o["w2"] = x["ffn_w2"].T.reshape(FC, P, H).transpose(1, 0, 2)
    o["b2"] = np.broadcast_to(x["ffn_b2"], (P, H))
    o["rw"] = x["ffn_router_w"].T.reshape(HC, P, E).transpose(1, 0, 2)
    inv = (f32(1.0) / np.power(f32(10000.0), np.arange(0, D, 2, dtype=f32) / f32(D))).astype(f32)
    ang = (np.arange(S, dtype=f32)[:, None] * inv).astype(f32)
    cos, sin = np.cos(ang).astype(f32).T, np.sin(ang).astype(f32).T
    o["rope"] = np.stack([np.concatenate([cos, cos]), np.concatenate([-sin, sin])], 1)
    q, k = np.arange(P)[:, None] % S, np.arange(S)[None, :]
    o["mask"] = np.where(k <= q, 0.0, MASKED).astype(f32)
    o["ident"] = np.eye(P, dtype=f32)
    upper = (np.arange(P)[:, None] <= np.arange(P)[None, :]).astype(f32)
    o["tri"] = np.stack([upper, np.ones((P, P), f32)], 1)
    e = np.arange(E, dtype=f32)
    o["iota"] = np.broadcast_to(np.stack([e, e + 100]), (P, 2, E))
    return {k: np.ascontiguousarray(v) for k, v in o.items()}


def kernel(**inputs):
    import concourse.bacc as bacc
    from concourse.bass_utils import run_bass_kernel_spmd

    nc = bacc.Bacc("TRN2", target_bir_lowering=False, num_devices=1)
    arrays = {f"in_{k}": v for k, v in laid_out(inputs).items()}
    a = {k.removeprefix("in_"): nc.dram_tensor(k, v.shape, mybir.dt.from_np(v.dtype), kind="ExternalInput").ap()
         for k, v in arrays.items()}
    out = nc.dram_tensor("out", (TILES, P, H), F32, kind="ExternalOutput").ap()
    perceiver_layer(nc, a, out)
    r = run_bass_kernel_spmd(nc, [arrays], core_ids=[0])
    return r.results[0]["out"].reshape(B, S, H)
```

```python
from contextlib import ExitStack

import numpy as np

import concourse.bass as bass
from concourse import mybir

F32 = mybir.dt.float32
I32 = mybir.dt.int32
F32R = mybir.dt.float32r
ALU = mybir.AluOpType
ACT = mybir.ActivationFunctionType
AX = mybir.AxisListType

P = 128
B, S, H = 16, 64, 512
TOK = B * S
TILES = TOK // P
HC = H // P
KEYS, KD = 1601, 256
DCA = 16
MAIN = KEYS - DCA
XH, XD = 16, 32
KDC = KD // P
KT_FULL = MAIN // P
KTILES = KT_FULL + 1
DCA_AT = KT_FULL * P + 64
KCOLS = DCA_AT + DCA
LAST = KCOLS - KT_FULL * P
SCH = KCOLS // 4
MAIN3 = MAIN - 3 * SCH
XSCALE = float(XD) ** -0.5
HQ, HKV, D = 16, 4, 128
REP = HQ // HKV
SSCALE = float(1.0 / np.sqrt(np.float32(D)))
E, CAP, F = 8, 128, 2048
FC = F // P
LN_EPS, QK_EPS, RMS_EPS = 1e-5, 1e-6, 1e-6
MASKED = -1e30
PAIRS = 4
KTS = (KTILES + 1) // 2
STEPS = 2 * KTS
AHEAD = 3
CHUNKS = ((0, 8), (8, KTILES))


def rsqrt(link, v, x, y, t):
    link(v.tensor_scalar(t.bitcast(I32), x.bitcast(I32), 1, None, ALU.logical_shift_right))
    link(v.tensor_scalar(y.bitcast(I32), t.bitcast(I32), -1.0, 1597463007.0, ALU.mult, ALU.add))
    for _ in range(3):
        link(v.tensor_tensor(t, y, y, ALU.mult))
        link(v.scalar_tensor_tensor(t, t, -0.5, x, ALU.mult, ALU.mult))
        link(v.scalar_tensor_tensor(y, t, 1.5, y, ALU.add, ALU.mult))


def chain(eng, sem):
    count = [0]

    def link(instruction):
        count[0] += 1
        instruction.then_inc(sem, 1)
        eng.wait_ge(sem, count[0])
    return link


def stage_a(nc, qT, ident, a):
    with ExitStack() as ctx:
        def sb(name, shape):
            return ctx.enter_context(nc.sbuf_tensor(name, shape, F32))

        def sem(name):
            return ctx.enter_context(nc.semaphore(name))

        x = sb("x_a", [P, TILES, H])
        wq = sb("wq", [P, HC, H])
        bq = sb("bq", [P, H])
        qnw = sb("qnw", [P, 1])
        qnb = sb("qnb", [P, 1])
        xn = sb("xn", [P, 2, H])
        xnT = sb("xnT", [P, 2, HC, P])
        q = sb("q", [P, TILES, H])
        sq = sb("sq_a", [P, TILES, H])
        stats = sb("stats_a", [P, TILES, 6])
        mv = sb("mv_a", [P, TILES, 2])
        r1 = sb("r1_a", [P, TILES])
        v1 = sb("v1_a", [P, TILES])
        t1 = sb("t1_a", [P, TILES])
        qm = sb("qm", [P, TILES * XH])
        qv = sb("qv", [P, TILES * XH])
        qr = sb("qr", [P, TILES * XH])
        qt = sb("qt", [P, TILES * XH])
        ps_t = [ctx.enter_context(nc.psum_tensor(f"a_t{i}", [P, H], F32)) for i in range(2)]
        ps_q = [ctx.enter_context(nc.psum_tensor(f"a_q{i}", [P, H], F32)) for i in range(2)]
        s_x, s_w, s_ch = sem("a_x"), sem("a_w"), sem("a_chain")
        xn_ready, xT_ready, xT_copied, q_ready = sem("xn_ready"), sem("xT_ready"), sem("xT_copied"), sem("q_ready")
        q_copied, qn_ready, qT_ready, qT_copied = sem("q_copied"), sem("qn_ready"), sem("qT_ready"), sem("qT_copied")
        block = ctx.enter_context(nc.Block())

        @block.sync
        def _(sp):
            sp.dma_start(x[:, :, :], a["x"]).then_inc(s_x, 16)
            sp.dma_start(ident[:, :], a["ident"]).then_inc(s_w, 16)
            sp.dma_start(wq[:, :, :], a["wq"]).then_inc(s_w, 16)
            sp.dma_start(bq[:, :], a["bq"]).then_inc(s_w, 16)
            sp.dma_start(qnw[:, :], a["qnw"]).then_inc(s_w, 16)
            sp.dma_start(qnb[:, :], a["qnb"]).then_inc(s_w, 16)

        @block.vector
        def _(dve):
            v = nc.vector
            link = chain(dve, s_ch)
            dve.wait_ge(s_x, 16)
            for t in range(TILES):
                link(v.bn_stats(stats[:, t, :], x[:, t, :]))
            for t in range(TILES):
                link(v.bn_aggr(mv[:, t, :], stats[:, t, :]))
            link(v.tensor_scalar(v1[:, :], mv[:, :, 1], LN_EPS, None, ALU.add))
            rsqrt(link, v, v1[:, :], r1[:, :], t1[:, :])
            dve.wait_ge(s_w, 80)

            def q_bias(t):
                dve.wait_ge(q_ready, t + 1)
                v.tensor_tensor(q[:, t, :], ps_q[t % 2][:, :], bq[:, :], ALU.add).then_inc(q_copied, 1)

            for t in range(TILES):
                if t >= 2:
                    dve.wait_ge(xT_ready, t - 1)
                v.tensor_scalar(xn[:, t % 2, :], x[:, t, :], mv[:, t, 0:1], r1[:, t:t + 1],
                                ALU.subtract, ALU.mult).then_inc(xn_ready, 1)
                if t:
                    q_bias(t - 1)
            q_bias(TILES - 1)
            dve.wait_ge(q_copied, TILES)
            heads = q[:, :, :].rearrange("p t (h d) -> p (t h) d", d=XD)
            sqh = sq[:, :, :].rearrange("p t (h d) -> p (t h) d", d=XD)
            link(v.tensor_reduce(qm[:, :], heads, AX.X, ALU.add))
            link(v.tensor_scalar(qm[:, :], qm[:, :], -1.0 / XD, None, ALU.mult))
            mean = qm[:, :].rearrange("p (n o) -> p n o", o=1).broadcast_to([P, TILES * XH, XD])
            link(v.tensor_tensor(heads, heads, mean, ALU.add))
            link(v.tensor_tensor(sqh, heads, heads, ALU.mult))
            link(v.tensor_reduce(qv[:, :], sqh, AX.X, ALU.add))
            link(v.tensor_scalar(qv[:, :], qv[:, :], 1.0 / XD, QK_EPS, ALU.mult, ALU.add))
            rsqrt(link, v, qv[:, :], qr[:, :], qt[:, :])
            for t in range(TILES):
                ht = q[:, t, :].rearrange("p (h d) -> p h d", d=XD)
                rt = qr[:, t * XH:(t + 1) * XH].rearrange("p (n o) -> p n o", o=1).broadcast_to([P, XH, XD])
                v.tensor_tensor(ht, ht, rt, ALU.mult).then_inc(qn_ready, 1)

        @block.scalar
        def _(act):
            for t in range(TILES):
                act.wait_ge(xT_ready, t + 1)
                if t >= 2:
                    act.wait_ge(q_ready, t - 1)
                nc.scalar.activation(xnT[:, t % 2, :, :].rearrange("p c n -> p (c n)"), ps_t[t % 2][:, :],
                                     ACT.Copy).then_inc(xT_copied, 1)
            act.wait_ge(s_w, 80)
            for t in range(TILES):
                act.wait_ge(qT_ready, t + 1)
                nc.scalar.activation(qT[:, :, t * P:(t + 1) * P],
                                     ps_t[t % 2][:, :].rearrange("p (g n) -> p g n", n=P), ACT.Identity,
                                     bias=qnb[:, 0:1], scale=qnw[:, 0:1]).then_inc(qT_copied, 1)

        @block.tensor
        def _(pe):
            pe.wait_ge(s_w, 80)

            def project(t):
                pe.wait_ge(xT_copied, t + 1)
                if t >= 2:
                    pe.wait_ge(q_copied, t - 1)
                for c in range(HC):
                    last = nc.tensor.matmul(ps_q[t % 2][:, :], xnT[:, t % 2, c, :], wq[:, c, :],
                                            start=c == 0, stop=c == HC - 1)
                last.then_inc(q_ready, 1)

            for t in range(TILES):
                pe.wait_ge(xn_ready, t + 1)
                if t >= 2:
                    pe.wait_ge(xT_copied, t - 1)
                for c in range(HC):
                    last = nc.tensor.transpose(ps_t[t % 2][:, c * P:(c + 1) * P], xn[:, t % 2, c * P:(c + 1) * P],
                                               ident[:, :])
                last.then_inc(xT_ready, 1)
                if t:
                    project(t - 1)
            project(TILES - 1)
            for t in range(TILES):
                pe.wait_ge(qn_ready, t + 1)
                pe.wait_ge(xT_copied, TILES)
                if t >= 2:
                    pe.wait_ge(qT_copied, t - 1)
                for g in range(HC):
                    last = nc.tensor.transpose(ps_t[t % 2][:, g * P:(g + 1) * P], q[:, t, g * P:(g + 1) * P],
                                               ident[:, :])
                last.then_inc(qT_ready, 1)


def bank_uses(more):
    order = [("V", m) for m in range(KTS)]
    if more:
        order += [("K", m) for m in range(KTS)]
    order += [("P", s) for s in range(AHEAD)]
    for s in range(STEPS):
        if more and s in KEY_STEPS:
            order.append(("T", KEY_STEPS.index(s)))
        if s + AHEAD < STEPS:
            order.append(("P", s + AHEAD))
    return order


KEY_STEPS = tuple(range(KTS - 1, STEPS - 1))
PROLOGUE = [("K", m) for m in range(KTS)] + [("T", j) for j in range(KTS)]


def stage_b(nc, up, ident, a):
    with ExitStack() as ctx:
        def sb(name, shape, dt=F32):
            return ctx.enter_context(nc.sbuf_tensor(name, shape, dt))

        def sem(name):
            return ctx.enter_context(nc.semaphore(name))

        HW = 8 * XD
        yh, yl = sb("yh", [P, KDC, KCOLS], F32R), sb("yl", [P, KDC, KCOLS], F32R)
        yraw = sb("yraw", [P, 2, KDC, 4 * P])
        yd = sb("yd", [P, KDC, LAST])
        wh, wl = sb("wh", [P, KDC, 2, 2 * HW], F32R), sb("wl", [P, KDC, 2, 2 * HW], F32R)
        wd = sb("w_dca", [P, KDC, 2, 2 * HW])
        bkm = sb("bk_main", [P, 2, HW])
        bkd = sb("bk_dca", [P, 2, HW])
        cols = sb("cols", [P, 12])
        mean_w = sb("mean_w", [P, 4, 8])
        Kc = sb("Kc", [P, KTILES, HW])
        Sq = sb("Sq", [P, KTILES, HW])
        Kf = sb("Kf", [P, 2, 2, 2 * P])
        kTh, kTl = sb("kTh", [P, 2, KCOLS], F32R), sb("kTl", [P, 2, KCOLS], F32R)
        Vh, Vl = sb("Vh", [P, KTILES, HW], F32R), sb("Vl", [P, KTILES, HW], F32R)
        qb = sb("qb", [P, 2, 2, P])
        qbh, qbl = sb("qbh", [P, 2, 2, P], F32R), sb("qbl", [P, 2, 2, P], F32R)
        Pr = sb("Pr", [P, PAIRS, KCOLS])
        PTh, PTl = sb("PTh", [P, AHEAD, 4 * P], F32R), sb("PTl", [P, AHEAD, 4 * P], F32R)
        nb = sb("nb", [P, PAIRS, 3])
        nbs = sb("nbs", [P, PAIRS, 2])
        sums = sb("sums", [P, PAIRS, 3])
        linv = sb("linv", [P, PAIRS, 2])
        NV = KTILES * 8
        var, rst, ntmp = sb("var", [P, NV]), sb("rst", [P, NV]), sb("ntmp", [P, NV])
        ps_s = ctx.enter_context(nc.psum_tensor("ps_s", [P, 4, 512], F32))
        ps_w = [ctx.enter_context(nc.psum_tensor(f"ps_w{i}", [P, 512], F32)) for i in range(3)]
        ps_v = ctx.enter_context(nc.psum_tensor("ps_v", [P, 512], F32))
        s_w = sem("b_w")
        s_y = [sem(f"b_y{c}") for c in range(4)]
        s_q = sem("b_q")
        dve_chain = sem("dve_chain")
        w_ready, pads_zero, yh_ready, y_split = sem("w_ready"), sem("pads_zero"), sem("yh_ready"), sem("y_split")
        filled, read = [sem(f"filled{i}") for i in range(3)], [sem(f"read{i}") for i in range(3)]
        s_done, bias_ready, exp_done, linv_ready, p_scaled = (
            sem("s_done"), sem("bias_ready"), sem("exp_done"), sem("linv_ready"), sem("p_scaled"))
        vh_ready, kf_ready, kh_ready, kl_ready = sem("vh_ready"), sem("kf_ready"), sem("kh_ready"), sem("kl_ready")
        sq_done, sums_done, var_ready, kn_ready = sem("sq_done"), sem("sums_done"), sem("var_ready"), sem("kn_ready")
        ph_ready, pv_done, ctx_copied, qb_ready = sem("ph_ready"), sem("pv_done"), sem("ctx_copied"), sem("qb_ready")
        Y0 = tuple(range(0, KTILES, 4))
        block = ctx.enter_context(nc.Block())

        def units(body, fori):
            with fori(0, B - 1) as i:
                body(i * 2, 0, True)
                body(i * 2, 1, True)
            body(2 * (B - 1), 0, True)
            body(2 * (B - 1), 1, False)

        FULL, ENDING = bank_uses(True), bank_uses(False)
        IN_SLOT = [len(range(i, len(FULL), 3)) for i in range(3)]
        IN_PROLOGUE = [len(range(i, len(PROLOGUE), 3)) for i in range(3)]

        def use(U, kind, j, more=True):
            if U is None:
                n = PROLOGUE.index((kind, j))
                return n % 3, n // 3
            n = (FULL if more else ENDING).index((kind, j))
            bank = n % 3
            return bank, U * IN_SLOT[bank] + (IN_PROLOGUE[bank] + n // 3)

        def tiles_of(m):
            return range(2 * m, min(2 * m + 2, KTILES))

        def rows_of(t):
            return P if t < KT_FULL else LAST

        @block.sync
        def _(sp):
            wraw = Pr[:, 0:2, :].rearrange("p a n -> p (a n)")[:, 0:4 * 2 * HW]
            sp.dma_start(wraw, a["wm"].rearrange("p c f n -> p (c f n)")).then_inc(s_w, 16)
            for dst, name in ((wd, "wd"), (bkm, "bkm"), (bkd, "bkd"), (cols, "cols")):
                sp.dma_start(dst[tuple([slice(None)] * len(dst.shape))], a[name]).then_inc(s_w, 16)

            def load(c, yb):
                if c < 3:
                    sp.dma_start(yraw[:, c % 2, :, :], yb[:, :, c * 4 * P:(c + 1) * 4 * P]).then_inc(s_y[c], 16)
                else:
                    sp.dma_start(yd[:, :, :], yb[:, :, KT_FULL * P:KCOLS]).then_inc(s_y[c], 16)

            def queries(par, at):
                for i in range(4):
                    r, c = slice(32 * i, 32 * i + 32), slice(64 * (i % 2), 64 * (i % 2) + 64)
                    sp.dma_start(qb[r, :, i // 2, c], up[r, 2 * par:2 * par + 2, bass.ds(at, S)]).then_inc(s_q, 16)

            y0 = a["yT"][0:1, :, :, :].rearrange("b p c n -> p (b c) n")
            load(0, y0)
            load(1, y0)
            load(3, y0)
            sp.wait_ge(pads_zero, 1)
            queries(0, 0)
            sp.wait_ge(y_split, 1)
            load(2, y0)

            def slot(u0, par, more):
                U = u0 + par
                if not more:
                    return
                sp.wait_ge(qb_ready, U + 1)
                queries(1 - par, u0 * 32 + (S if par else 0))
                if isinstance(u0, int):
                    return
                b = u0 // 2 + 1
                yb = a["yT"][bass.ds(b, 1), :, :, :].rearrange("b p c n -> p (b c) n")
                if par == 0:
                    sp.wait_ge(y_split, u0 * 2 + 3)
                    load(0, yb)
                    load(1, yb)
                else:
                    sp.wait_ge(y_split, u0 * 2 + 5)
                    load(2, yb)
                    bank, n = use(U, "V", KTS - 1)
                    sp.wait_ge(filled[bank], n + 1)
                    load(3, yb)

            units(slot, sp.Fori)

        @block.tensor
        def _(pe):
            def three(out, lhs, rhs, start, stop):
                (lh, ll), (rh, rl) = lhs, rhs
                nc.tensor.matmul(out, lh, rh, start=start, stop=False)
                nc.tensor.matmul(out, ll, rh, start=False, stop=False)
                return nc.tensor.matmul(out, lh, rl, start=False, stop=stop)

            def free(b, n):
                if not (isinstance(n, int) and n == 0):
                    pe.wait_ge(read[b], n)

            def project(b, n, par, kv, m):
                free(b, n)
                bank = ps_w[b]
                for t in tiles_of(m):
                    r, at = rows_of(t), slice(t * P, t * P + rows_of(t))
                    o = bank[0:r, (t % 2) * HW:(t % 2 + 1) * HW]
                    ch = slice(kv * HW, (kv + 1) * HW)
                    for c in range(KDC):
                        last = three(o, (yh[:, c, at], yl[:, c, at]), (wh[:, c, par, ch], wl[:, c, par, ch]),
                                     c == 0, c == KDC - 1)
                    if t == KTILES - 1:
                        for c in range(KDC):
                            last = nc.tensor.matmul(bank[0:r, HW:2 * HW], yd[:, c, :], wd[:, c, par, ch],
                                                    start=c == 0, stop=c == KDC - 1)
                last.then_inc(filled[b], 1)

            def make_keys(b, n, par, m, batch4):
                if batch4 is not None and 2 * m in Y0:
                    pe.wait_ge(y_split, batch4 + (Y0.index(2 * m) + 1))
                project(b, n, par, 0, m)

            def key_transposes(b, n, W, j):
                pe.wait_ge(kn_ready, W * KTS + (j + 1))
                free(b, n)
                for t in tiles_of(j):
                    r = rows_of(t)
                    for g in range(2):
                        at = g * 256 + (t % 2) * P
                        last = nc.tensor.transpose(ps_w[b][:, at:at + r], Kc[0:r, t, g * P:(g + 1) * P],
                                                   ident[0:r, 0:r])
                last.then_inc(filled[b], 1)

            pe.wait_ge(w_ready, 1)
            for m in range(KTS):
                make_keys(*use(None, "K", m), 0, m, 0)
            for j in range(KTS):
                key_transposes(*use(None, "T", j), 0, j)

            def slot(u0, par, more):
                U = u0 + par
                batch4 = (u0 * 2 + 4) if par else None

                def values(m):
                    project(*use(U, "V", m, more), par, 1, m)

                def keys(m):
                    if more:
                        make_keys(*use(U, "K", m), 1 - par, m, batch4)

                def scores(p):
                    g, i = p // 2, p % 2
                    pe.wait_ge(exp_done, U * PAIRS + (p + 1))
                    if p == 0:
                        pe.wait_ge(kl_ready, (U + 1) * KTS)
                        pe.wait_ge(qb_ready, U + 1)
                    for c in range(4):
                        at = slice(c * SCH, (c + 1) * SCH)
                        last = three(ps_s[:, c, 0:SCH], (qbh[:, g, i, :], qbl[:, g, i, :]),
                                     (kTh[:, g, at], kTl[:, g, at]), True, True)
                    last.then_inc(s_done, 1)

                def turn(s):
                    g, j = s // KTS, s % KTS
                    b, n = use(U, "P", s, more)
                    if j == 0:
                        pe.wait_ge(p_scaled, U * PAIRS + (2 * g + 2))
                    free(b, n)
                    for t in tiles_of(j):
                        r = rows_of(t)
                        for i in range(2):
                            at = (t % 2) * 256 + i * P
                            last = nc.tensor.transpose(ps_w[b][0:r, at:at + P],
                                                       Pr[:, 2 * g + i, t * P:t * P + r], ident[:, :])
                    last.then_inc(filled[b], 1)

                def weigh(s):
                    g, j = s // KTS, s % KTS
                    b, n = use(U, "P", s, more)
                    if j == 0 and (g == 1 or par == 1):
                        pe.wait_ge(ctx_copied, U * 2 + g)
                    pe.wait_ge(read[b], n + 1)
                    for t in tiles_of(j):
                        r, ch, at = rows_of(t), slice(g * P, (g + 1) * P), slice((t % 2) * 256, (t % 2) * 256 + 256)
                        last = three(ps_v[:, 0:256], (Vh[0:r, t, ch], Vl[0:r, t, ch]),
                                     (PTh[0:r, s % AHEAD, at], PTl[0:r, s % AHEAD, at]), t == 0, t == KTILES - 1)
                    if j == KTS - 1:
                        last.then_inc(pv_done, 1)

                for m in range(0, 3):
                    values(m)
                scores(0)
                for m in range(3, KTS):
                    values(m)
                scores(1)
                for m in range(0, 4):
                    keys(m)
                scores(2)
                for m in range(4, KTS):
                    keys(m)
                scores(3)
                for s in range(AHEAD):
                    turn(s)
                for s in range(STEPS):
                    weigh(s)
                    if more and s in KEY_STEPS:
                        j = KEY_STEPS.index(s)
                        key_transposes(*use(U, "T", j), U + 1, j)
                    if s + AHEAD < STEPS:
                        turn(s + AHEAD)

            units(slot, pe.Fori)

        @block.vector
        def _(dve):
            v = nc.vector
            made = [0]
            base = [0]

            def link(instruction):
                instruction.then_inc(dve_chain, 1)
                made[0] += 1
                dve.wait_ge(dve_chain, base[0] + made[0])

            v.memset(Kc[:, KTILES - 1, :], 0.0)
            v.memset(qb[:, :, :, :], 0.0).then_inc(pads_zero, 1)
            dve.wait_ge(s_w, 80)
            wm = Pr[:, 0:2, :].rearrange("p a n -> p (a n)")[:, 0:4 * 2 * HW].rearrange(
                "p (c f n) -> p c f n", c=KDC, f=2)
            for wt, bt in ((wm, bkm), (wd, bkd)):
                for c in range(KDC):
                    kw = wt[:, c, :, 0:HW].rearrange("p f (h d) -> p f h d", d=XD)
                    m = mean_w[:, 0:2, :]
                    link(v.tensor_reduce(m, kw, AX.X, ALU.add))
                    link(v.tensor_scalar(m, m, -1.0 / XD, None, ALU.mult))
                    for f in range(2):
                        mf = mean_w[:, f, :].rearrange("p (h o) -> p h o", o=1).broadcast_to([P, 8, XD])
                        link(v.tensor_tensor(kw[:, f, :, :], kw[:, f, :, :], mf, ALU.add))
                bh = bt[:, :, :].rearrange("p f (h d) -> p (f h) d", d=XD)
                m = mean_w[:, 0:2, :].rearrange("p f h -> p (f h)")
                link(v.tensor_reduce(m, bh, AX.X, ALU.add))
                link(v.tensor_scalar(m, m, -1.0 / XD, None, ALU.mult))
                link(v.tensor_tensor(bh, bh, m.rearrange("p (h o) -> p h o", o=1).broadcast_to([P, 16, XD]), ALU.add))
            link(v.tensor_copy(wh[:, :, :, :], wm))
            link(v.tensor_tensor(wl[:, :, :, :], wm, wh[:, :, :, :].bitcast(F32), ALU.subtract))
            link(v.memset(Pr[:, :, MAIN:DCA_AT], 0.0))
            v.memset(nb[:, :, :], 0.0).then_inc(w_ready, 1)

            def key_bias(b, n, par, m):
                dve.wait_ge(filled[b], n + 1)
                if m < KTS - 1:
                    both = bkm[:, par:par + 1, :].broadcast_to([P, 2, HW])
                    v.tensor_tensor(Kc[:, 2 * m:2 * m + 2, :], ps_w[b][:, :].rearrange("p (t n) -> p t n", n=HW),
                                    both, ALU.add).then_inc(read[b], 1)
                else:
                    v.tensor_tensor(Kc[0:64, KT_FULL, :], ps_w[b][0:64, 0:HW], bkm[0:64, par, :], ALU.add)
                    v.tensor_tensor(Kc[64:LAST, KT_FULL, :], ps_w[b][64:LAST, HW:2 * HW], bkd[64:LAST, par, :],
                                    ALU.add).then_inc(read[b], 1)

            def square_sums(W, c):
                t0, t1 = CHUNKS[c]
                dve.wait_ge(sq_done, W * 2 + (c + 1))
                link(v.tensor_reduce(var[:, t0 * 8:t1 * 8],
                                     Sq[:, t0:t1, :].rearrange("p t (h d) -> p (t h) d", d=XD), AX.X, ALU.add))

            def root_start():
                link(v.tensor_scalar(var[:, :], var[:, :], 1.0 / XD, QK_EPS, ALU.mult, ALU.add))
                link(v.tensor_scalar(ntmp[:, :].bitcast(I32), var[:, :].bitcast(I32), 1, None,
                                     ALU.logical_shift_right))
                link(v.tensor_scalar(rst[:, :].bitcast(I32), ntmp[:, :].bitcast(I32), -1.0, 1597463007.0,
                                     ALU.mult, ALU.add))

            def root_step(last):
                link(v.tensor_tensor(ntmp[:, :], rst[:, :], rst[:, :], ALU.mult))
                link(v.scalar_tensor_tensor(ntmp[:, :], ntmp[:, :], -0.5, var[:, :], ALU.mult, ALU.mult))
                step = v.scalar_tensor_tensor(rst[:, :], ntmp[:, :], 1.5, rst[:, :], ALU.add, ALU.mult)
                if last:
                    step.then_inc(var_ready, 1)
                else:
                    link(step)

            def keys_high(W, j):
                dve.wait_ge(kf_ready, W * KTS + (j + 1))
                n = 2 * P if j < KTS - 1 else LAST
                v.tensor_copy(kTh[:, :, j * 256:j * 256 + n], Kf[:, j % 2, :, 0:n]).then_inc(kh_ready, 1)

            def queries(W):
                dve.wait_ge(s_q, W * 64 + 64)
                link(v.tensor_copy(qbh[:, :, :, :], qb[:, :, :, :]))
                v.tensor_tensor(qbl[:, :, :, :], qb[:, :, :, :], qbh[:, :, :, :].bitcast(F32),
                                ALU.subtract).then_inc(qb_ready, 1)

            for m in range(KTS):
                key_bias(*use(None, "K", m), 0, m)
            square_sums(0, 0)
            square_sums(0, 1)
            root_start()
            for i in range(3):
                root_step(i == 2)
            queries(0)
            for j in range(KTS):
                keys_high(0, j)
            before = made[0]

            def slot(u0, par, more):
                U = u0 + par
                if par == 0:
                    made[0] = 0
                    base[0] = u0 * LINKS + before

                def values_low(m):
                    b, n = use(U, "V", m, more)
                    dve.wait_ge(vh_ready, U * KTS + (m + 1))
                    if m < KTS - 1:
                        v.tensor_tensor(Vl[:, 2 * m:2 * m + 2, :], ps_w[b][:, :].rearrange("p (t n) -> p t n", n=HW),
                                        Vh[:, 2 * m:2 * m + 2, :].bitcast(F32), ALU.subtract).then_inc(read[b], 1)
                    else:
                        for r, c0 in ((slice(0, 64), 0), (slice(64, LAST), HW)):
                            last = v.tensor_tensor(Vl[r, KT_FULL, :], ps_w[b][r, c0:c0 + HW],
                                                   Vh[r, KT_FULL, :].bitcast(F32), ALU.subtract)
                        last.then_inc(read[b], 1)

                def maxima(p):
                    dve.wait_ge(s_done, U * PAIRS + (p + 1))
                    v.tensor_reduce(nb[:, p, 0:1], ps_s[:, 0:3, 0:SCH], AX.XY, ALU.max, negate=True)
                    v.tensor_reduce(nb[:, p, 1:2], ps_s[:, 3, 0:MAIN3], AX.X, ALU.max, negate=True)
                    link(v.tensor_reduce(nb[:, p, 2:3], ps_s[:, 3, DCA_AT - 3 * SCH:SCH], AX.X, ALU.max,
                                         negate=True))
                    v.tensor_scalar(nbs[:, p, 0:1], nb[:, p, 0:1], nb[:, p, 1:2], XSCALE, ALU.min, ALU.mult)
                    v.tensor_scalar(nbs[:, p, 1:2], nb[:, p, 2:3], XSCALE, None,
                                    ALU.mult).then_inc(bias_ready, 1)

                def inverse(p):
                    dve.wait_ge(exp_done, U * PAIRS + (p + 2))
                    link(v.tensor_tensor(sums[:, p, 0:1], sums[:, p, 0:1], sums[:, p, 2:3], ALU.add))
                    v.reciprocal(linv[:, p, :], sums[:, p, 0:2]).then_inc(linv_ready, 1)

                def keys(m):
                    if more:
                        key_bias(*use(U, "K", m), 1 - par, m)

                def low(s):
                    b, _ = use(U, "P", s, more)
                    dve.wait_ge(ph_ready, U * STEPS + (s + 1))
                    n, c1 = (P, 512) if s % KTS < KTS - 1 else (LAST, 256)
                    v.tensor_tensor(PTl[0:n, s % AHEAD, 0:c1], ps_w[b][0:n, 0:c1],
                                    PTh[0:n, s % AHEAD, 0:c1].bitcast(F32), ALU.subtract).then_inc(read[b], 1)

                def context(g):
                    dve.wait_ge(pv_done, U * 2 + (g + 1))
                    gg = 2 * par + g
                    for i in range(4):
                        r = slice(32 * i, 32 * i + 32)
                        last = v.tensor_scalar(up[r, gg, bass.ds(u0 * 32, S)], ps_v[r, 64 * i:64 * i + 64],
                                               cols[r, 4 + gg:5 + gg], cols[r, 8 + gg:9 + gg], ALU.add, ALU.add)
                    last.then_inc(ctx_copied, 1)

                for m in range(0, 3):
                    values_low(m)
                maxima(0)
                for m in range(3, 6):
                    values_low(m)
                inverse(0)
                values_low(6)
                maxima(1)
                for m in range(0, 3):
                    keys(m)
                inverse(1)
                keys(3)
                maxima(2)
                for m in range(4, KTS):
                    keys(m)
                if more:
                    square_sums(U + 1, 0)
                maxima(3)
                inverse(2)
                if more:
                    square_sums(U + 1, 1)
                low(0)
                if more:
                    root_start()
                low(1)
                if more:
                    root_step(False)
                low(2)
                if more:
                    root_step(False)
                low(3)
                if more:
                    root_step(True)
                inverse(3)
                low(4)
                low(5)
                if more:
                    queries(U + 1)
                for s in range(6, 9):
                    low(s)
                context(0)
                for s in range(9, STEPS):
                    low(s)
                    if more:
                        keys_high(U + 1, s - 9)
                if more:
                    for j in range(STEPS - 9, KTS):
                        keys_high(U + 1, j)
                context(1)
                if more:
                    assert made[0] == (par + 1) * LINKS, made

            LINKS = 2 * PAIRS + 2 + 3 + 8 + 1
            units(slot, dve.Fori)

        @block.scalar
        def _(act):
            s_ = nc.scalar

            def y_high(c, batch):
                act.wait_ge(s_y[c], batch * 16 + 16)
                src = yraw[:, c % 2, :, :] if c < 3 else yd[:, :, :]
                s_.activation(yh[:, :, Y0[c] * P:min((Y0[c] + 4) * P, KCOLS)], src, ACT.Copy).then_inc(yh_ready, 1)

            def squares(W, c, b, n):
                t0, t1 = CHUNKS[c]
                act.wait_ge(read[b], n + 1)
                s_.activation(Sq[:, t0:t1, :], Kc[:, t0:t1, :], ACT.Square).then_inc(sq_done, 1)

            def keys_out(b, n, W, j):
                act.wait_ge(filled[b], n + 1)
                if not (isinstance(W, int) and W == 0 and j < 2):
                    act.wait_ge(kl_ready, W * KTS + (j - 1))
                src = ps_w[b][:, :].rearrange("p (g n) -> p g n", g=2)
                if j < KTS - 1:
                    s_.activation(Kf[:, j % 2, :, :], src, ACT.Identity, scale=cols[:, 0:1],
                                  bias=cols[:, 1:2]).then_inc(kf_ready, 1)
                else:
                    s_.activation(Kf[:, j % 2, :, 0:64], src[:, :, 0:64], ACT.Identity, scale=cols[:, 0:1],
                                  bias=cols[:, 1:2])
                    s_.activation(Kf[:, j % 2, :, 64:LAST], src[:, :, 64:LAST], ACT.Identity, scale=cols[:, 2:3],
                                  bias=cols[:, 3:4]).then_inc(kf_ready, 1)
                act.wait_ge(kf_ready, W * KTS + (j + 1))
                act.sem_inc(read[b], 1)

            for c in range(4):
                y_high(c, 0)
            act.wait_ge(w_ready, 1)
            squares(0, 0, *use(None, "K", 3))
            squares(0, 1, *use(None, "K", KTS - 1))
            for j in range(KTS):
                keys_out(*use(None, "T", j), 0, j)
            s_.activation(sums[:, 0, :], nb[:, 0, :], ACT.Copy).then_inc(exp_done, 1)

            def slot(u0, par, more):
                U = u0 + par

                def values(m):
                    b, n = use(U, "V", m, more)
                    act.wait_ge(filled[b], n + 1)
                    if m < KTS - 1:
                        s_.activation(Vh[:, 2 * m:2 * m + 2, :], ps_w[b][:, :].rearrange("p (t n) -> p t n", n=HW),
                                      ACT.Copy).then_inc(vh_ready, 1)
                    else:
                        s_.activation(Vh[0:64, KT_FULL, :], ps_w[b][0:64, 0:HW], ACT.Copy)
                        s_.activation(Vh[64:LAST, KT_FULL, :], ps_w[b][64:LAST, HW:2 * HW],
                                      ACT.Copy).then_inc(vh_ready, 1)

                def next_y(c):
                    if par == 1 and more:
                        y_high(c, u0 // 2 + 1)

                def exps(p):
                    act.wait_ge(bias_ready, U * PAIRS + (p + 1))
                    s_.activation(Pr[:, p, 0:3 * SCH].rearrange("p (c n) -> p c n", n=SCH), ps_s[:, 0:3, 0:SCH],
                                  ACT.Exp, bias=nbs[:, p, 0:1], scale=XSCALE, accum_out=sums[:, p, 0:1])
                    s_.activation(Pr[:, p, 3 * SCH:MAIN], ps_s[:, 3, 0:MAIN3], ACT.Exp, bias=nbs[:, p, 0:1],
                                  scale=XSCALE, accum_out=sums[:, p, 2:3])
                    s_.activation(Pr[:, p, DCA_AT:KCOLS], ps_s[:, 3, DCA_AT - 3 * SCH:SCH], ACT.Exp,
                                  bias=nbs[:, p, 1:2], scale=XSCALE, accum_out=sums[:, p, 1:2]).then_inc(exp_done, 1)

                def high(s):
                    b, n = use(U, "P", s, more)
                    act.wait_ge(filled[b], n + 1)
                    r, c1 = (P, 512) if s % KTS < KTS - 1 else (LAST, 256)
                    s_.activation(PTh[0:r, s % AHEAD, 0:c1], ps_w[b][0:r, 0:c1], ACT.Copy).then_inc(ph_ready, 1)

                values(0)
                values(1)
                next_y(0)
                values(2)
                values(3)
                exps(0)
                next_y(1)
                for m in range(4, KTS):
                    values(m)
                next_y(2)
                exps(1)
                next_y(3)
                if more:
                    squares(U + 1, 0, *use(U, "K", 3))
                exps(2)
                if more:
                    squares(U + 1, 1, *use(U, "K", KTS - 1))
                exps(3)
                for s in range(9):
                    high(s)
                if more:
                    keys_out(*use(U, "T", 0), U + 1, 0)
                for s in range(9, STEPS):
                    high(s)
                    if more:
                        keys_out(*use(U, "T", s - 8), U + 1, s - 8)
                if more:
                    for j in range(STEPS - 8, KTS):
                        keys_out(*use(U, "T", j), U + 1, j)

            units(slot, act.Fori)

        @block.gpsimd
        def _(pool):
            g_ = nc.gpsimd

            def y_low(c, batch4):
                pool.wait_ge(yh_ready, batch4 + (c + 1))
                src = yraw[:, c % 2, :, :] if c < 3 else yd[:, :, :]
                at = slice(Y0[c] * P, min((Y0[c] + 4) * P, KCOLS))
                g_.tensor_tensor(yl[:, :, at], src, yh[:, :, at].bitcast(F32), ALU.subtract).then_inc(y_split, 1)

            def normalise(W, j):
                if j == 0:
                    pool.wait_ge(var_ready, W + 1)
                n = len(tiles_of(j))
                kh = Kc[:, 2 * j:2 * j + n, :].rearrange("p t (h d) -> p (t h) d", d=XD)
                rr = rst[:, 16 * j:(2 * j + n) * 8].rearrange("p (h o) -> p h o", o=1)
                g_.tensor_tensor(kh, kh, rr.broadcast_to([P, n * 8, XD]), ALU.mult).then_inc(kn_ready, 1)

            def keys_low(W, j):
                pool.wait_ge(kh_ready, W * KTS + (j + 1))
                n = 2 * P if j < KTS - 1 else LAST
                at = slice(j * 256, j * 256 + n)
                g_.tensor_tensor(kTl[:, :, at], Kf[:, j % 2, :, 0:n], kTh[:, :, at].bitcast(F32),
                                 ALU.subtract).then_inc(kl_ready, 1)

            def norm_and_low(W):
                for j in range(4):
                    normalise(W, j)
                for j in range(KTS):
                    keys_low(W, j)
                    if j + 4 < KTS:
                        normalise(W, j + 4)

            for c in range(4):
                y_low(c, 0)
            norm_and_low(0)

            def slot(u0, par, more):
                U = u0 + par

                def next_y(c):
                    if par == 1 and more:
                        y_low(c, u0 * 2 + 4)

                def scale(p):
                    pool.wait_ge(linv_ready, U * PAIRS + (p + 1))
                    g_.tensor_tensor(Pr[:, p, DCA_AT:KCOLS], Pr[:, p, DCA_AT:KCOLS],
                                     linv[:, p, 1:2].broadcast_to([P, DCA]), ALU.mult)
                    g_.tensor_scalar(Pr[:, p, 0:MAIN], Pr[:, p, 0:MAIN], linv[:, p, 0:1], 1.0,
                                     ALU.mult, ALU.mult).then_inc(p_scaled, 1)

                next_y(0)
                next_y(1)
                scale(0)
                next_y(2)
                next_y(3)
                scale(1)
                scale(2)
                scale(3)
                if more:
                    norm_and_low(U + 1)

            units(slot, pool.Fori)


def stage_c_norms(nc, x, ctxT, hT, ident, a):
    with ExitStack() as ctx:
        def sb(name, shape):
            return ctx.enter_context(nc.sbuf_tensor(name, shape, F32))

        def sem(name):
            return ctx.enter_context(nc.semaphore(name))

        wo = sb("wo", [P, HC, H])
        bo = sb("bo", [P, H])
        lnw = sb("lnw", [P, H])
        h = sb("h", [P, TILES, H])
        hs = sb("hs", [P, 2, H])
        stats = sb("stats_c", [P, TILES, 6])
        mv = sb("mv_c", [P, TILES, 2])
        v1, r1, t1 = sb("v1_c", [P, TILES]), sb("r1_c", [P, TILES]), sb("t1_c", [P, TILES])
        ss, r2 = sb("ss_c", [P, TILES]), sb("r2_c", [P, TILES])
        ps_o = [ctx.enter_context(nc.psum_tensor(f"c_o{i}", [P, H], F32)) for i in range(2)]
        ps_t = [ctx.enter_context(nc.psum_tensor(f"c_t{i}", [P, H], F32)) for i in range(2)]
        s_w, s_ch = sem("c_w"), sem("c_chain")
        o_done, o_copied, h_ready, sq_done = sem("o_done"), sem("o_copied"), sem("h_ready"), sem("c_sq")
        hn_ready, hT_done, hT_copied = sem("hn_ready"), sem("hT_done"), sem("hT_copied")
        block = ctx.enter_context(nc.Block())

        @block.sync
        def _(sp):
            sp.dma_start(x[:, :, :], a["x"]).then_inc(s_w, 16)
            sp.dma_start(wo[:, :, :], a["wo"]).then_inc(s_w, 16)
            sp.dma_start(bo[:, :], a["bo"]).then_inc(s_w, 16)
            sp.dma_start(lnw[:, :], a["lnw"]).then_inc(s_w, 16)

        @block.tensor
        def _(pe):
            pe.wait_ge(s_w, 64)
            for t in range(TILES):
                if t >= 2:
                    pe.wait_ge(o_copied, t - 1)
                for g in range(HC):
                    last = nc.tensor.matmul(ps_o[t % 2][:, :], ctxT[:, g, t * P:(t + 1) * P], wo[:, g, :],
                                            start=g == 0, stop=g == HC - 1)
                last.then_inc(o_done, 1)
            for t in range(TILES):
                pe.wait_ge(hn_ready, t + 1)
                if t >= 2:
                    pe.wait_ge(hT_copied, t - 1)
                for c in range(HC):
                    last = nc.tensor.transpose(ps_t[t % 2][:, c * P:(c + 1) * P], h[:, t, c * P:(c + 1) * P],
                                               ident[:, :])
                last.then_inc(hT_done, 1)

        @block.vector
        def _(dve):
            v = nc.vector
            link = chain(dve, s_ch)
            dve.wait_ge(s_w, 64)
            for t in range(TILES):
                dve.wait_ge(o_done, t + 1)
                v.tensor_tensor(hs[:, 0, :], ps_o[t % 2][:, :], bo[:, :], ALU.add).then_inc(o_copied, 1)
                dve.wait_ge(o_copied, t + 1)
                link(v.tensor_tensor(x[:, t, :], x[:, t, :], hs[:, 0, :], ALU.add))
                link(v.bn_stats(stats[:, t, :], x[:, t, :]))
            for t in range(TILES):
                link(v.bn_aggr(mv[:, t, :], stats[:, t, :]))
            link(v.tensor_scalar(v1[:, :], mv[:, :, 1], LN_EPS, None, ALU.add))
            rsqrt(link, v, v1[:, :], r1[:, :], t1[:, :])
            for t in range(TILES):
                v.tensor_scalar(h[:, t, :], x[:, t, :], mv[:, t, 0:1], r1[:, t:t + 1],
                                ALU.subtract, ALU.mult).then_inc(h_ready, 1)
            dve.wait_ge(sq_done, TILES)
            link(v.tensor_scalar(ss[:, :], ss[:, :], 1.0 / H, RMS_EPS, ALU.mult, ALU.add))
            rsqrt(link, v, ss[:, :], r2[:, :], t1[:, :])
            for t in range(TILES):
                v.scalar_tensor_tensor(h[:, t, :], h[:, t, :], r2[:, t:t + 1], lnw[:, :],
                                       ALU.mult, ALU.mult).then_inc(hn_ready, 1)

        @block.scalar
        def _(act):
            for t in range(TILES):
                act.wait_ge(h_ready, t + 1)
                nc.scalar.activation(hs[:, 1, :], h[:, t, :], ACT.Square,
                                     accum_out=ss[:, t:t + 1]).then_inc(sq_done, 1)
                act.wait_ge(sq_done, t + 1)
            for t in range(TILES):
                act.wait_ge(hT_done, t + 1)
                nc.scalar.activation(hT[:, :, t * P:(t + 1) * P], ps_t[t % 2][:, :].rearrange("p (c n) -> p c n", n=P),
                                     ACT.Copy).then_inc(hT_copied, 1)


def stage_c_project(nc, hT, qk, a):
    heads = HQ + HKV
    half = TOK // 2
    with ExitStack() as ctx:
        def sb(name, shape):
            return ctx.enter_context(nc.sbuf_tensor(name, shape, F32))

        def sem(name):
            return ctx.enter_context(nc.semaphore(name))

        wqk = sb("wqk", [P, HC, heads * D])
        bqk = sb("bqk", [P, heads])
        rope = sb("rope", [P, 2, S])
        raw, swapped = sb("raw", [P, 2, half]), sb("swapped", [P, 2, half])
        ra, rb = sb("ra", [P, 2, half]), sb("rb", [P, 2, half])
        ps = [ctx.enter_context(nc.psum_tensor(f"cp{i}", [P, half], F32)) for i in range(2)]
        s_w = [sem(f"cp_w{c}") for c in range(3)]
        s_b = sem("cp_b")
        made, raw_ready, cos_ready, sin_ready, qk_ready = (
            sem("cp_made"), sem("raw_ready"), sem("cos_ready"), sem("sin_ready"), sem("qk_ready"))
        s_swap = [sem(f"swap{i}") for i in range(2)]
        block = ctx.enter_context(nc.Block())
        parts = ((0, 2), (2, 8), (8, heads))
        n_steps = 2 * heads

        @block.sync
        def _(sp):
            sp.dma_start(bqk[:, :], a["bqk"]).then_inc(s_b, 16)
            sp.dma_start(rope[:, :, :], a["rope"]).then_inc(s_b, 16)
            for i, (h0, h1) in enumerate(parts):
                sp.dma_start(wqk[:, :, h0 * D:h1 * D], a["wqk"][:, :, h0 * D:h1 * D]).then_inc(s_w[i], 16)
            for n in range(n_steps):
                sp.wait_ge(raw_ready, n + 1)
                if n >= 2:
                    sp.wait_ge(sin_ready, n - 1)
                sp.dma_start(swapped[0:64, n % 2, :], raw[64:P, n % 2, :]).then_inc(s_swap[n % 2], 16)
                sp.dma_start(swapped[64:P, n % 2, :], raw[0:64, n % 2, :]).then_inc(s_swap[n % 2], 16)

        @block.tensor
        def _(pe):
            for n in range(n_steps):
                hd, f = n // 2, n % 2
                for i, (h0, _) in enumerate(parts):
                    if f == 0 and hd == h0:
                        pe.wait_ge(s_w[i], 16)
                if n >= 2:
                    pe.wait_ge(raw_ready, n - 1)
                for c in range(HC):
                    last = nc.tensor.matmul(ps[n % 2][:, :], wqk[:, c, hd * D:(hd + 1) * D],
                                            hT[:, c, f * half:(f + 1) * half], start=c == 0, stop=c == HC - 1)
                last.then_inc(made, 1)

        @block.scalar
        def _(act):
            act.wait_ge(s_b, 32)
            for n in range(n_steps):
                act.wait_ge(made, n + 1)
                if n >= 2:
                    act.wait_ge(cos_ready, n - 1)
                    act.wait_ge(s_swap[n % 2], 32 * (n // 2))
                nc.scalar.activation(raw[:, n % 2, :], ps[n % 2][:, :], ACT.Identity,
                                     bias=bqk[:, n // 2:n // 2 + 1]).then_inc(raw_ready, 1)

        def table(k):
            return rope[:, k:k + 1, :].broadcast_to([P, half // S, S])

        def by_batch(t):
            return t.rearrange("p (b s) -> p b s", s=S)

        @block.vector
        def _(dve):
            dve.wait_ge(s_b, 32)

            def add(n):
                dve.wait_ge(sin_ready, n + 1)
                nc.vector.tensor_tensor(qk[:, n // 2, (n % 2) * half:(n % 2 + 1) * half], ra[:, n % 2, :],
                                        rb[:, n % 2, :], ALU.add).then_inc(qk_ready, 1)

            for n in range(n_steps):
                dve.wait_ge(raw_ready, n + 1)
                if n >= 2:
                    dve.wait_ge(qk_ready, n - 1)
                nc.vector.tensor_tensor(by_batch(ra[:, n % 2, :]), by_batch(raw[:, n % 2, :]), table(0),
                                        ALU.mult).then_inc(cos_ready, 1)
                if n >= 1:
                    if n == 1:
                        dve.wait_ge(cos_ready, 1)
                    dve.wait_ge(cos_ready, n)
                    add(n - 1)
            dve.wait_ge(cos_ready, n_steps)
            add(n_steps - 1)

        @block.gpsimd
        def _(pool):
            pool.wait_ge(s_b, 32)
            for n in range(n_steps):
                pool.wait_ge(s_swap[n % 2], 32 * (n // 2 + 1))
                if n >= 2:
                    pool.wait_ge(qk_ready, n - 1)
                nc.gpsimd.tensor_tensor(by_batch(rb[:, n % 2, :]), by_batch(swapped[:, n % 2, :]), table(1),
                                        ALU.mult).then_inc(sin_ready, 1)


def stage_c_attend(nc, x, hT, qk, ident, a):
    pairs = HQ // 2
    with ExitStack() as ctx:
        def sb(name, shape):
            return ctx.enter_context(nc.sbuf_tensor(name, shape, F32))

        def sem(name):
            return ctx.enter_context(nc.semaphore(name))

        wv = sb("wv", [P, HC, HKV * D])
        wot = sb("wot", [P, HQ, H])
        bv = sb("bv_c", [P, HKV])
        mask = sb("mask", [P, S])
        qs = sb("qs", [P, 2, HQ, S])
        hb = sb("hb", [P, 2, HC, S])
        Vs = sb("Vs", [S, 2, HKV * D])
        sc = sb("sc", [P, 2, pairs, S])
        pr = sb("pr", [P, 2, pairs, S])
        mx, sm = sb("mx", [P, 2, pairs]), sb("sm", [P, 2, pairs])
        pT = sb("pT", [S, 2, HQ * S])
        aT = sb("aT", [P, HQ, P])
        ps_s = [ctx.enter_context(nc.psum_tensor(f"ca_s{i}", [P, pairs, S], F32)) for i in range(2)]
        ps_v = ctx.enter_context(nc.psum_tensor("ca_v", [P, H], F32))
        ps_t = [ctx.enter_context(nc.psum_tensor(f"ca_t{i}", [P, H], F32)) for i in range(2)]
        ps_c = [ctx.enter_context(nc.psum_tensor(f"ca_c{i}", [P, 2, REP * S], F32)) for i in range(2)]
        ps_o = ctx.enter_context(nc.psum_tensor("ca_o", [P, H], F32))
        s_w, s_wo = sem("ca_w"), sem("ca_wo")
        q_staged, s_made, v_made, v_copied, masked = (
            sem("q_staged"), sem("s_made"), sem("v_made"), sem("v_copied"), sem("masked"))
        shifted, expd, p_ready, t_made = sem("shifted"), sem("expd"), sem("p_ready"), sem("t_made")
        t_act, t_dve, c_made, c_act, c_dve, o_made, o_added, soft = (
            sem("t_act"), sem("t_dve"), sem("c_made"), sem("c_act"), sem("c_dve"), sem("o_made"),
            sem("o_added"), sem("soft"))
        block = ctx.enter_context(nc.Block())

        @block.sync
        def _(sp):
            sp.dma_start(wv[:, :, :], a["wv"]).then_inc(s_w, 16)
            sp.dma_start(bv[:, :], a["bv_c"]).then_inc(s_w, 16)
            sp.dma_start(mask[:, :], a["mask"]).then_inc(s_w, 16)
            sp.dma_start(wot[:, :, :], a["wot"]).then_inc(s_wo, 16)

        @block.tensor
        def _(pe):
            def batch(i, par):
                n = i * 2 + par
                pe.wait_ge(q_staged, n * 2 + 2)
                for j in range(pairs):
                    kv = j // 2
                    last = nc.tensor.matmul(ps_s[par][:, j, :], qs[:, par, 2 * j:2 * j + 2, :],
                                            qk[:, HQ + kv, bass.ds(i * P + par * S, S)], start=True, stop=True)
                last.then_inc(s_made, 1)
                if par:
                    pe.wait_ge(v_copied, n)
                for c in range(HC):
                    last = nc.tensor.matmul(ps_v[0:S, :], hb[:, par, c, :], wv[:, c, :],
                                            start=c == 0, stop=c == HC - 1)
                last.then_inc(v_made, 1)

            def attend(i, par):
                n = i * 2 + par
                pe.wait_ge(p_ready, n + 1)
                nc.tensor.transpose(ps_t[0][:, 0:P], pr[:, par, 0:2, :], ident[:, :])
                for j in range(1, pairs):
                    last = nc.tensor.transpose(ps_t[j // 4][0:S, (j % 4) * P:(j % 4 + 1) * P], pr[:, par, j, :],
                                               ident[:, :])
                last.then_inc(t_made, 1)
                pe.wait_ge(t_act, n + 1)
                pe.wait_ge(t_dve, n + 1)
                for kv in range(HKV):
                    last = nc.tensor.matmul(ps_c[kv // 2][:, kv % 2, :], Vs[:, par, kv * D:(kv + 1) * D],
                                            pT[:, par, kv * REP * S:(kv + 1) * REP * S], start=True, stop=True)
                last.then_inc(c_made, 1)

            pe.wait_ge(s_w, 48)
            pe.wait_ge(s_wo, 16)
            with pe.Fori(0, TILES) as i:
                batch(i, 0)
                batch(i, 1)
                attend(i, 0)
                pe.wait_ge(c_act, i * 2 + 1)
                pe.wait_ge(c_dve, i * 2 + 1)
                attend(i, 1)
                pe.wait_ge(c_act, i * 2 + 2)
                pe.wait_ge(c_dve, i * 2 + 2)
                for h in range(HQ):
                    last = nc.tensor.matmul(ps_o[:, :], aT[:, h, :], wot[:, h, :], start=h == 0, stop=h == HQ - 1)
                last.then_inc(o_made, 1)

        @block.scalar
        def _(act):
            s = nc.scalar
            act.wait_ge(s_w, 48)
            with act.Fori(0, TILES) as i:
                for par in range(2):
                    at = bass.ds(i * P + par * S, S)
                    s.activation(qs[:, par, :, :], qk[:, 0:HQ, at], ACT.Copy).then_inc(q_staged, 1)
                    s.activation(hb[:, par, :, :], hT[:, :, at], ACT.Copy).then_inc(q_staged, 1)
                for par in range(2):
                    n = i * 2 + par
                    act.wait_ge(v_made, n + 1)
                    s.activation(Vs[:, par, :], ps_v[0:S, :], ACT.Copy).then_inc(v_copied, 1)
                    act.wait_ge(shifted, n + 1)
                    s.activation(pr[:, par, :, :], sc[:, par, :, :], ACT.Exp, scale=SSCALE).then_inc(expd, 1)
                for par in range(2):
                    n = i * 2 + par
                    act.wait_ge(t_made, n + 1)
                    s.activation(pT[:, par, 0:H], ps_t[0][0:S, :], ACT.Copy).then_inc(t_act, 1)
                    act.wait_ge(c_made, n + 1)
                    for kv in range(2):
                        last = s.activation(aT[:, kv * REP:(kv + 1) * REP, par * S:(par + 1) * S],
                                            ps_c[0][:, kv, :].rearrange("p (h q) -> p h q", q=S), ACT.Identity,
                                            bias=bv[:, kv:kv + 1])
                    last.then_inc(c_act, 1)

        @block.vector
        def _(dve):
            v = nc.vector
            dve.wait_ge(s_w, 48)
            with dve.Fori(0, TILES) as i:
                steps = [0]

                def link(instruction):
                    steps[0] += 1
                    instruction.then_inc(soft, 1)
                    dve.wait_ge(soft, i * 10 + steps[0])

                def shift(par):
                    dve.wait_ge(s_made, i * 2 + (par + 1))
                    m = mask[:, :].rearrange("p (o s) -> p o s", o=1).broadcast_to([P, pairs, S])
                    link(v.tensor_tensor(sc[:, par, :, :], ps_s[par][:, :, :], m, ALU.add))
                    link(v.tensor_reduce(mx[:, par, :], sc[:, par, :, :], AX.X, ALU.max))
                    top = mx[:, par, :].rearrange("p (j o) -> p j o", o=1).broadcast_to([P, pairs, S])
                    v.tensor_tensor(sc[:, par, :, :], sc[:, par, :, :], top, ALU.subtract).then_inc(shifted, 1)

                def norm(par):
                    dve.wait_ge(expd, i * 2 + (par + 1))
                    link(v.tensor_reduce(sm[:, par, :], pr[:, par, :, :], AX.X, ALU.add))
                    link(v.reciprocal(sm[:, par, :], sm[:, par, :]))
                    inv = sm[:, par, :].rearrange("p (j o) -> p j o", o=1).broadcast_to([P, pairs, S])
                    v.tensor_tensor(pr[:, par, :, :], pr[:, par, :, :], inv, ALU.mult).then_inc(p_ready, 1)

                shift(0)
                norm(0)
                shift(1)
                norm(1)
                for par in range(2):
                    n = i * 2 + par
                    dve.wait_ge(t_made, n + 1)
                    v.tensor_copy(pT[:, par, H:2 * H], ps_t[1][0:S, :]).then_inc(t_dve, 1)
                    dve.wait_ge(c_made, n + 1)
                    for kv in range(2, HKV):
                        last = v.tensor_scalar(aT[:, kv * REP:(kv + 1) * REP, par * S:(par + 1) * S],
                                               ps_c[1][:, kv - 2, :].rearrange("p (h q) -> p h q", q=S),
                                               bv[:, kv:kv + 1], None, ALU.add)
                    last.then_inc(c_dve, 1)
                dve.wait_ge(o_made, i + 1)
                xt = x[:, bass.ds(i, 1), :].rearrange("p o n -> p (o n)")
                link(v.tensor_tensor(xt, ps_o[:, :], xt, ALU.add))
                link(v.tensor_copy(sm[:, 0, 0:1], sm[:, 0, 1:2]))
                assert steps[0] == 10, steps


def stage_d(nc, x, xT, ident, a, out):
    with ExitStack() as ctx:
        def sb(name, shape):
            return ctx.enter_context(nc.sbuf_tensor(name, shape, F32))

        def sem(name):
            return ctx.enter_context(nc.semaphore(name))

        TE = TILES * E
        half = TOK // 2
        w1 = sb("w1", [P, HC, F])
        w2 = sb("w2", [P, FC, H])
        b1 = sb("b1", [P, FC])
        b2 = sb("b2", [P, H])
        rw = sb("rw", [P, HC, E])
        tri = sb("tri", [P, 2, P])
        iota = sb("iota", [P, 2, E])
        xf = sb("xf", [P, 2, H])
        hh = sb("hh", [P, FC, TOK])
        stats, mv = sb("stats_d", [P, TILES, 6]), sb("mv_d", [P, TILES, 2])
        v1, r1, t1 = sb("v1_d", [P, TILES]), sb("r1_d", [P, TILES]), sb("t1_d", [P, TILES])
        pp, cand = sb("pp", [P, TILES, E]), sb("cand", [P, TILES, E])
        oh = sb("oh", [P, 2, TILES, E])
        top, pick = sb("top", [P, 2, TILES]), sb("pick", [P, TILES])
        cum, off = sb("cum", [P, 2, TILES, E]), sb("off", [P, 2 * TILES, E])
        tot = sb("tot", [P, 2 * TILES, E])
        room, wt = sb("room", [P, 2, TILES]), sb("wt", [P, TILES])
        y = sb("y", [P, 2, H])
        ps_t = [ctx.enter_context(nc.psum_tensor(f"d_t{i}", [P, H], F32)) for i in range(2)]
        ps_r = ctx.enter_context(nc.psum_tensor("d_r", [P, TILES, E], F32))
        ps_c = ctx.enter_context(nc.psum_tensor("d_c", [P, 2, 2 * TE], F32))
        ps_f = [ctx.enter_context(nc.psum_tensor(f"d_f{i}", [P, half], F32)) for i in range(2)]
        ps_y = [ctx.enter_context(nc.psum_tensor(f"d_y{i}", [P, H], F32)) for i in range(2)]
        s_w, s_w1, s_w2, s_ch = sem("d_w"), sem("d_w1"), sem("d_w2"), sem("d_chain")
        xf_ready, xT_done, xT_copied, logits, r_shift, r_exp = (
            sem("xf_ready"), sem("d_xT_done"), sem("d_xT_copied"), sem("logits"), sem("r_shift"), sem("r_exp"))
        chosen, counted, f_made, f_out, y_made, y_read, y_ready, s_out = (
            sem("chosen"), sem("counted"), sem("f_made"), sem("f_out"), sem("y_made"), sem("y_read"),
            sem("y_ready"), sem("s_out"))
        block = ctx.enter_context(nc.Block())

        @block.sync
        def _(sp):
            for dst, name in ((b1, "b1"), (b2, "b2"), (rw, "rw"), (tri, "tri"), (iota, "iota")):
                sp.dma_start(dst[tuple([slice(None)] * len(dst.shape))], a[name]).then_inc(s_w, 16)
            sp.dma_start(w1[:, :, :], a["w1"]).then_inc(s_w1, 16)
            sp.dma_start(w2[:, :, :], a["w2"]).then_inc(s_w2, 16)
            for t in range(TILES):
                sp.wait_ge(y_ready, t + 1)
                sp.dma_start(out[t, :, :], x[:, t, :]).then_inc(s_out, 16)
            sp.wait_ge(s_out, 16 * TILES)

        @block.vector
        def _(dve):
            v = nc.vector
            link = chain(dve, s_ch)
            for t in range(TILES):
                link(v.bn_stats(stats[:, t, :], x[:, t, :]))
            for t in range(TILES):
                link(v.bn_aggr(mv[:, t, :], stats[:, t, :]))
            link(v.tensor_scalar(v1[:, :], mv[:, :, 1], LN_EPS, None, ALU.add))
            rsqrt(link, v, v1[:, :], r1[:, :], t1[:, :])
            for t in range(TILES):
                if t >= 2:
                    dve.wait_ge(xT_done, t - 1)
                v.tensor_scalar(xf[:, t % 2, :], x[:, t, :], mv[:, t, 0:1], r1[:, t:t + 1],
                                ALU.subtract, ALU.mult).then_inc(xf_ready, 1)

            def over_e(s_):
                return s_.rearrange("p (t o) -> p t o", o=1).broadcast_to([P, TILES, E])

            def experts(k):
                return iota[:, k:k + 1, :].broadcast_to([P, TILES, E])

            dve.wait_ge(s_w, 80)
            dve.wait_ge(logits, 1)
            link(v.tensor_reduce(pick[:, :], ps_r[:, :, :], AX.X, ALU.max))
            v.tensor_tensor(pp[:, :, :], ps_r[:, :, :], over_e(pick[:, :]), ALU.subtract).then_inc(r_shift, 1)
            dve.wait_ge(r_exp, 1)
            link(v.tensor_reduce(pick[:, :], pp[:, :, :], AX.X, ALU.add))
            link(v.reciprocal(pick[:, :], pick[:, :]))
            link(v.tensor_tensor(pp[:, :, :], pp[:, :, :], over_e(pick[:, :]), ALU.mult))
            for k in range(2):
                link(v.tensor_reduce(top[:, k, :], pp[:, :, :], AX.X, ALU.max))
                link(v.tensor_tensor(cand[:, :, :], pp[:, :, :], over_e(top[:, k, :]), ALU.is_equal))
                link(v.tensor_scalar(cand[:, :, :], cand[:, :, :], -100.0, None, ALU.mult))
                link(v.tensor_tensor(cand[:, :, :], cand[:, :, :], experts(1), ALU.add))
                link(v.tensor_reduce(pick[:, :], cand[:, :, :], AX.X, ALU.min))
                link(v.tensor_tensor(oh[:, k, :, :], over_e(pick[:, :]), experts(0), ALU.is_equal))
                if k == 0:
                    link(v.tensor_scalar(cand[:, :, :], oh[:, 0, :, :], -2.0, None, ALU.mult))
                    link(v.tensor_tensor(pp[:, :, :], pp[:, :, :], cand[:, :, :], ALU.add))
            v.memset(off[:, 0, :], 0.0).then_inc(chosen, 1)
            dve.wait_ge(counted, 1)
            link(v.tensor_copy(tot[:, :, :].rearrange("p n e -> p (n e)"), ps_c[:, 1, :]))
            for n in range(1, 2 * TILES):
                link(v.tensor_tensor(off[:, n, :], off[:, n - 1, :], tot[:, n - 1, :], ALU.add))
            flat = cum[:, :, :, :].rearrange("p k t e -> p (k t e)")
            link(v.tensor_tensor(flat, ps_c[:, 0, :], off[:, :, :].rearrange("p n e -> p (n e)"), ALU.add))
            link(v.tensor_tensor(flat, flat, oh[:, :, :, :].rearrange("p k t e -> p (k t e)"), ALU.mult))
            link(v.tensor_reduce(room[:, :, :].rearrange("p k t -> p (k t)"),
                                 cum[:, :, :, :].rearrange("p k t e -> p (k t) e"), AX.X, ALU.add))
            link(v.tensor_scalar(room[:, :, :], room[:, :, :], float(CAP), None, ALU.is_le))
            link(v.tensor_tensor(room[:, :, :], room[:, :, :], top[:, :, :], ALU.mult))
            link(v.tensor_tensor(wt[:, :], room[:, 0, :], room[:, 1, :], ALU.add))
            for t in range(TILES):
                dve.wait_ge(y_made, t + 1)
                v.tensor_tensor(y[:, t % 2, :], ps_y[t % 2][:, :], b2[:, :], ALU.add).then_inc(y_read, 1)
                dve.wait_ge(y_read, t + 1)
                v.scalar_tensor_tensor(x[:, t, :], y[:, t % 2, :], wt[:, t:t + 1], x[:, t, :],
                                       ALU.mult, ALU.add).then_inc(y_ready, 1)

        @block.scalar
        def _(act):
            s = nc.scalar
            for t in range(TILES):
                act.wait_ge(xT_done, t + 1)
                s.activation(xT[:, :, t * P:(t + 1) * P], ps_t[t % 2][:, :].rearrange("p (c n) -> p c n", n=P),
                             ACT.Copy).then_inc(xT_copied, 1)
            act.wait_ge(r_shift, 1)
            s.activation(pp[:, :, :], pp[:, :, :], ACT.Exp).then_inc(r_exp, 1)
            act.wait_ge(s_w, 80)
            for n in range(2 * FC):
                act.wait_ge(f_made, n + 1)
                s.activation(hh[:, n // 2, (n % 2) * half:(n % 2 + 1) * half], ps_f[n % 2][:, :], ACT.Gelu,
                             bias=b1[:, n // 2:n // 2 + 1]).then_inc(f_out, 1)

        @block.tensor
        def _(pe):
            for t in range(TILES):
                pe.wait_ge(xf_ready, t + 1)
                if t >= 2:
                    pe.wait_ge(xT_copied, t - 1)
                for c in range(HC):
                    last = nc.tensor.transpose(ps_t[t % 2][:, c * P:(c + 1) * P], xf[:, t % 2, c * P:(c + 1) * P],
                                               ident[:, :])
                last.then_inc(xT_done, 1)
            pe.wait_ge(s_w, 80)
            pe.wait_ge(xT_copied, TILES)
            for t in range(TILES):
                for c in range(HC):
                    last = nc.tensor.matmul(ps_r[:, t, :], xT[:, c, t * P:(t + 1) * P], rw[:, c, :],
                                            start=c == 0, stop=c == HC - 1)
            last.then_inc(logits, 1)
            pe.wait_ge(s_w1, 16)

            def hidden(n):
                if n >= 2:
                    pe.wait_ge(f_out, n - 1)
                for c in range(HC):
                    last = nc.tensor.matmul(ps_f[n % 2][:, :], w1[:, c, (n // 2) * P:(n // 2 + 1) * P],
                                            xT[:, c, (n % 2) * half:(n % 2 + 1) * half],
                                            start=c == 0, stop=c == HC - 1)
                last.then_inc(f_made, 1)

            for n in range(FC):
                hidden(n)
            pe.wait_ge(chosen, 1)
            for k in range(2):
                last = nc.tensor.matmul(ps_c[:, k, :], tri[:, k, :], oh[:, :, :, :].rearrange("p k t e -> p (k t e)"),
                                        start=True, stop=True)
            last.then_inc(counted, 1)
            for n in range(FC, 2 * FC):
                hidden(n)
            pe.wait_ge(s_w2, 16)
            pe.wait_ge(f_out, 2 * FC)
            for t in range(TILES):
                if t >= 2:
                    pe.wait_ge(y_read, t - 1)
                for f in range(FC):
                    last = nc.tensor.matmul(ps_y[t % 2][:, :], hh[:, f, t * P:(t + 1) * P], w2[:, f, :],
                                            start=f == 0, stop=f == FC - 1)
                last.then_inc(y_made, 1)


def perceiver_layer(nc, a, out):
    with ExitStack() as ctx:
        def sb(name, shape):
            return ctx.enter_context(nc.sbuf_tensor(name, shape, F32))

        up = sb("up", [P, HC, TOK])
        ident = sb("ident_sb", [P, P])
        stage_a(nc, up, ident, a)
        stage_b(nc, up, ident, a)
        x = sb("x_sb", [P, TILES, H])
        up2 = sb("up2", [P, HC, TOK])
        stage_c_norms(nc, x, up, up2, ident, a)
        with nc.sbuf_tensor("qk", [P, HQ + HKV, TOK], F32) as qk:
            stage_c_project(nc, up2, qk, a)
            stage_c_attend(nc, x, up2, qk, ident, a)
        stage_d(nc, x, up, ident, a, out)


def laid_out(i):
    n = {k.removeprefix("L0_"): np.asarray(v) for k, v in i.items()}
    x = {k: v for k, v in n.items()}
    o = {}
    f32 = np.float32
    o["x"] = x["x"].reshape(TILES, P, H).transpose(1, 0, 2)
    yT = x["ctx_1024"].transpose(0, 2, 1).reshape(B, KDC, P, KEYS)
    y = np.zeros((B, KDC, P, KCOLS), yT.dtype)
    y[..., :MAIN] = yT[..., :MAIN]
    y[..., DCA_AT:] = yT[..., MAIN:]
    o["yT"] = y.transpose(0, 2, 1, 3)
    o["wq"] = x["xattn_Wq"].reshape(HC, P, H).transpose(1, 0, 2)
    o["bq"] = np.broadcast_to(x["xattn_bq"], (P, H))
    rep = P // XD
    o["qnw"] = np.tile(x["xattn_qn_w"], rep)[:, None]
    o["qnb"] = np.tile(x["xattn_qn_b"], rep)[:, None]
    w = np.concatenate([x["xattn_Wk"], x["xattn_Wv"]], 1).reshape(KDC, P, 2, 8, 2, XD)
    o["wm"] = w.transpose(1, 0, 2, 4, 3, 5).reshape(P, KDC, 2, 16 * XD)
    w = x["xattn_Wkv_dca"].reshape(KDC, P, 2, 2, 8, XD)
    o["wd"] = w.transpose(1, 0, 3, 2, 4, 5).reshape(P, KDC, 2, 16 * XD)
    b = np.concatenate([x["xattn_bk"], x["xattn_bv"]]).reshape(XH, 2, XD)
    bd = x["xattn_bkv_dca"].reshape(2, XH, XD)
    o["bkm"] = np.broadcast_to(b[:, 0].reshape(2, 8 * XD), (P, 2, 8 * XD))
    o["bkd"] = np.broadcast_to(bd[0].reshape(2, 8 * XD), (P, 2, 8 * XD))
    norms = [np.tile(x["xattn_" + k], rep)[:, None] for k in ("kn_w", "kn_b", "kn_dca_w", "kn_dca_b")]
    o["cols"] = np.concatenate(norms + [b[:, 1].reshape(4, P).T, bd[1].reshape(4, P).T], 1)
    o["wo"] = x["xattn_Wo"].reshape(HC, P, H).transpose(1, 0, 2)
    o["bo"] = np.broadcast_to(x["xattn_bo"], (P, H))
    o["lnw"] = np.broadcast_to(x["attn_ln_weight"], (P, H))
    w = np.concatenate([x["attn_q_project"], x["attn_k_project"]], 0).T.reshape(HC, P, (HQ + HKV) * D)
    o["wqk"] = w.transpose(1, 0, 2)
    o["bqk"] = np.concatenate([x["attn_q_bias"], x["attn_k_bias"]]).reshape(HQ + HKV, D).T
    o["wv"] = x["attn_v_project"].T.reshape(HC, P, HKV * D).transpose(1, 0, 2)
    o["bv_c"] = x["attn_v_bias"].reshape(HKV, D).T
    o["wot"] = x["attn_o_project"].T.reshape(HQ, P, H).transpose(1, 0, 2)
    o["w1"] = x["ffn_w1"].T.reshape(HC, P, F).transpose(1, 0, 2)
    o["b1"] = x["ffn_b1"].reshape(FC, P).T
    o["w2"] = x["ffn_w2"].T.reshape(FC, P, H).transpose(1, 0, 2)
    o["b2"] = np.broadcast_to(x["ffn_b2"], (P, H))
    o["rw"] = x["ffn_router_w"].T.reshape(HC, P, E).transpose(1, 0, 2)
    inv = (f32(1.0) / np.power(f32(10000.0), np.arange(0, D, 2, dtype=f32) / f32(D))).astype(f32)
    ang = (np.arange(S, dtype=f32)[:, None] * inv).astype(f32)
    cos, sin = np.cos(ang).astype(f32).T, np.sin(ang).astype(f32).T
    o["rope"] = np.stack([np.concatenate([cos, cos]), np.concatenate([-sin, sin])], 1)
    q, k = np.arange(P)[:, None] % S, np.arange(S)[None, :]
    o["mask"] = np.where(k <= q, 0.0, MASKED).astype(f32)
    o["ident"] = np.eye(P, dtype=f32)
    upper = (np.arange(P)[:, None] <= np.arange(P)[None, :]).astype(f32)
    o["tri"] = np.stack([upper, np.ones((P, P), f32)], 1)
    e = np.arange(E, dtype=f32)
    o["iota"] = np.broadcast_to(np.stack([e, e + 100]), (P, 2, E))
    return {k: np.ascontiguousarray(v) for k, v in o.items()}


def kernel(**inputs):
    import concourse.bacc as bacc
    from concourse.bass_utils import run_bass_kernel_spmd

    nc = bacc.Bacc("TRN2", target_bir_lowering=False, num_devices=1)
    arrays = {f"in_{k}": v for k, v in laid_out(inputs).items()}
    a = {k.removeprefix("in_"): nc.dram_tensor(k, v.shape, mybir.dt.from_np(v.dtype), kind="ExternalInput").ap()
         for k, v in arrays.items()}
    out = nc.dram_tensor("out", (TILES, P, H), F32, kind="ExternalOutput").ap()
    perceiver_layer(nc, a, out)
    r = run_bass_kernel_spmd(nc, [arrays], core_ids=[0])
    return r.results[0]["out"].reshape(B, S, H)
```

```python
from contextlib import ExitStack

import numpy as np

import concourse.bass as bass
from concourse import mybir

F32 = mybir.dt.float32
I32 = mybir.dt.int32
F32R = mybir.dt.float32r
ALU = mybir.AluOpType
ACT = mybir.ActivationFunctionType
AX = mybir.AxisListType

P = 128
B, S, H = 16, 64, 512
TOK = B * S
TILES = TOK // P
HC = H // P
KEYS, KD = 1601, 256
DCA = 16
MAIN = KEYS - DCA
XH, XD = 16, 32
KDC = KD // P
KT_FULL = MAIN // P
KTILES = KT_FULL + 1
DCA_AT = KT_FULL * P + 64
KCOLS = DCA_AT + DCA
LAST = KCOLS - KT_FULL * P
SCH = KCOLS // 4
MAIN3 = MAIN - 3 * SCH
XSCALE = float(XD) ** -0.5
HQ, HKV, D = 16, 4, 128
REP = HQ // HKV
SSCALE = float(1.0 / np.sqrt(np.float32(D)))
E, CAP, F = 8, 128, 2048
FC = F // P
LN_EPS, QK_EPS, RMS_EPS = 1e-5, 1e-6, 1e-6
MASKED = -1e30
PAIRS = 4
HW = 8 * XD
KTS = (KTILES + 1) // 2
STEPS = 2 * KTS
AHEAD = 3
CHUNKS = ((0, 8), (8, KTILES))


def rsqrt(link, v, x, y, t):
    link(v.tensor_scalar(t.bitcast(I32), x.bitcast(I32), 1, None, ALU.logical_shift_right))
    link(v.tensor_scalar(y.bitcast(I32), t.bitcast(I32), -1.0, 1597463007.0, ALU.mult, ALU.add))
    for _ in range(3):
        link(v.tensor_tensor(t, y, y, ALU.mult))
        link(v.scalar_tensor_tensor(t, t, -0.5, x, ALU.mult, ALU.mult))
        link(v.scalar_tensor_tensor(y, t, 1.5, y, ALU.add, ALU.mult))


def chain(eng, sem):
    count = [0]

    def link(instruction):
        count[0] += 1
        instruction.then_inc(sem, 1)
        eng.wait_ge(sem, count[0])
    return link


def stage_a(nc, qT, ident, kv, a):
    with ExitStack() as ctx:
        def sb(name, shape):
            return ctx.enter_context(nc.sbuf_tensor(name, shape, F32))

        def sem(name):
            return ctx.enter_context(nc.semaphore(name))

        x = sb("x_a", [P, TILES, H])
        wq = sb("wq", [P, HC, H])
        bq = sb("bq", [P, H])
        qnw = sb("qnw", [P, 1])
        qnb = sb("qnb", [P, 1])
        xn = sb("xn", [P, TILES, H])
        xnT = sb("xnT", [P, 2, HC, P])
        q = sb("q", [P, TILES, H])
        sq = sb("sq_a", [P, TILES, H])
        stats = sb("stats_a", [P, TILES, 6])
        mv = sb("mv_a", [P, TILES, 2])
        r1 = sb("r1_a", [P, TILES])
        v1 = sb("v1_a", [P, TILES])
        t1 = sb("t1_a", [P, TILES])
        qm = sb("qm", [P, TILES * XH])
        qv = sb("qv", [P, TILES * XH])
        qr = sb("qr", [P, TILES * XH])
        qt = sb("qt", [P, TILES * XH])
        wh, wl, wd, bkm, bkd = kv
        wm = sb("wm", [P, KDC, 2, 2 * HW])
        mean_w, mean_b = sb("mean_w", [P, 2 * KDC, 8]), sb("mean_b", [P, 2 * 8])
        ps_t = [ctx.enter_context(nc.psum_tensor(f"a_t{i}", [P, H], F32)) for i in range(2)]
        ps_q = [ctx.enter_context(nc.psum_tensor(f"a_q{i}", [P, H], F32)) for i in range(4)]
        s_x = [sem(f"a_x{i}") for i in range(4)]
        s_w, s_ch = sem("a_w"), sem("a_chain")
        xn_ready, xT_ready, xT_copied, q_ready = sem("xn_ready"), sem("xT_ready"), sem("xT_copied"), sem("q_ready")
        q_copied, q_centred, q_squared = sem("q_copied"), sem("q_centred"), sem("q_squared")
        qn_ready, qT_ready, qT_copied = sem("qn_ready"), sem("qT_ready"), sem("qT_copied")
        s_kv, centred, kv_centred, wh_ready = sem("a_kv"), sem("centred"), sem("kv_centred"), sem("kv_wh")
        qr_ready, qn_ready_dve = sem("qr_ready"), sem("qn_ready_dve")
        block = ctx.enter_context(nc.Block())
        HT = TILES // 2

        def scale(engine, t):
            ht = q[:, t, :].rearrange("p (h d) -> p h d", d=XD)
            rt = qr[:, t * XH:(t + 1) * XH].rearrange("p (n o) -> p n o", o=1).broadcast_to([P, XH, XD])
            engine.tensor_tensor(ht, ht, rt, ALU.mult).then_inc(qn_ready if t < HT else qn_ready_dve, 1)

        @block.sync
        def _(sp):
            for i in range(4):
                sp.dma_start(x[:, 2 * i:2 * i + 2, :], a["x"][:, 2 * i:2 * i + 2, :]).then_inc(s_x[i], 16)
                if i == 1:
                    sp.dma_start(ident[:, :], a["ident"]).then_inc(s_w, 16)
                    sp.dma_start(wq[:, :, :], a["wq"]).then_inc(s_w, 16)
                    sp.dma_start(bq[:, :], a["bq"]).then_inc(s_w, 16)
                    sp.dma_start(qnw[:, :], a["qnw"]).then_inc(s_w, 16)
                    sp.dma_start(qnb[:, :], a["qnb"]).then_inc(s_w, 16)
            for dst, name in ((wm, "wm"), (wd, "wd"), (bkm, "bkm"), (bkd, "bkd")):
                sp.dma_start(dst[tuple([slice(None)] * len(dst.shape))], a[name]).then_inc(s_kv, 16)

        @block.vector
        def _(dve):
            v = nc.vector
            link = chain(dve, s_ch)

            def normalise(hf):
                ts = range(hf * HT, (hf + 1) * HT)
                for t in ts:
                    if t % 2 == 0:
                        dve.wait_ge(s_x[t // 2], 16)
                    link(v.bn_stats(stats[:, t, :], x[:, t, :]))
                for t in ts:
                    link(v.bn_aggr(mv[:, t, :], stats[:, t, :]))
                of = slice(hf * HT, (hf + 1) * HT)
                link(v.tensor_scalar(v1[:, of], mv[:, of, 1], LN_EPS, None, ALU.add))
                rsqrt(link, v, v1[:, of], r1[:, of], t1[:, of])
                for t in ts:
                    v.tensor_scalar(xn[:, t, :], x[:, t, :], mv[:, t, 0:1], r1[:, t:t + 1],
                                    ALU.subtract, ALU.mult).then_inc(xn_ready, 1)

            def queries(hf):
                for t in range(hf * HT, (hf + 1) * HT):
                    dve.wait_ge(q_ready, t + 1)
                    v.tensor_tensor(q[:, t, :], ps_q[t % 4][:, :], bq[:, :], ALU.add).then_inc(q_copied, 1)
                dve.wait_ge(q_copied, (hf + 1) * HT)
                of = slice(hf * HT * XH, (hf + 1) * HT * XH)
                heads = q[:, :, :].rearrange("p t (h d) -> p (t h) d", d=XD)[:, of, :]
                sqh = sq[:, :, :].rearrange("p t (h d) -> p (t h) d", d=XD)[:, of, :]
                link(v.tensor_reduce(qm[:, of], heads, AX.X, ALU.add))
                link(v.tensor_scalar(qm[:, of], qm[:, of], -1.0 / XD, None, ALU.mult))
                mean = qm[:, of].rearrange("p (n o) -> p n o", o=1).broadcast_to([P, HT * XH, XD])
                v.tensor_tensor(heads, heads, mean, ALU.add).then_inc(q_centred, 1)
                dve.wait_ge(q_squared, hf + 1)
                link(v.tensor_reduce(qv[:, of], sqh, AX.X, ALU.add))
                link(v.tensor_scalar(qv[:, of], qv[:, of], 1.0 / XD, QK_EPS, ALU.mult, ALU.add))
                rsqrt(link, v, qv[:, of], qr[:, of], qt[:, of])
                if hf == 0:
                    v.tensor_copy(qt[:, 0:1], qr[:, 0:1]).then_inc(qr_ready, 1)
                else:
                    for t in range(HT, TILES):
                        scale(v, t)

            def centre():
                dve.wait_ge(s_kv, 64)
                for wt, bt in ((wm, bkm), (wd, bkd)):
                    kw = wt[:, :, :, 0:HW].rearrange("p c f (h d) -> p (c f) h d", d=XD)
                    link(v.tensor_reduce(mean_w[:, :, :], kw, AX.X, ALU.add))
                    link(v.tensor_scalar(mean_w[:, :, :], mean_w[:, :, :], -1.0 / XD, None, ALU.mult))
                    for f in range(2 * KDC):
                        mf = mean_w[:, f, :].rearrange("p (h o) -> p h o", o=1).broadcast_to([P, 8, XD])
                        v.tensor_tensor(kw[:, f, :, :], kw[:, f, :, :], mf, ALU.add).then_inc(centred, 1)
                    bh = bt[:, :, :].rearrange("p f (h d) -> p (f h) d", d=XD)
                    m = mean_b[:, :]
                    link(v.tensor_reduce(m, bh, AX.X, ALU.add))
                    link(v.tensor_scalar(m, m, -1.0 / XD, None, ALU.mult))
                    v.tensor_tensor(bh, bh, m.rearrange("p (h o) -> p h o", o=1).broadcast_to([P, 16, XD]),
                                    ALU.add).then_inc(kv_centred, 1)
                    dve.wait_ge(centred, 4 * KDC if wt is wd else 2 * KDC)
                    dve.wait_ge(kv_centred, 2 if wt is wd else 1)

            normalise(0)
            normalise(1)
            dve.wait_ge(s_w, 80)
            centre()
            queries(0)
            queries(1)

        @block.scalar
        def _(act):
            def transposed(t):
                act.wait_ge(xT_ready, t + 1)
                if t >= 2:
                    act.wait_ge(q_ready, t - 1)
                nc.scalar.activation(xnT[:, t % 2, :, :].rearrange("p c n -> p (c n)"), ps_t[t % 2][:, :],
                                     ACT.Copy).then_inc(xT_copied, 1)

            def squares(hf):
                act.wait_ge(q_centred, hf + 1)
                of = slice(hf * HT, (hf + 1) * HT)
                nc.scalar.activation(sq[:, of, :], q[:, of, :], ACT.Square).then_inc(q_squared, 1)

            for t in range(TILES):
                transposed(t)
            squares(0)
            act.wait_ge(kv_centred, 2)
            nc.scalar.activation(wh[:, :, :, :], wm[:, :, :, :], ACT.Copy).then_inc(wh_ready, 1)
            act.wait_ge(s_w, 80)
            for t in range(TILES):
                if t == HT:
                    squares(1)
                act.wait_ge(qT_ready, t + 1)
                nc.scalar.activation(qT[:, :, t * P:(t + 1) * P],
                                     ps_t[t % 2][:, :].rearrange("p (g n) -> p g n", n=P), ACT.Identity,
                                     bias=qnb[:, 0:1], scale=qnw[:, 0:1]).then_inc(qT_copied, 1)

        @block.gpsimd
        def _(pool):
            pool.wait_ge(qr_ready, 1)
            for t in range(HT):
                scale(nc.gpsimd, t)
            pool.wait_ge(wh_ready, 1)
            nc.gpsimd.tensor_tensor(wl[:, :, :, :], wm[:, :, :, :], wh[:, :, :, :].bitcast(F32), ALU.subtract)

        @block.tensor
        def _(pe):
            pe.wait_ge(s_w, 80)

            def project(t):
                pe.wait_ge(xT_copied, t + 1)
                if t >= 4:
                    pe.wait_ge(q_copied, t - 3)
                for c in range(HC):
                    last = nc.tensor.matmul(ps_q[t % 4][:, :], xnT[:, t % 2, c, :], wq[:, c, :],
                                            start=c == 0, stop=c == HC - 1)
                last.then_inc(q_ready, 1)

            for t in range(TILES):
                pe.wait_ge(xn_ready, t + 1)
                if t >= 2:
                    pe.wait_ge(xT_copied, t - 1)
                for c in range(HC):
                    last = nc.tensor.transpose(ps_t[t % 2][:, c * P:(c + 1) * P], xn[:, t, c * P:(c + 1) * P],
                                               ident[:, :])
                last.then_inc(xT_ready, 1)
                if t:
                    project(t - 1)
            project(TILES - 1)
            for t in range(TILES):
                if t < HT:
                    pe.wait_ge(qn_ready, t + 1)
                else:
                    pe.wait_ge(qn_ready_dve, t + 1 - HT)
                pe.wait_ge(xT_copied, TILES)
                if t >= 2:
                    pe.wait_ge(qT_copied, t - 1)
                for g in range(HC):
                    last = nc.tensor.transpose(ps_t[t % 2][:, g * P:(g + 1) * P], q[:, t, g * P:(g + 1) * P],
                                               ident[:, :])
                last.then_inc(qT_ready, 1)


def bank_uses(more):
    order = [("V", m) for m in range(KTS)]
    if more:
        order += [("K", m) for m in range(KTS)]
    order += [("P", s) for s in range(AHEAD)]
    for s in range(STEPS):
        if more:
            order += [("T", j) for j in range(KTS) if KEY_STEPS[j] == s]
        if s + AHEAD < STEPS:
            order.append(("P", s + AHEAD))
    return order


POOL_STEPS = (2, 4)
KEY_STEPS = tuple(KTS - 1 + max(j - 1, 0) for j in range(KTS))
PROLOGUE = [("K", m) for m in range(KTS)] + [("T", j) for j in range(KTS)]


def stage_b(nc, up, ident, kv, a):
    with ExitStack() as ctx:
        def sb(name, shape, dt=F32):
            return ctx.enter_context(nc.sbuf_tensor(name, shape, dt))

        def sem(name):
            return ctx.enter_context(nc.semaphore(name))

        yh, yl = sb("yh", [P, KDC, KCOLS], F32R), sb("yl", [P, KDC, KCOLS], F32R)
        yraw = sb("yraw", [P, 2, KDC, 4 * P])
        yd = sb("yd", [P, KDC, LAST])
        wh, wl, wd, bkm, bkd = kv
        cols = sb("cols", [P, 12])
        Kc = sb("Kc", [P, KTILES, HW])
        Sq = sb("Sq", [P, KTILES, HW])
        Kf = sb("Kf", [P, 2, 2, 2 * P])
        kTh, kTl = sb("kTh", [P, 2, KCOLS], F32R), sb("kTl", [P, 2, KCOLS], F32R)
        Vh, Vl = sb("Vh", [P, KTILES, HW], F32R), sb("Vl", [P, KTILES, HW], F32R)
        qb = sb("qb", [P, 2, 2, P])
        qbh, qbl = sb("qbh", [P, 2, 2, P], F32R), sb("qbl", [P, 2, 2, P], F32R)
        Pr = sb("Pr", [P, PAIRS, KCOLS])
        PTh, PTl = sb("PTh", [P, AHEAD, 4 * P], F32R), sb("PTl", [P, AHEAD, 4 * P], F32R)
        PTf = sb("PTf", [P, 4 * P])
        nb = sb("nb", [P, PAIRS, 4])
        nbs = sb("nbs", [P, PAIRS, 2])
        sums = sb("sums", [P, PAIRS, 3])
        linv = sb("linv", [P, PAIRS, 2])
        NV = KTILES * 8
        var, rst, ntmp = sb("var", [P, NV]), sb("rst", [P, NV]), sb("ntmp", [P, NV])
        ps_s = ctx.enter_context(nc.psum_tensor("ps_s", [P, 4, 512], F32))
        ps_w = [ctx.enter_context(nc.psum_tensor(f"ps_w{i}", [P, 512], F32)) for i in range(3)]
        ps_v = ctx.enter_context(nc.psum_tensor("ps_v", [P, 512], F32))
        s_w = sem("b_w")
        s_y = [sem(f"b_y{c}") for c in range(4)]
        s_q = sem("b_q")
        dve_chain = sem("dve_chain")
        w_ready, pads_zero, yh_ready, y_split = sem("w_ready"), sem("pads_zero"), sem("yh_ready"), sem("y_split")
        filled, read = [sem(f"filled{i}") for i in range(3)], [sem(f"read{i}") for i in range(3)]
        s_done, bias_ready, exp_done, linv_ready, p_scaled = (
            sem("s_done"), sem("bias_ready"), sem("exp_done"), sem("linv_ready"), sem("p_scaled"))
        vh_ready, kf_ready, kh_ready, kl_ready = sem("vh_ready"), sem("kf_ready"), sem("kh_ready"), sem("kl_ready")
        sq_done, var_ready, kn_ready = sem("sq_done"), sem("var_ready"), sem("kn_ready")
        ph_ready, pv_done, ctx_copied, qb_ready = sem("ph_ready"), sem("pv_done"), sem("ctx_copied"), sem("qb_ready")
        pf_ready, pl_ready = sem("pf_ready"), sem("pl_ready")
        Y0 = tuple(range(0, KTILES, 4))
        block = ctx.enter_context(nc.Block())

        def units(body, fori):
            with fori(0, B - 1) as i:
                body(i * 2, 0, True)
                body(i * 2, 1, True)
            body(2 * (B - 1), 0, True)
            body(2 * (B - 1), 1, False)

        FULL, ENDING = bank_uses(True), bank_uses(False)
        IN_SLOT = [len(range(i, len(FULL), 3)) for i in range(3)]
        IN_PROLOGUE = [len(range(i, len(PROLOGUE), 3)) for i in range(3)]

        def use(U, kind, j, more=True):
            if U is None:
                n = PROLOGUE.index((kind, j))
                return n % 3, n // 3
            n = (FULL if more else ENDING).index((kind, j))
            bank = n % 3
            return bank, U * IN_SLOT[bank] + (IN_PROLOGUE[bank] + n // 3)

        def tiles_of(m):
            return range(2 * m, min(2 * m + 2, KTILES))

        def normalise(engine, W, j):
            n = len(tiles_of(j))
            kh = Kc[:, 2 * j:2 * j + n, :].rearrange("p t (h d) -> p (t h) d", d=XD)
            rr = rst[:, 16 * j:(2 * j + n) * 8].rearrange("p (h o) -> p h o", o=1)
            engine.tensor_tensor(kh, kh, rr.broadcast_to([P, n * 8, XD]), ALU.mult).then_inc(kn_ready, 1)

        def rows_of(t):
            return P if t < KT_FULL else LAST

        @block.sync
        def _(sp):
            sp.dma_start(cols[:, :], a["cols"]).then_inc(s_w, 16)

            def load(c, yb):
                if c < 3:
                    sp.dma_start(yraw[:, c % 2, :, :], yb[:, :, c * 4 * P:(c + 1) * 4 * P]).then_inc(s_y[c], 16)
                else:
                    sp.dma_start(yd[:, :, :], yb[:, :, KT_FULL * P:KCOLS]).then_inc(s_y[c], 16)

            def queries(par, at):
                for i in range(4):
                    r, c = slice(32 * i, 32 * i + 32), slice(64 * (i % 2), 64 * (i % 2) + 64)
                    sp.dma_start(qb[r, :, i // 2, c], up[r, 2 * par:2 * par + 2, bass.ds(at, S)]).then_inc(s_q, 16)

            y0 = a["yT"][0:1, :, :, :].rearrange("b p c n -> p (b c) n")
            load(0, y0)
            load(1, y0)
            load(3, y0)
            sp.wait_ge(pads_zero, 1)
            queries(0, 0)
            sp.wait_ge(y_split, 1)
            load(2, y0)

            def slot(u0, par, more):
                U = u0 + par
                if not more:
                    return
                sp.wait_ge(qb_ready, U + 1)
                queries(1 - par, u0 * 32 + (S if par else 0))
                if isinstance(u0, int):
                    return
                b = u0 // 2 + 1
                yb = a["yT"][bass.ds(b, 1), :, :, :].rearrange("b p c n -> p (b c) n")
                if par == 0:
                    sp.wait_ge(y_split, u0 * 2 + 3)
                    load(0, yb)
                    load(1, yb)
                else:
                    sp.wait_ge(y_split, u0 * 2 + 5)
                    load(2, yb)
                    bank, n = use(U, "V", KTS - 1)
                    sp.wait_ge(filled[bank], n + 1)
                    load(3, yb)

            units(slot, sp.Fori)

        @block.tensor
        def _(pe):
            def three(out, lhs, rhs, start, stop):
                (lh, ll), (rh, rl) = lhs, rhs
                nc.tensor.matmul(out, lh, rh, start=start, stop=False)
                nc.tensor.matmul(out, ll, rh, start=False, stop=False)
                return nc.tensor.matmul(out, lh, rl, start=False, stop=stop)

            def free(b, n):
                if not (isinstance(n, int) and n == 0):
                    pe.wait_ge(read[b], n)

            def project(b, n, par, kv, m):
                free(b, n)
                bank = ps_w[b]
                for t in tiles_of(m):
                    r, at = rows_of(t), slice(t * P, t * P + rows_of(t))
                    o = bank[0:r, (t % 2) * HW:(t % 2 + 1) * HW]
                    ch = slice(kv * HW, (kv + 1) * HW)
                    for c in range(KDC):
                        last = three(o, (yh[:, c, at], yl[:, c, at]), (wh[:, c, par, ch], wl[:, c, par, ch]),
                                     c == 0, c == KDC - 1)
                    if t == KTILES - 1:
                        for c in range(KDC):
                            last = nc.tensor.matmul(bank[0:r, HW:2 * HW], yd[:, c, :], wd[:, c, par, ch],
                                                    start=c == 0, stop=c == KDC - 1)
                last.then_inc(filled[b], 1)

            def make_keys(b, n, par, m, batch4):
                if batch4 is not None and 2 * m in Y0:
                    pe.wait_ge(y_split, batch4 + (Y0.index(2 * m) + 1))
                project(b, n, par, 0, m)

            def key_transposes(b, n, W, j):
                pe.wait_ge(kn_ready, W * KTS + (j + 1))
                free(b, n)
                for t in tiles_of(j):
                    r = rows_of(t)
                    for g in range(2):
                        at = g * 256 + (t % 2) * P
                        last = nc.tensor.transpose(ps_w[b][:, at:at + r], Kc[0:r, t, g * P:(g + 1) * P],
                                                   ident[0:r, 0:r])
                last.then_inc(filled[b], 1)

            for m in range(KTS):
                make_keys(*use(None, "K", m), 0, m, 0)
            for j in range(KTS):
                key_transposes(*use(None, "T", j), 0, j)

            def slot(u0, par, more):
                U = u0 + par
                batch4 = (u0 * 2 + 4) if par else None

                def values(m):
                    project(*use(U, "V", m, more), par, 1, m)

                def keys(m):
                    if more:
                        make_keys(*use(U, "K", m), 1 - par, m, batch4)

                def scores(p):
                    g, i = p // 2, p % 2
                    if p == 0:
                        pe.wait_ge(kl_ready, (U + 1) * KTS)
                        pe.wait_ge(qb_ready, U + 1)
                    for c in range(4):
                        at = slice(c * SCH, (c + 1) * SCH)
                        if c == 0:
                            pe.wait_ge(exp_done, U * 8 + (2 * p + 1))
                        if c == 3:
                            pe.wait_ge(exp_done, U * 8 + (2 * p + 2))
                        last = three(ps_s[:, c, 0:SCH], (qbh[:, g, i, :], qbl[:, g, i, :]),
                                     (kTh[:, g, at], kTl[:, g, at]), True, True)
                        if c >= 1:
                            last.then_inc(s_done, 1)

                def turn(s):
                    g, j = s // KTS, s % KTS
                    b, n = use(U, "P", s, more)
                    if j == 0:
                        pe.wait_ge(p_scaled, U * PAIRS + (2 * g + 2))
                    free(b, n)
                    for t in tiles_of(j):
                        r = rows_of(t)
                        for i in range(2):
                            at = (t % 2) * 256 + i * P
                            last = nc.tensor.transpose(ps_w[b][0:r, at:at + P],
                                                       Pr[:, 2 * g + i, t * P:t * P + r], ident[:, :])
                    last.then_inc(filled[b], 1)

                def weigh(s):
                    g, j = s // KTS, s % KTS
                    b, n = use(U, "P", s, more)
                    if j == 0 and (g == 1 or par == 1):
                        pe.wait_ge(ctx_copied, U * 2 + g)
                    if s in POOL_STEPS:
                        pe.wait_ge(pl_ready, U * len(POOL_STEPS) + (POOL_STEPS.index(s) + 1))
                    else:
                        pe.wait_ge(read[b], n + 1)
                    for t in tiles_of(j):
                        r, ch, at = rows_of(t), slice(g * P, (g + 1) * P), slice((t % 2) * 256, (t % 2) * 256 + 256)
                        last = three(ps_v[:, 0:256], (Vh[0:r, t, ch], Vl[0:r, t, ch]),
                                     (PTh[0:r, s % AHEAD, at], PTl[0:r, s % AHEAD, at]), t == 0, t == KTILES - 1)
                    if j == KTS - 1:
                        last.then_inc(pv_done, 1)

                for m in range(0, 3):
                    values(m)
                scores(0)
                for m in range(3, KTS):
                    values(m)
                scores(1)
                for m in range(0, 3):
                    keys(m)
                scores(2)
                for m in range(3, 6):
                    keys(m)
                scores(3)
                for m in range(6, KTS):
                    keys(m)
                for s in range(AHEAD):
                    turn(s)
                for s in range(STEPS):
                    weigh(s)
                    for j in range(KTS):
                        if more and KEY_STEPS[j] == s:
                            key_transposes(*use(U, "T", j), U + 1, j)
                    if s + AHEAD < STEPS:
                        turn(s + AHEAD)

            units(slot, pe.Fori)

        @block.vector
        def _(dve):
            v = nc.vector
            made = [0]
            base = [0]

            def link(instruction):
                instruction.then_inc(dve_chain, 1)
                made[0] += 1
                dve.wait_ge(dve_chain, base[0] + made[0])

            v.memset(Kc[:, KTILES - 1, :], 0.0)
            v.memset(qb[:, :, :, :], 0.0).then_inc(pads_zero, 1)
            v.memset(Pr[:, :, MAIN:DCA_AT], 0.0)
            dve.wait_ge(s_w, 16)
            v.memset(nb[:, :, :], 0.0).then_inc(w_ready, 1)
            dve.wait_ge(w_ready, 1)

            def key_bias(b, n, par, m):
                dve.wait_ge(filled[b], n + 1)
                if m < KTS - 1:
                    both = bkm[:, par:par + 1, :].broadcast_to([P, 2, HW])
                    v.tensor_tensor(Kc[:, 2 * m:2 * m + 2, :], ps_w[b][:, :].rearrange("p (t n) -> p t n", n=HW),
                                    both, ALU.add).then_inc(read[b], 1)
                else:
                    v.tensor_tensor(Kc[0:64, KT_FULL, :], ps_w[b][0:64, 0:HW], bkm[0:64, par, :], ALU.add)
                    v.tensor_tensor(Kc[64:LAST, KT_FULL, :], ps_w[b][64:LAST, HW:2 * HW], bkd[64:LAST, par, :],
                                    ALU.add).then_inc(read[b], 1)

            def square_sums(W, t0, t1):
                dve.wait_ge(sq_done, W * 2 + (1 if t1 <= CHUNKS[0][1] else 2))
                link(v.tensor_reduce(var[:, t0 * 8:t1 * 8],
                                     Sq[:, t0:t1, :].rearrange("p t (h d) -> p (t h) d", d=XD), AX.X, ALU.add))

            def root_start():
                link(v.tensor_scalar(var[:, :], var[:, :], 1.0 / XD, QK_EPS, ALU.mult, ALU.add))
                link(v.tensor_scalar(ntmp[:, :].bitcast(I32), var[:, :].bitcast(I32), 1, None,
                                     ALU.logical_shift_right))
                link(v.tensor_scalar(rst[:, :].bitcast(I32), ntmp[:, :].bitcast(I32), -1.0, 1597463007.0,
                                     ALU.mult, ALU.add))

            def root_step(last):
                link(v.tensor_tensor(ntmp[:, :], rst[:, :], rst[:, :], ALU.mult))
                link(v.scalar_tensor_tensor(ntmp[:, :], ntmp[:, :], -0.5, var[:, :], ALU.mult, ALU.mult))
                step = v.scalar_tensor_tensor(rst[:, :], ntmp[:, :], 1.5, rst[:, :], ALU.add, ALU.mult)
                if last:
                    step.then_inc(var_ready, 1)
                else:
                    link(step)

            def keys_high(W, j):
                dve.wait_ge(kf_ready, W * KTS + (j + 1))
                n = 2 * P if j < KTS - 1 else LAST
                v.tensor_copy(kTh[:, :, j * 256:j * 256 + n], Kf[:, j % 2, :, 0:n]).then_inc(kh_ready, 1)

            def queries(W):
                dve.wait_ge(s_q, W * 64 + 64)
                link(v.tensor_copy(qbh[:, :, :, :], qb[:, :, :, :]))
                v.tensor_tensor(qbl[:, :, :, :], qb[:, :, :, :], qbh[:, :, :, :].bitcast(F32),
                                ALU.subtract).then_inc(qb_ready, 1)

            for m in range(KTS):
                key_bias(*use(None, "K", m), 0, m)
            square_sums(0, 0, 8)
            square_sums(0, 8, KTILES)
            root_start()
            for i in range(3):
                root_step(i == 2)
            dve.wait_ge(var_ready, 1)
            for j in range(KTS):
                normalise(v, 0, j)
            queries(0)
            for j in range(KTS):
                keys_high(0, j)
            before = made[0]

            def slot(u0, par, more):
                U = u0 + par
                if par == 0:
                    made[0] = 0
                    base[0] = u0 * LINKS + before

                def values_low(m):
                    b, n = use(U, "V", m, more)
                    dve.wait_ge(vh_ready, U * KTS + (m + 1))
                    if m < KTS - 1:
                        v.tensor_tensor(Vl[:, 2 * m:2 * m + 2, :], ps_w[b][:, :].rearrange("p (t n) -> p t n", n=HW),
                                        Vh[:, 2 * m:2 * m + 2, :].bitcast(F32), ALU.subtract).then_inc(read[b], 1)
                    else:
                        for r, c0 in ((slice(0, 64), 0), (slice(64, LAST), HW)):
                            last = v.tensor_tensor(Vl[r, KT_FULL, :], ps_w[b][r, c0:c0 + HW],
                                                   Vh[r, KT_FULL, :].bitcast(F32), ALU.subtract)
                        last.then_inc(read[b], 1)

                def maxima(p):
                    def done(part):
                        return U * 3 * PAIRS + (3 * p + part)

                    dve.wait_ge(s_done, done(1))
                    v.tensor_reduce(nb[:, p, 0:1], ps_s[:, 0:2, 0:SCH], AX.XY, ALU.max, negate=True)
                    dve.wait_ge(s_done, done(2))
                    link(v.tensor_reduce(nb[:, p, 1:2], ps_s[:, 2, 0:SCH], AX.X, ALU.max, negate=True))
                    v.tensor_tensor(nb[:, p, 0:1], nb[:, p, 0:1], nb[:, p, 1:2], ALU.min)
                    dve.wait_ge(s_done, done(3))
                    v.tensor_reduce(nb[:, p, 2:3], ps_s[:, 3, 0:MAIN3], AX.X, ALU.max, negate=True)
                    link(v.tensor_reduce(nb[:, p, 3:4], ps_s[:, 3, DCA_AT - 3 * SCH:SCH], AX.X, ALU.max,
                                         negate=True))
                    v.tensor_scalar(nbs[:, p, 0:1], nb[:, p, 0:1], nb[:, p, 2:3], XSCALE, ALU.min, ALU.mult)
                    v.tensor_scalar(nbs[:, p, 1:2], nb[:, p, 3:4], XSCALE, None,
                                    ALU.mult).then_inc(bias_ready, 1)

                def inverse(p):
                    dve.wait_ge(exp_done, U * 8 + (2 * p + 4))
                    link(v.tensor_tensor(sums[:, p, 0:1], sums[:, p, 0:1], sums[:, p, 2:3], ALU.add))
                    v.reciprocal(linv[:, p, :], sums[:, p, 0:2]).then_inc(linv_ready, 1)

                def keys(m):
                    if more:
                        key_bias(*use(U, "K", m), 1 - par, m)

                def low(s):
                    b, _ = use(U, "P", s, more)
                    dve.wait_ge(ph_ready, U * STEPS + (s + 1))
                    n, c1 = (P, 512) if s % KTS < KTS - 1 else (LAST, 256)
                    v.tensor_tensor(PTl[0:n, s % AHEAD, 0:c1], ps_w[b][0:n, 0:c1],
                                    PTh[0:n, s % AHEAD, 0:c1].bitcast(F32), ALU.subtract).then_inc(read[b], 1)

                def context(g):
                    dve.wait_ge(pv_done, U * 2 + (g + 1))
                    gg = 2 * par + g
                    for i in range(4):
                        r = slice(32 * i, 32 * i + 32)
                        last = v.tensor_scalar(up[r, gg, bass.ds(u0 * 32, S)], ps_v[r, 64 * i:64 * i + 64],
                                               cols[r, 4 + gg:5 + gg], cols[r, 8 + gg:9 + gg], ALU.add, ALU.add)
                    last.then_inc(ctx_copied, 1)

                for m in range(0, 3):
                    values_low(m)
                maxima(0)
                for m in range(3, KTS):
                    values_low(m)
                inverse(0)
                maxima(1)
                for m in range(0, 3):
                    keys(m)
                inverse(1)
                maxima(2)
                for m in range(3, 6):
                    keys(m)
                inverse(2)
                maxima(3)
                keys(6)
                low(0)
                if more:
                    square_sums(U + 1, 0, 4)
                low(1)
                if more:
                    square_sums(U + 1, 4, 8)
                inverse(3)
                if more:
                    square_sums(U + 1, 8, KTILES)
                low(3)
                if more:
                    root_start()
                    for i in range(3):
                        root_step(i == 2)
                for s in range(5, 9):
                    low(s)
                context(0)
                if more:
                    keys_high(U + 1, 0)
                for s in range(9, STEPS):
                    low(s)
                    if more:
                        keys_high(U + 1, s - 8)
                if more:
                    queries(U + 1)
                    for j in range(STEPS - 8, KTS):
                        keys_high(U + 1, j)
                context(1)
                if more:
                    assert made[0] == (par + 1) * LINKS, made

            LINKS = 3 * PAIRS + 3 + 11 + 1
            units(slot, dve.Fori)

        @block.scalar
        def _(act):
            s_ = nc.scalar

            def y_high(c, batch):
                act.wait_ge(s_y[c], batch * 16 + 16)
                src = yraw[:, c % 2, :, :] if c < 3 else yd[:, :, :]
                s_.activation(yh[:, :, Y0[c] * P:min((Y0[c] + 4) * P, KCOLS)], src, ACT.Copy).then_inc(yh_ready, 1)

            def squares(W, c, b, n):
                t0, t1 = CHUNKS[c]
                act.wait_ge(read[b], n + 1)
                s_.activation(Sq[:, t0:t1, :], Kc[:, t0:t1, :], ACT.Square).then_inc(sq_done, 1)

            def keys_out(b, n, W, j):
                act.wait_ge(filled[b], n + 1)
                if not (isinstance(W, int) and W == 0 and j < 2):
                    act.wait_ge(kl_ready, W * KTS + (j - 1))
                src = ps_w[b][:, :].rearrange("p (g n) -> p g n", g=2)
                if j < KTS - 1:
                    s_.activation(Kf[:, j % 2, :, :], src, ACT.Identity, scale=cols[:, 0:1],
                                  bias=cols[:, 1:2]).then_inc(kf_ready, 1)
                else:
                    s_.activation(Kf[:, j % 2, :, 0:64], src[:, :, 0:64], ACT.Identity, scale=cols[:, 0:1],
                                  bias=cols[:, 1:2])
                    s_.activation(Kf[:, j % 2, :, 64:LAST], src[:, :, 64:LAST], ACT.Identity, scale=cols[:, 2:3],
                                  bias=cols[:, 3:4]).then_inc(kf_ready, 1)
                act.wait_ge(kf_ready, W * KTS + (j + 1))
                act.sem_inc(read[b], 1)

            for c in range(4):
                y_high(c, 0)
            act.wait_ge(w_ready, 1)
            squares(0, 0, *use(None, "K", 3))
            squares(0, 1, *use(None, "K", KTS - 1))
            for j in range(KTS):
                keys_out(*use(None, "T", j), 0, j)
            s_.activation(sums[:, 0, :], nb[:, 0, 0:3], ACT.Copy).then_inc(exp_done, 2)

            def slot(u0, par, more):
                U = u0 + par

                def values(m):
                    b, n = use(U, "V", m, more)
                    act.wait_ge(filled[b], n + 1)
                    if m < KTS - 1:
                        s_.activation(Vh[:, 2 * m:2 * m + 2, :], ps_w[b][:, :].rearrange("p (t n) -> p t n", n=HW),
                                      ACT.Copy).then_inc(vh_ready, 1)
                    else:
                        s_.activation(Vh[0:64, KT_FULL, :], ps_w[b][0:64, 0:HW], ACT.Copy)
                        s_.activation(Vh[64:LAST, KT_FULL, :], ps_w[b][64:LAST, HW:2 * HW],
                                      ACT.Copy).then_inc(vh_ready, 1)

                def next_y(c):
                    if par == 1 and more:
                        y_high(c, u0 // 2 + 1)

                def exps(p):
                    act.wait_ge(bias_ready, U * PAIRS + (p + 1))
                    s_.activation(Pr[:, p, 0:3 * SCH].rearrange("p (c n) -> p c n", n=SCH), ps_s[:, 0:3, 0:SCH],
                                  ACT.Exp, bias=nbs[:, p, 0:1], scale=XSCALE, accum_out=sums[:, p, 0:1]).then_inc(exp_done, 1)
                    s_.activation(Pr[:, p, 3 * SCH:MAIN], ps_s[:, 3, 0:MAIN3], ACT.Exp, bias=nbs[:, p, 0:1],
                                  scale=XSCALE, accum_out=sums[:, p, 2:3])
                    s_.activation(Pr[:, p, DCA_AT:KCOLS], ps_s[:, 3, DCA_AT - 3 * SCH:SCH], ACT.Exp,
                                  bias=nbs[:, p, 1:2], scale=XSCALE, accum_out=sums[:, p, 1:2]).then_inc(exp_done, 1)

                def high(s):
                    b, n = use(U, "P", s, more)
                    act.wait_ge(filled[b], n + 1)
                    r, c1 = (P, 512) if s % KTS < KTS - 1 else (LAST, 256)
                    s_.activation(PTh[0:r, s % AHEAD, 0:c1], ps_w[b][0:r, 0:c1], ACT.Copy).then_inc(ph_ready, 1)
                    if s in POOL_STEPS:
                        k = POOL_STEPS.index(s)
                        if k:
                            act.wait_ge(pl_ready, U * len(POOL_STEPS) + k)
                        s_.activation(PTf[:, :], ps_w[b][:, :], ACT.Copy).then_inc(pf_ready, 1)
                        act.wait_ge(pf_ready, U * len(POOL_STEPS) + (k + 1))
                        act.sem_inc(read[b], 1)

                values(0)
                values(1)
                next_y(0)
                values(2)
                values(3)
                exps(0)
                next_y(1)
                values(4)
                values(5)
                values(6)
                next_y(2)
                exps(1)
                next_y(3)
                exps(2)
                if more:
                    squares(U + 1, 0, *use(U, "K", 3))
                high(0)
                high(1)
                exps(3)
                if more:
                    squares(U + 1, 1, *use(U, "K", KTS - 1))
                high(2)
                high(3)
                for s in range(4, 9):
                    high(s)
                if more:
                    keys_out(*use(U, "T", 0), U + 1, 0)
                    keys_out(*use(U, "T", 1), U + 1, 1)
                for s in range(9, STEPS):
                    high(s)
                    if more and s - 7 < KTS:
                        keys_out(*use(U, "T", s - 7), U + 1, s - 7)

            units(slot, act.Fori)

        @block.gpsimd
        def _(pool):
            g_ = nc.gpsimd

            def y_low(c, batch4):
                pool.wait_ge(yh_ready, batch4 + (c + 1))
                src = yraw[:, c % 2, :, :] if c < 3 else yd[:, :, :]
                at = slice(Y0[c] * P, min((Y0[c] + 4) * P, KCOLS))
                g_.tensor_tensor(yl[:, :, at], src, yh[:, :, at].bitcast(F32), ALU.subtract).then_inc(y_split, 1)

            def keys_low(W, j):
                pool.wait_ge(kh_ready, W * KTS + (j + 1))
                n = 2 * P if j < KTS - 1 else LAST
                at = slice(j * 256, j * 256 + n)
                g_.tensor_tensor(kTl[:, :, at], Kf[:, j % 2, :, 0:n], kTh[:, :, at].bitcast(F32),
                                 ALU.subtract).then_inc(kl_ready, 1)

            def norm_and_low(W):
                pool.wait_ge(var_ready, W + 1)
                for j in range(4):
                    normalise(g_, W, j)
                for j in range(KTS):
                    keys_low(W, j)
                    if j + 4 < KTS:
                        normalise(g_, W, j + 4)

            for c in range(4):
                y_low(c, 0)
            for j in range(KTS):
                keys_low(0, j)

            def slot(u0, par, more):
                U = u0 + par

                def next_y(c):
                    if par == 1 and more:
                        y_low(c, u0 * 2 + 4)

                def low(s):
                    pool.wait_ge(pf_ready, U * len(POOL_STEPS) + (POOL_STEPS.index(s) + 1))
                    g_.tensor_tensor(PTl[:, s % AHEAD, :], PTf[:, :], PTh[:, s % AHEAD, :].bitcast(F32),
                                     ALU.subtract).then_inc(pl_ready, 1)

                def scale(p):
                    pool.wait_ge(linv_ready, U * PAIRS + (p + 1))
                    g_.tensor_tensor(Pr[:, p, DCA_AT:KCOLS], Pr[:, p, DCA_AT:KCOLS],
                                     linv[:, p, 1:2].broadcast_to([P, DCA]), ALU.mult)
                    g_.tensor_scalar(Pr[:, p, 0:MAIN], Pr[:, p, 0:MAIN], linv[:, p, 0:1], 1.0,
                                     ALU.mult, ALU.mult).then_inc(p_scaled, 1)

                next_y(0)
                next_y(1)
                scale(0)
                next_y(2)
                next_y(3)
                scale(1)
                scale(2)
                for s in POOL_STEPS:
                    low(s)
                scale(3)
                if more:
                    norm_and_low(U + 1)

            units(slot, pool.Fori)


def stage_c_norms(nc, x, ctxT, hT, hTh, hTl, wqk, s_wqk, ident, a):
    with ExitStack() as ctx:
        def sb(name, shape):
            return ctx.enter_context(nc.sbuf_tensor(name, shape, F32))

        def sem(name):
            return ctx.enter_context(nc.semaphore(name))

        wo = sb("wo", [P, HC, H])
        bo = sb("bo", [P, H])
        lnw = sb("lnw", [P, H])
        h = sb("h", [P, TILES, H])
        hs = sb("hs", [P, H])
        stats = sb("stats_c", [P, TILES, 6])
        mv = sb("mv_c", [P, TILES, 2])
        v1, r1, t1 = sb("v1_c", [P, TILES]), sb("r1_c", [P, TILES]), sb("t1_c", [P, TILES])
        ss, r2 = sb("ss_c", [P, TILES]), sb("r2_c", [P, TILES])
        ps_o = [ctx.enter_context(nc.psum_tensor(f"c_o{i}", [P, H], F32)) for i in range(4)]
        ps_t = [ctx.enter_context(nc.psum_tensor(f"c_t{i}", [P, H], F32)) for i in range(2)]
        s_wo, s_x, s_ch = sem("c_wo"), [sem(f"c_x{i}") for i in range(2)], sem("c_chain")
        xb_ready, o_done, o_added, h_ready, sq_done = (
            sem("xb_ready"), sem("o_done"), sem("o_added"), sem("h_ready"), sem("c_sq"))
        hn_ready, hT_done, hTh_ready, hTl_ready = sem("hn_ready"), sem("hT_done"), sem("hTh_ready"), sem("hTl_ready")
        block = ctx.enter_context(nc.Block())
        HT = TILES // 2

        @block.sync
        def _(sp):
            sp.dma_start(wo[:, :, :], a["wo"]).then_inc(s_wo, 16)
            sp.dma_start(bo[:, :], a["bo"]).then_inc(s_x[0], 16)
            sp.dma_start(x[:, 0:HT, :], a["x"][:, 0:HT, :]).then_inc(s_x[0], 16)
            sp.dma_start(x[:, HT:TILES, :], a["x"][:, HT:TILES, :]).then_inc(s_x[1], 16)
            sp.dma_start(lnw[:, :], a["lnw"]).then_inc(s_x[1], 16)
            for i in range(2):
                sp.dma_start(wqk[:, i, :, :], a["wqk"][:, :, 4 * i * D:4 * (i + 1) * D]).then_inc(s_wqk[i], 16)

        @block.tensor
        def _(pe):
            pe.wait_ge(s_wo, 16)
            for t in range(TILES):
                if t >= 4:
                    pe.wait_ge(o_added, t - 3)
                for g in range(HC):
                    last = nc.tensor.matmul(ps_o[t % 4][:, :], ctxT[:, g, t * P:(t + 1) * P], wo[:, g, :],
                                            start=g == 0, stop=g == HC - 1)
                last.then_inc(o_done, 1)
            for t in range(TILES):
                pe.wait_ge(hn_ready, t + 1)
                if t >= 2:
                    pe.wait_ge(hTl_ready, t - 1)
                for c in range(HC):
                    last = nc.tensor.transpose(ps_t[t % 2][:, c * P:(c + 1) * P], h[:, t, c * P:(c + 1) * P],
                                               ident[:, :])
                last.then_inc(hT_done, 1)

        @block.vector
        def _(dve):
            v = nc.vector
            link = chain(dve, s_ch)

            def of(hf):
                return slice(hf * HT, (hf + 1) * HT)

            def bias(hf):
                dve.wait_ge(s_x[hf], 32)
                for t in range(TILES)[of(hf)]:
                    v.tensor_tensor(x[:, t, :], x[:, t, :], bo[:, :], ALU.add).then_inc(xb_ready, 1)

            def norm(hf):
                for t in range(TILES)[of(hf)]:
                    dve.wait_ge(xb_ready, TILES)
                    dve.wait_ge(o_done, t + 1)
                    v.tensor_tensor(x[:, t, :], ps_o[t % 4][:, :], x[:, t, :], ALU.add).then_inc(o_added, 1)
                    dve.wait_ge(o_added, t + 1)
                    link(v.bn_stats(stats[:, t, :], x[:, t, :]))
                for t in range(TILES)[of(hf)]:
                    link(v.bn_aggr(mv[:, t, :], stats[:, t, :]))
                s = of(hf)
                link(v.tensor_scalar(v1[:, s], mv[:, s, 1], LN_EPS, None, ALU.add))
                rsqrt(link, v, v1[:, s], r1[:, s], t1[:, s])
                for t in range(TILES)[of(hf)]:
                    v.tensor_scalar(h[:, t, :], x[:, t, :], mv[:, t, 0:1], r1[:, t:t + 1],
                                    ALU.subtract, ALU.mult).then_inc(h_ready, 1)

            def rms(hf):
                dve.wait_ge(sq_done, (hf + 1) * HT)
                s = of(hf)
                link(v.tensor_scalar(ss[:, s], ss[:, s], 1.0 / H, RMS_EPS, ALU.mult, ALU.add))
                rsqrt(link, v, ss[:, s], r2[:, s], t1[:, s])
                for t in range(TILES)[of(hf)]:
                    v.scalar_tensor_tensor(h[:, t, :], h[:, t, :], r2[:, t:t + 1], lnw[:, :],
                                           ALU.mult, ALU.mult).then_inc(hn_ready, 1)

            def low(t):
                dve.wait_ge(hTh_ready, t + 1)
                at = slice(t * P, (t + 1) * P)
                v.tensor_tensor(hTl[:, :, at], ps_t[t % 2][:, :].rearrange("p (c n) -> p c n", n=P),
                                hTh[:, :, at].bitcast(F32), ALU.subtract).then_inc(hTl_ready, 1)

            bias(0)
            bias(1)
            norm(0)
            rms(0)
            norm(1)
            for t in range(HT):
                low(t)
            rms(1)
            for t in range(HT, TILES):
                low(t)

        @block.scalar
        def _(act):
            s = nc.scalar

            def squares(hf):
                for t in range(hf * HT, (hf + 1) * HT):
                    act.wait_ge(h_ready, t + 1)
                    s.activation(hs[:, :], h[:, t, :], ACT.Square, accum_out=ss[:, t:t + 1]).then_inc(sq_done, 1)
                    act.wait_ge(sq_done, t + 1)

            def transposed(t):
                act.wait_ge(hT_done, t + 1)
                src = ps_t[t % 2][:, :].rearrange("p (c n) -> p c n", n=P)
                s.activation(hT[:, :, t * P:(t + 1) * P], src, ACT.Copy)
                s.activation(hTh[:, :, t * P:(t + 1) * P], src, ACT.Copy).then_inc(hTh_ready, 1)

            squares(0)
            transposed(0)
            transposed(1)
            squares(1)
            for t in range(2, TILES):
                transposed(t)


def stage_c_project(nc, hTh, hTl, qk, wqk, s_wqk, a):
    heads = HQ + HKV
    half = TOK // 2
    with ExitStack() as ctx:
        def sb(name, shape, dt=F32):
            return ctx.enter_context(nc.sbuf_tensor(name, shape, dt))

        def sem(name):
            return ctx.enter_context(nc.semaphore(name))

        wh, wl = sb("wqk_h", [P, 2, HC, D], F32R), sb("wqk_l", [P, 2, HC, D], F32R)
        bqk = sb("bqk", [P, heads])
        rope = sb("rope", [P, 2, S])
        raw, swapped = sb("raw", [P, 2, half]), sb("swapped", [P, 2, half])
        ra, rb = sb("ra", [P, 2, half]), sb("rb", [P, 2, half])
        ps = [ctx.enter_context(nc.psum_tensor(f"cp{i}", [P, half], F32)) for i in range(4)]
        s_b = sem("cp_b")
        wh_ready, wl_ready = sem("cp_wh"), sem("cp_wl")
        made, raw_ready, cos_ready, sin_ready, qk_ready = (
            sem("cp_made"), sem("raw_ready"), sem("cos_ready"), sem("sin_ready"), sem("qk_ready"))
        s_swap = [sem(f"swap{i}") for i in range(2)]
        block = ctx.enter_context(nc.Block())
        n_steps = 2 * heads

        @block.sync
        def _(sp):
            sp.dma_start(bqk[:, :], a["bqk"]).then_inc(s_b, 16)
            sp.dma_start(rope[:, :, :], a["rope"]).then_inc(s_b, 16)
            for n in range(n_steps):
                if n % 8 == 0 and 2 <= n // 8 + 1 < heads // 4:
                    i = n // 8 + 1
                    sp.wait_ge(wl_ready, 4 * (i - 1))
                    sp.dma_start(wqk[:, i % 2, :, :], a["wqk"][:, :, 4 * i * D:4 * (i + 1) * D]).then_inc(
                        s_wqk[i % 2], 16)
                sp.wait_ge(raw_ready, n + 1)
                if n >= 2:
                    sp.wait_ge(sin_ready, n - 1)
                sp.dma_start(swapped[0:64, n % 2, :], raw[64:P, n % 2, :]).then_inc(s_swap[n % 2], 16)
                sp.dma_start(swapped[64:P, n % 2, :], raw[0:64, n % 2, :]).then_inc(s_swap[n % 2], 16)

        @block.tensor
        def _(pe):
            def three(out, lhs, rhs, start, stop):
                (lh, ll), (rh, rl) = lhs, rhs
                nc.tensor.matmul(out, lh, rh, start=start, stop=False)
                nc.tensor.matmul(out, ll, rh, start=False, stop=False)
                return nc.tensor.matmul(out, lh, rl, start=False, stop=stop)

            for n in range(n_steps):
                hd, f = n // 2, n % 2
                if f == 0:
                    pe.wait_ge(wl_ready, hd + 1)
                if n >= 4:
                    pe.wait_ge(raw_ready, n - 3)
                at = slice(f * half, (f + 1) * half)
                for c in range(HC):
                    last = three(ps[n % 4][:, :], (wh[:, hd % 2, c, :], wl[:, hd % 2, c, :]),
                                 (hTh[:, c, at], hTl[:, c, at]), c == 0, c == HC - 1)
                last.then_inc(made, 1)

        def head_weights(hd):
            return wqk[:, hd // 4 % 2, :, hd % 4 * D:(hd % 4 + 1) * D]

        @block.scalar
        def _(act):
            def weights(hd):
                act.wait_ge(s_wqk[hd // 4 % 2], 16 * (hd // 8 + 1))
                nc.scalar.activation(wh[:, hd % 2, :, :], head_weights(hd), ACT.Copy).then_inc(wh_ready, 1)

            weights(0)
            weights(1)
            act.wait_ge(s_b, 32)
            for n in range(n_steps):
                act.wait_ge(made, n + 1)
                if n >= 2:
                    act.wait_ge(cos_ready, n - 1)
                    act.wait_ge(s_swap[n % 2], 32 * (n // 2))
                nc.scalar.activation(raw[:, n % 2, :], ps[n % 4][:, :], ACT.Identity,
                                     bias=bqk[:, n // 2:n // 2 + 1]).then_inc(raw_ready, 1)
                if n % 2 and n // 2 + 2 < heads:
                    weights(n // 2 + 2)

        def table(k):
            return rope[:, k:k + 1, :].broadcast_to([P, half // S, S])

        def by_batch(t):
            return t.rearrange("p (b s) -> p b s", s=S)

        @block.vector
        def _(dve):
            def weights(hd):
                dve.wait_ge(wh_ready, hd + 1)
                nc.vector.tensor_tensor(wl[:, hd % 2, :, :], head_weights(hd), wh[:, hd % 2, :, :].bitcast(F32),
                                        ALU.subtract).then_inc(wl_ready, 1)

            weights(0)
            weights(1)
            dve.wait_ge(s_b, 32)

            def add(n):
                dve.wait_ge(sin_ready, n + 1)
                nc.vector.tensor_tensor(qk[:, n // 2, (n % 2) * half:(n % 2 + 1) * half], ra[:, n % 2, :],
                                        rb[:, n % 2, :], ALU.add).then_inc(qk_ready, 1)

            for n in range(n_steps):
                dve.wait_ge(raw_ready, n + 1)
                if n >= 2:
                    dve.wait_ge(qk_ready, n - 1)
                nc.vector.tensor_tensor(by_batch(ra[:, n % 2, :]), by_batch(raw[:, n % 2, :]), table(0),
                                        ALU.mult).then_inc(cos_ready, 1)
                if n % 2 and n // 2 + 2 < heads:
                    weights(n // 2 + 2)
                if n >= 1:
                    if n == 1:
                        dve.wait_ge(cos_ready, 1)
                    dve.wait_ge(cos_ready, n)
                    add(n - 1)
            dve.wait_ge(cos_ready, n_steps)
            add(n_steps - 1)

        @block.gpsimd
        def _(pool):
            pool.wait_ge(s_b, 32)
            for n in range(n_steps):
                pool.wait_ge(s_swap[n % 2], 32 * (n // 2 + 1))
                if n >= 2:
                    pool.wait_ge(qk_ready, n - 1)
                nc.gpsimd.tensor_tensor(by_batch(rb[:, n % 2, :]), by_batch(swapped[:, n % 2, :]), table(1),
                                        ALU.mult).then_inc(sin_ready, 1)


def stage_c_attend(nc, x, hT, qk, mv, ident, a):
    pairs = HQ // 2
    with ExitStack() as ctx:
        def sb(name, shape):
            return ctx.enter_context(nc.sbuf_tensor(name, shape, F32))

        def sem(name):
            return ctx.enter_context(nc.semaphore(name))

        wv = sb("wv", [P, HC, HKV * D])
        wot = sb("wot", [P, HQ, H])
        bv = sb("bv_c", [P, HKV])
        mask = sb("mask", [P, S])
        qs = sb("qs", [P, 2, HQ, S])
        hb = sb("hb", [P, HC, P])
        Vs = sb("Vs", [P, HKV * D])
        sc = sb("sc", [P, 2, pairs, S])
        pr = sb("pr", [P, pairs, 2, S])
        mx, sm = sb("mx", [P, 2, pairs]), sb("sm", [P, 2, pairs])
        pT = sb("pT", [P, pairs * P])
        aT = sb("aT", [P, HQ, P])
        xs, stats, mvs = sb("xs", [P, H]), sb("stats_ca", [P, 6]), sb("mvs", [P, 2])
        ps_s = [ctx.enter_context(nc.psum_tensor(f"ca_s{i}", [P, pairs, S], F32)) for i in range(2)]
        ps_v = ctx.enter_context(nc.psum_tensor("ca_v", [P, H], F32))
        ps_t = [ctx.enter_context(nc.psum_tensor(f"ca_t{i}", [P, H], F32)) for i in range(2)]
        ps_c = [ctx.enter_context(nc.psum_tensor(f"ca_c{i}", [P, 2, REP * S], F32)) for i in range(2)]
        ps_o = ctx.enter_context(nc.psum_tensor("ca_o", [P, H], F32))
        s_w, s_wv, s_wo, x_added = sem("ca_w"), sem("ca_wv"), sem("ca_wo"), sem("x_added")
        q_staged, s_made, v_made, v_copied = sem("q_staged"), sem("s_made"), sem("v_made"), sem("v_copied")
        shifted, expd, p_ready, t_made = sem("shifted"), sem("expd"), sem("p_ready"), sem("t_made")
        t_act, t_dve, c_made, c_act, c_dve, o_made, soft = (
            sem("t_act"), sem("t_dve"), sem("c_made"), sem("c_act"), sem("c_dve"), sem("o_made"), sem("soft"))
        block = ctx.enter_context(nc.Block())

        def tiles(body, fori):
            with fori(0, TILES - 1) as i:
                body(i, True)
            body(TILES - 1, False)

        @block.sync
        def _(sp):
            sp.dma_start(bv[:, :], a["bv_c"]).then_inc(s_w, 16)
            sp.dma_start(mask[:, :], a["mask"]).then_inc(s_w, 16)
            sp.dma_start(wv[:, :, :], a["wv"]).then_inc(s_wv, 16)
            sp.dma_start(wot[:, :, :], a["wot"]).then_inc(s_wo, 16)

        @block.tensor
        def _(pe):
            def scores(i, par):
                pe.wait_ge(q_staged, i * 3 + (par + 1))
                for j in range(pairs):
                    last = nc.tensor.matmul(ps_s[par][:, j, :], qs[:, par, 2 * j:2 * j + 2, :],
                                            qk[:, HQ + j // 2, bass.ds(i * P + par * S, S)], start=True, stop=True)
                last.then_inc(s_made, 1)

            def values(i):
                pe.wait_ge(q_staged, i * 3 + 3)
                for c in range(HC):
                    last = nc.tensor.matmul(ps_v[:, :], hb[:, c, :], wv[:, c, :], start=c == 0, stop=c == HC - 1)
                last.then_inc(v_made, 1)

            def attend(i, par):
                b = slice(par * S, (par + 1) * S)
                for kv in range(HKV):
                    last = nc.tensor.matmul(ps_c[kv // 2][:, kv % 2, :], Vs[b, kv * D:(kv + 1) * D],
                                            pT[b, kv * REP * S:(kv + 1) * REP * S], start=True, stop=True)
                last.then_inc(c_made, 1)

            scores(0, 0)
            scores(0, 1)
            pe.wait_ge(s_wv, 16)
            values(0)
            pe.wait_ge(s_wo, 16)

            def tile(i, more):
                pe.wait_ge(p_ready, i * 2 + 2)
                for j in range(pairs):
                    last = nc.tensor.transpose(ps_t[j // 4][:, (j % 4) * P:(j % 4 + 1) * P], pr[:, j, :, :],
                                               ident[:, :])
                last.then_inc(t_made, 1)
                if more:
                    scores(i + 1, 0)
                pe.wait_ge(v_copied, i + 1)
                pe.wait_ge(t_act, i + 1)
                pe.wait_ge(t_dve, i + 1)
                attend(i, 0)
                if more:
                    scores(i + 1, 1)
                pe.wait_ge(c_act, i * 2 + 1)
                pe.wait_ge(c_dve, i * 2 + 1)
                attend(i, 1)
                if more:
                    values(i + 1)
                pe.wait_ge(c_act, i * 2 + 2)
                pe.wait_ge(c_dve, i * 2 + 2)
                for h in range(HQ):
                    last = nc.tensor.matmul(ps_o[:, :], aT[:, h, :], wot[:, h, :], start=h == 0, stop=h == HQ - 1)
                last.then_inc(o_made, 1)

            tiles(tile, pe.Fori)

        @block.scalar
        def _(act):
            s = nc.scalar

            def stage(i):
                for par in range(2):
                    s.activation(qs[:, par, :, :], qk[:, 0:HQ, bass.ds(i * P + par * S, S)],
                                 ACT.Copy).then_inc(q_staged, 1)
                s.activation(hb[:, :, :], hT[:, :, bass.ds(i * P, P)], ACT.Copy).then_inc(q_staged, 1)

            def values_and_exps(i):
                act.wait_ge(v_made, i + 1)
                s.activation(Vs[:, :], ps_v[:, :], ACT.Copy).then_inc(v_copied, 1)
                for par in range(2):
                    act.wait_ge(shifted, i * 2 + (par + 1))
                    s.activation(pr[:, :, par, :], sc[:, par, :, :], ACT.Exp, scale=SSCALE).then_inc(expd, 1)

            stage(0)
            act.wait_ge(s_w, 32)
            values_and_exps(0)

            def tile(i, more):
                if more:
                    act.wait_ge(v_copied, i + 1)
                    stage(i + 1)
                act.wait_ge(t_made, i + 1)
                s.activation(pT[:, 0:H], ps_t[0][:, :], ACT.Copy).then_inc(t_act, 1)
                for par in range(2):
                    act.wait_ge(c_made, i * 2 + (par + 1))
                    for kv in range(2):
                        last = s.activation(aT[:, kv * REP:(kv + 1) * REP, par * S:(par + 1) * S],
                                            ps_c[0][:, kv, :].rearrange("p (h q) -> p h q", q=S), ACT.Identity,
                                            bias=bv[:, kv:kv + 1])
                    last.then_inc(c_act, 1)
                if more:
                    values_and_exps(i + 1)

            tiles(tile, act.Fori)

        @block.vector
        def _(dve):
            v = nc.vector
            LINKS = 8
            made, base = [0], [0]

            def link(instruction):
                made[0] += 1
                instruction.then_inc(soft, 1)
                dve.wait_ge(soft, base[0] + made[0])

            def softmax(i):
                made[0], base[0] = 0, i * LINKS
                for par in range(2):
                    dve.wait_ge(s_made, i * 2 + (par + 1))
                    m = mask[:, :].rearrange("p (o s) -> p o s", o=1).broadcast_to([P, pairs, S])
                    link(v.tensor_tensor(sc[:, par, :, :], ps_s[par][:, :, :], m, ALU.add))
                    link(v.tensor_reduce(mx[:, par, :], sc[:, par, :, :], AX.X, ALU.max))
                    top = mx[:, par, :].rearrange("p (j o) -> p j o", o=1).broadcast_to([P, pairs, S])
                    v.tensor_tensor(sc[:, par, :, :], sc[:, par, :, :], top, ALU.subtract).then_inc(shifted, 1)
                for par in range(2):
                    dve.wait_ge(expd, i * 2 + (par + 1))
                    link(v.tensor_reduce(sm[:, par, :], pr[:, :, par, :], AX.X, ALU.add))
                    link(v.reciprocal(sm[:, par, :], sm[:, par, :]))
                    inv = sm[:, par, :].rearrange("p (j o) -> p j o", o=1).broadcast_to([P, pairs, S])
                    v.tensor_tensor(pr[:, :, par, :], pr[:, :, par, :], inv, ALU.mult).then_inc(p_ready, 1)
                assert made[0] == LINKS, made

            def evacuate(i):
                dve.wait_ge(t_made, i + 1)
                v.tensor_copy(pT[:, H:2 * H], ps_t[1][:, :]).then_inc(t_dve, 1)
                for par in range(2):
                    dve.wait_ge(c_made, i * 2 + (par + 1))
                    for kv in range(2, HKV):
                        last = v.tensor_scalar(aT[:, kv * REP:(kv + 1) * REP, par * S:(par + 1) * S],
                                               ps_c[1][:, kv - 2, :].rearrange("p (h q) -> p h q", q=S),
                                               bv[:, kv:kv + 1], None, ALU.add)
                    last.then_inc(c_dve, 1)

            def tile_of(t, i):
                return t[:, bass.ds(i, 1), :].rearrange("p o n -> p (o n)")

            def add(i):
                dve.wait_ge(o_made, i + 1)
                v.tensor_tensor(xs[:, :], ps_o[:, :], tile_of(x, i), ALU.add).then_inc(x_added, 1)

            def finish(i):
                xt = tile_of(x, i)
                dve.wait_ge(x_added, i * 3 + 1)
                v.tensor_tensor(xt[:, 0:H // 2], xs[:, 0:H // 2], xs[:, 0:H // 2], ALU.max)
                v.bn_stats(stats[:, :], xs[:, :]).then_inc(x_added, 1)
                dve.wait_ge(x_added, i * 3 + 2)
                v.tensor_tensor(xt[:, H // 2:H], xs[:, H // 2:H], xs[:, H // 2:H], ALU.max)
                v.bn_aggr(mvs[:, :], stats[:, :]).then_inc(x_added, 1)
                dve.wait_ge(x_added, i * 3 + 3)
                v.tensor_tensor(tile_of(mv, i), mvs[:, :], mvs[:, :], ALU.max)

            dve.wait_ge(s_w, 32)
            softmax(0)
            evacuate(0)
            with dve.Fori(0, TILES - 1) as i:
                softmax(i + 1)
                add(i)
                evacuate(i + 1)
                finish(i)
            add(TILES - 1)
            finish(TILES - 1)


def stage_d(nc, x, xT, mv, ident, a, out):
    with ExitStack() as ctx:
        def sb(name, shape, dt=F32):
            return ctx.enter_context(nc.sbuf_tensor(name, shape, dt))

        def sem(name):
            return ctx.enter_context(nc.semaphore(name))

        TE = TILES * E
        half = TOK // 2
        STEPS_F = 2 * FC
        HT = TILES // 2
        w1 = sb("w1", [P, 2, HC, 2 * P])
        w2 = sb("w2", [P, FC, H])
        w1h, w1l = sb("w1h", [P, HC, F], F32R), sb("w1l", [P, HC, F], F32R)
        w2h, w2l = sb("w2h", [P, 2, H], F32R), sb("w2l", [P, 2, H], F32R)
        xTh, xTl = sb("xTh", [P, HC, TOK], F32R), sb("xTl", [P, HC, TOK], F32R)
        b1 = sb("b1", [P, FC])
        b2 = sb("b2", [P, H])
        rw = sb("rw", [P, HC, E])
        tri = sb("tri", [P, 2, P])
        iota = sb("iota", [P, 2, E])
        xf = sb("xf", [P, 2, H])
        hf = sb("hf", [P, 2, half])
        hh, hl = sb("hh", [P, 2, half], F32R), sb("hl", [P, 2, half], F32R)
        v1, r1, t1 = sb("v1_d", [P, TILES]), sb("r1_d", [P, TILES]), sb("t1_d", [P, TILES])
        pp, cand = sb("pp", [P, TILES, E]), sb("cand", [P, TILES, E])
        oh = sb("oh", [P, 2, TILES, E])
        top, pick = sb("top", [P, 2, TILES]), sb("pick", [P, TILES])
        cum, off = sb("cum", [P, 2, TILES, E]), sb("off", [P, 2 * TILES, E])
        tot = sb("tot", [P, 2 * TILES, E])
        room, wt = sb("room", [P, 2, TILES]), sb("wt", [P, TILES])
        y = sb("y", [P, 2, H])
        ps_t = [ctx.enter_context(nc.psum_tensor(f"d_t{i}", [P, H], F32)) for i in range(2)]
        ps_r = ps_t[0][:, 0:TE].rearrange("p (t e) -> p t e", e=E)
        ps_c = ps_t[1][:, 0:4 * TE].rearrange("p (k n) -> p k n", k=2)
        ps_f = [ctx.enter_context(nc.psum_tensor(f"d_f{i}", [P, half], F32)) for i in range(2)]
        ps_y = [ctx.enter_context(nc.psum_tensor(f"d_y{i}", [P, H], F32)) for i in range(HT)]
        s_w, s_ch = sem("d_w"), sem("d_chain")
        s_w1, s_w2 = [sem(f"d_w1{i}") for i in range(2)], [sem(f"d_w2{i}") for i in range(4)]
        xf_ready, xT_done, xTh_ready, xTl_ready, logits, r_shift, r_exp = (
            sem("xf_ready"), sem("d_xT_done"), sem("xTh_ready"), sem("xTl_ready"), sem("logits"), sem("r_shift"),
            sem("r_exp"))
        w1h_ready, w1l_ready, w2h_ready, w2l_ready = (
            sem("w1h_ready"), sem("w1l_ready"), sem("w2h_ready"), sem("w2l_ready"))
        chosen, counted, f_made, hf_ready, hh_ready, hl_ready, y_step, y_read, y_ready, s_out = (
            sem("chosen"), sem("counted"), sem("f_made"), sem("hf_ready"), sem("hh_ready"), sem("hl_ready"),
            sem("y_step"), sem("y_read"), sem("y_ready"), sem("s_out"))
        block = ctx.enter_context(nc.Block())

        @block.sync
        def _(sp):
            def load_w1(i):
                sp.dma_start(w1[:, i % 2, :, :], a["w1"][:, :, 2 * i * P:2 * (i + 1) * P]).then_inc(s_w1[i % 2], 16)

            load_w1(0)
            load_w1(1)
            for dst, name in ((b1, "b1"), (b2, "b2"), (rw, "rw"), (tri, "tri"), (iota, "iota")):
                sp.dma_start(dst[tuple([slice(None)] * len(dst.shape))], a[name]).then_inc(s_w, 16)
            for i in range(4):
                fs = slice(i * FC // 4, (i + 1) * FC // 4)
                sp.dma_start(w2[:, fs, :], a["w2"][:, fs, :]).then_inc(s_w2[i], 16)
            for i in range(2, FC // 2):
                sp.wait_ge(w1l_ready, 2 * (i - 1))
                load_w1(i)
            for t in range(TILES):
                sp.wait_ge(y_ready, t + 1)
                sp.dma_start(out[t, :, :], x[:, t, :]).then_inc(s_out, 16)
            sp.wait_ge(s_out, 16 * TILES)

        @block.vector
        def _(dve):
            v = nc.vector
            link = chain(dve, s_ch)
            link(v.tensor_scalar(v1[:, :], mv[:, :, 1], LN_EPS, None, ALU.add))
            rsqrt(link, v, v1[:, :], r1[:, :], t1[:, :])

            def low(t):
                dve.wait_ge(xTh_ready, t + 1)
                at = slice(t * P, (t + 1) * P)
                v.tensor_tensor(xTl[:, :, at], ps_t[t % 2][:, :].rearrange("p (c n) -> p c n", n=P),
                                xTh[:, :, at].bitcast(F32), ALU.subtract).then_inc(xTl_ready, 1)

            for t in range(TILES):
                if t >= 2:
                    dve.wait_ge(xT_done, t - 1)
                v.tensor_scalar(xf[:, t % 2, :], x[:, t, :], mv[:, t, 0:1], r1[:, t:t + 1],
                                ALU.subtract, ALU.mult).then_inc(xf_ready, 1)
                if t:
                    low(t - 1)
            low(TILES - 1)

            def over_e(s_):
                return s_.rearrange("p (t o) -> p t o", o=1).broadcast_to([P, TILES, E])

            def experts(k):
                return iota[:, k:k + 1, :].broadcast_to([P, TILES, E])

            dve.wait_ge(s_w, 80)
            dve.wait_ge(logits, 1)
            link(v.tensor_reduce(pick[:, :], ps_r[:, :, :], AX.X, ALU.max))
            v.tensor_tensor(pp[:, :, :], ps_r[:, :, :], over_e(pick[:, :]), ALU.subtract).then_inc(r_shift, 1)
            dve.wait_ge(r_exp, 1)
            link(v.tensor_reduce(pick[:, :], pp[:, :, :], AX.X, ALU.add))
            link(v.reciprocal(pick[:, :], pick[:, :]))
            link(v.tensor_tensor(pp[:, :, :], pp[:, :, :], over_e(pick[:, :]), ALU.mult))
            for k in range(2):
                link(v.tensor_reduce(top[:, k, :], pp[:, :, :], AX.X, ALU.max))
                link(v.tensor_tensor(cand[:, :, :], pp[:, :, :], over_e(top[:, k, :]), ALU.is_equal))
                link(v.tensor_scalar(cand[:, :, :], cand[:, :, :], -100.0, None, ALU.mult))
                link(v.tensor_tensor(cand[:, :, :], cand[:, :, :], experts(1), ALU.add))
                link(v.tensor_reduce(pick[:, :], cand[:, :, :], AX.X, ALU.min))
                link(v.tensor_tensor(oh[:, k, :, :], over_e(pick[:, :]), experts(0), ALU.is_equal))
                if k == 0:
                    link(v.tensor_scalar(cand[:, :, :], oh[:, 0, :, :], -2.0, None, ALU.mult))
                    link(v.tensor_tensor(pp[:, :, :], pp[:, :, :], cand[:, :, :], ALU.add))
            v.memset(off[:, 0, :], 0.0).then_inc(chosen, 1)
            dve.wait_ge(counted, 1)
            link(v.tensor_copy(tot[:, :, :].rearrange("p n e -> p (n e)"), ps_c[:, 1, :]))
            for n in range(1, 2 * TILES):
                link(v.tensor_tensor(off[:, n, :], off[:, n - 1, :], tot[:, n - 1, :], ALU.add))
            flat = cum[:, :, :, :].rearrange("p k t e -> p (k t e)")
            link(v.tensor_tensor(flat, ps_c[:, 0, :], off[:, :, :].rearrange("p n e -> p (n e)"), ALU.add))
            link(v.tensor_tensor(flat, flat, oh[:, :, :, :].rearrange("p k t e -> p (k t e)"), ALU.mult))
            link(v.tensor_reduce(room[:, :, :].rearrange("p k t -> p (k t)"),
                                 cum[:, :, :, :].rearrange("p k t e -> p (k t) e"), AX.X, ALU.add))
            link(v.tensor_scalar(room[:, :, :], room[:, :, :], float(CAP), None, ALU.is_le))
            link(v.tensor_tensor(room[:, :, :], room[:, :, :], top[:, :, :], ALU.mult))
            link(v.tensor_tensor(wt[:, :], room[:, 0, :], room[:, 1, :], ALU.add))
            for t in range(TILES):
                dve.wait_ge(y_step, (t // HT + 1) * FC)
                v.tensor_tensor(y[:, t % 2, :], ps_y[t % HT][:, :], b2[:, :], ALU.add).then_inc(y_read, 1)
                dve.wait_ge(y_read, t + 1)
                v.scalar_tensor_tensor(x[:, t, :], y[:, t % 2, :], wt[:, t:t + 1], x[:, t, :],
                                       ALU.mult, ALU.add).then_inc(y_ready, 1)

        @block.scalar
        def _(act):
            s = nc.scalar
            def w1_high(f):
                act.wait_ge(s_w1[f // 2 % 2], 16 * (f // 4 + 1))
                s.activation(w1h[:, :, f * P:(f + 1) * P], w1[:, f // 2 % 2, :, f % 2 * P:(f % 2 + 1) * P],
                             ACT.Copy).then_inc(w1h_ready, 1)

            def w2_high(n):
                if n < FC and n % (FC // 4) == 0:
                    act.wait_ge(s_w2[n // (FC // 4)], 16)
                if n >= 2:
                    act.wait_ge(y_step, n - 1)
                s.activation(w2h[:, n % 2, :], w2[:, n % FC, :], ACT.Copy).then_inc(w2h_ready, 1)

            for f in range(2):
                w1_high(f)
            for t in range(TILES):
                act.wait_ge(xT_done, t + 1)
                src = ps_t[t % 2][:, :].rearrange("p (c n) -> p c n", n=P)
                s.activation(xT[:, :, t * P:(t + 1) * P], src, ACT.Copy)
                s.activation(xTh[:, :, t * P:(t + 1) * P], src, ACT.Copy).then_inc(xTh_ready, 1)
            w2_high(0)
            act.wait_ge(r_shift, 1)
            s.activation(pp[:, :, :], pp[:, :, :], ACT.Exp).then_inc(r_exp, 1)
            act.wait_ge(s_w, 80)
            for n in range(STEPS_F):
                f = n % FC
                if n + 2 < FC:
                    w1_high(n + 2)
                act.wait_ge(f_made, n + 1)
                if n >= 2:
                    act.wait_ge(hl_ready, n - 1)
                s.activation(hf[:, n % 2, :], ps_f[n % 2][:, :], ACT.Gelu, bias=b1[:, f:f + 1]).then_inc(hf_ready, 1)
                act.wait_ge(hf_ready, n + 1)
                s.activation(hh[:, n % 2, :], hf[:, n % 2, :], ACT.Copy).then_inc(hh_ready, 1)
                if n + 1 < STEPS_F:
                    w2_high(n + 1)

        @block.gpsimd
        def _(pool):
            g = nc.gpsimd

            def w1_low(f):
                pool.wait_ge(w1h_ready, f + 1)
                at = slice(f * P, (f + 1) * P)
                g.tensor_tensor(w1l[:, :, at], w1[:, f // 2 % 2, :, f % 2 * P:(f % 2 + 1) * P],
                                w1h[:, :, at].bitcast(F32), ALU.subtract).then_inc(w1l_ready, 1)

            def w2_low(n):
                pool.wait_ge(w2h_ready, n + 1)
                g.tensor_tensor(w2l[:, n % 2, :], w2[:, n % FC, :], w2h[:, n % 2, :].bitcast(F32),
                                ALU.subtract).then_inc(w2l_ready, 1)

            for f in range(2):
                w1_low(f)
            w2_low(0)
            for n in range(STEPS_F):
                if n + 2 < FC:
                    w1_low(n + 2)
                pool.wait_ge(hh_ready, n + 1)
                g.tensor_tensor(hl[:, n % 2, :], hf[:, n % 2, :], hh[:, n % 2, :].bitcast(F32),
                                ALU.subtract).then_inc(hl_ready, 1)
                if n + 1 < STEPS_F:
                    w2_low(n + 1)

        @block.tensor
        def _(pe):
            def three(out, lhs, rhs, start, stop):
                (lh, ll), (rh, rl) = lhs, rhs
                nc.tensor.matmul(out, lh, rh, start=start, stop=False)
                nc.tensor.matmul(out, ll, rh, start=False, stop=False)
                return nc.tensor.matmul(out, lh, rl, start=False, stop=stop)

            for t in range(TILES):
                pe.wait_ge(xf_ready, t + 1)
                if t >= 2:
                    pe.wait_ge(xTl_ready, t - 1)
                for c in range(HC):
                    last = nc.tensor.transpose(ps_t[t % 2][:, c * P:(c + 1) * P], xf[:, t % 2, c * P:(c + 1) * P],
                                               ident[:, :])
                last.then_inc(xT_done, 1)
            pe.wait_ge(s_w, 80)
            pe.wait_ge(xTl_ready, TILES)
            for t in range(TILES):
                for c in range(HC):
                    last = nc.tensor.matmul(ps_r[:, t, :], xT[:, c, t * P:(t + 1) * P], rw[:, c, :],
                                            start=c == 0, stop=c == HC - 1)
            last.then_inc(logits, 1)

            def hidden(n):
                f, at = n % FC, slice(n // FC * half, (n // FC + 1) * half)
                if n < FC:
                    pe.wait_ge(w1l_ready, n + 1)
                if n >= 2:
                    pe.wait_ge(hh_ready, n - 1)
                for c in range(HC):
                    fs = slice(f * P, (f + 1) * P)
                    last = three(ps_f[n % 2][:, :], (w1h[:, c, fs], w1l[:, c, fs]), (xTh[:, c, at], xTl[:, c, at]),
                                 c == 0, c == HC - 1)
                last.then_inc(f_made, 1)

            def results(n):
                pe.wait_ge(hl_ready, n + 1)
                pe.wait_ge(w2l_ready, n + 1)
                for t in range(HT):
                    if n == FC:
                        pe.wait_ge(y_read, t + 1)
                    at = slice(t * P, (t + 1) * P)
                    last = three(ps_y[t][:, :], (hh[:, n % 2, at], hl[:, n % 2, at]), (w2h[:, n % 2, :], w2l[:, n % 2, :]),
                                 n % FC == 0, n % FC == FC - 1)
                last.then_inc(y_step, 1)

            COUNT_STEP = 6
            for n in range(STEPS_F):
                hidden(n)
                if n:
                    results(n - 1)
                if n == COUNT_STEP:
                    pe.wait_ge(chosen, 1)
                    for k in range(2):
                        last = nc.tensor.matmul(ps_c[:, k, :], tri[:, k, :],
                                                oh[:, :, :, :].rearrange("p k t e -> p (k t e)"),
                                                start=True, stop=True)
                    last.then_inc(counted, 1)
            results(STEPS_F - 1)


def perceiver_layer(nc, a, out):
    with ExitStack() as ctx:
        def sb(name, shape):
            return ctx.enter_context(nc.sbuf_tensor(name, shape, F32))

        up = sb("up", [P, HC, TOK])
        ident = sb("ident_sb", [P, P])
        with ExitStack() as cross:
            kv = [cross.enter_context(nc.sbuf_tensor(name, shape, dt)) for name, shape, dt in (
                ("kv_wh", [P, KDC, 2, 2 * HW], F32R), ("kv_wl", [P, KDC, 2, 2 * HW], F32R),
                ("w_dca", [P, KDC, 2, 2 * HW], F32), ("bk_main", [P, 2, HW], F32), ("bk_dca", [P, 2, HW], F32))]
            stage_a(nc, up, ident, kv, a)
            stage_b(nc, up, ident, kv, a)
        x = sb("x_sb", [P, TILES, H])
        mv = sb("mv_out", [P, TILES, 2])
        with ExitStack() as late:
            up2 = late.enter_context(nc.sbuf_tensor("up2", [P, HC, TOK], F32))
            qk = late.enter_context(nc.sbuf_tensor("qk", [P, HQ + HKV, TOK], F32))
            with ExitStack() as c:
                hTh = c.enter_context(nc.sbuf_tensor("hTh", [P, HC, TOK], F32R))
                hTl = c.enter_context(nc.sbuf_tensor("hTl", [P, HC, TOK], F32R))
                wqk = c.enter_context(nc.sbuf_tensor("wqk", [P, 2, HC, 4 * D], F32))
                s_wqk = [c.enter_context(nc.semaphore(f"s_wqk{i}")) for i in range(2)]
                stage_c_norms(nc, x, up, up2, hTh, hTl, wqk, s_wqk, ident, a)
                stage_c_project(nc, hTh, hTl, qk, wqk, s_wqk, a)
            stage_c_attend(nc, x, up2, qk, mv, ident, a)
        stage_d(nc, x, up, mv, ident, a, out)


def laid_out(i):
    n = {k.removeprefix("L0_"): np.asarray(v) for k, v in i.items()}
    x = {k: v for k, v in n.items()}
    o = {}
    f32 = np.float32
    o["x"] = x["x"].reshape(TILES, P, H).transpose(1, 0, 2)
    yT = x["ctx_1024"].transpose(0, 2, 1).reshape(B, KDC, P, KEYS)
    y = np.zeros((B, KDC, P, KCOLS), yT.dtype)
    y[..., :MAIN] = yT[..., :MAIN]
    y[..., DCA_AT:] = yT[..., MAIN:]
    o["yT"] = y.transpose(0, 2, 1, 3)
    o["wq"] = x["xattn_Wq"].reshape(HC, P, H).transpose(1, 0, 2)
    o["bq"] = np.broadcast_to(x["xattn_bq"], (P, H))
    rep = P // XD
    o["qnw"] = np.tile(x["xattn_qn_w"], rep)[:, None]
    o["qnb"] = np.tile(x["xattn_qn_b"], rep)[:, None]
    w = np.concatenate([x["xattn_Wk"], x["xattn_Wv"]], 1).reshape(KDC, P, 2, 8, 2, XD)
    o["wm"] = w.transpose(1, 0, 2, 4, 3, 5).reshape(P, KDC, 2, 16 * XD)
    w = x["xattn_Wkv_dca"].reshape(KDC, P, 2, 2, 8, XD)
    o["wd"] = w.transpose(1, 0, 3, 2, 4, 5).reshape(P, KDC, 2, 16 * XD)
    b = np.concatenate([x["xattn_bk"], x["xattn_bv"]]).reshape(XH, 2, XD)
    bd = x["xattn_bkv_dca"].reshape(2, XH, XD)
    o["bkm"] = np.broadcast_to(b[:, 0].reshape(2, 8 * XD), (P, 2, 8 * XD))
    o["bkd"] = np.broadcast_to(bd[0].reshape(2, 8 * XD), (P, 2, 8 * XD))
    norms = [np.tile(x["xattn_" + k], rep)[:, None] for k in ("kn_w", "kn_b", "kn_dca_w", "kn_dca_b")]
    o["cols"] = np.concatenate(norms + [b[:, 1].reshape(4, P).T, bd[1].reshape(4, P).T], 1)
    o["wo"] = x["xattn_Wo"].reshape(HC, P, H).transpose(1, 0, 2)
    o["bo"] = np.broadcast_to(x["xattn_bo"], (P, H))
    o["lnw"] = np.broadcast_to(x["attn_ln_weight"], (P, H))
    w = np.concatenate([x["attn_q_project"], x["attn_k_project"]], 0).T.reshape(HC, P, (HQ + HKV) * D)
    o["wqk"] = w.transpose(1, 0, 2)
    o["bqk"] = np.concatenate([x["attn_q_bias"], x["attn_k_bias"]]).reshape(HQ + HKV, D).T
    o["wv"] = x["attn_v_project"].T.reshape(HC, P, HKV * D).transpose(1, 0, 2)
    o["bv_c"] = x["attn_v_bias"].reshape(HKV, D).T
    o["wot"] = x["attn_o_project"].T.reshape(HQ, P, H).transpose(1, 0, 2)
    o["w1"] = x["ffn_w1"].T.reshape(HC, P, F).transpose(1, 0, 2)
    o["b1"] = x["ffn_b1"].reshape(FC, P).T
    o["w2"] = x["ffn_w2"].T.reshape(FC, P, H).transpose(1, 0, 2)
    o["b2"] = np.broadcast_to(x["ffn_b2"], (P, H))
    o["rw"] = x["ffn_router_w"].T.reshape(HC, P, E).transpose(1, 0, 2)
    inv = (f32(1.0) / np.power(f32(10000.0), np.arange(0, D, 2, dtype=f32) / f32(D))).astype(f32)
    ang = (np.arange(S, dtype=f32)[:, None] * inv).astype(f32)
    cos, sin = np.cos(ang).astype(f32).T, np.sin(ang).astype(f32).T
    o["rope"] = np.stack([np.concatenate([cos, cos]), np.concatenate([-sin, sin])], 1)
    q, k = np.arange(P)[:, None] % S, np.arange(S)[None, :]
    o["mask"] = np.where(k <= q, 0.0, MASKED).astype(f32)
    o["ident"] = np.eye(P, dtype=f32)
    upper = (np.arange(P)[:, None] <= np.arange(P)[None, :]).astype(f32)
    o["tri"] = np.stack([upper, np.ones((P, P), f32)], 1)
    e = np.arange(E, dtype=f32)
    o["iota"] = np.broadcast_to(np.stack([e, e + 100]), (P, 2, E))
    return {k: np.ascontiguousarray(v) for k, v in o.items()}


def kernel(**inputs):
    import concourse.bacc as bacc
    from concourse.bass_utils import run_bass_kernel_spmd

    nc = bacc.Bacc("TRN2", target_bir_lowering=False, num_devices=1)
    arrays = {f"in_{k}": v for k, v in laid_out(inputs).items()}
    a = {k.removeprefix("in_"): nc.dram_tensor(k, v.shape, mybir.dt.from_np(v.dtype), kind="ExternalInput").ap()
         for k, v in arrays.items()}
    out = nc.dram_tensor("out", (TILES, P, H), F32, kind="ExternalOutput").ap()
    perceiver_layer(nc, a, out)
    r = run_bass_kernel_spmd(nc, [arrays], core_ids=[0])
    return r.results[0]["out"].reshape(B, S, H)
```
